# Optimizing a Trainium2 kernel written in Bass

```python
import numpy as np
import jax
import jax.numpy as jnp

def _softmax(x, axis=-1):
    return jax.nn.softmax(x, axis=axis)

def _gelu(x):
    return jax.nn.gelu(x, approximate=True)

def _silu(x):
    return jax.nn.silu(x)

def _sigmoid(x):
    return jax.nn.sigmoid(x)

def _layernorm(x, axis=-1, eps=1e-05):
    m = jnp.mean(x, axis=axis, keepdims=True)
    v = jnp.var(x, axis=axis, keepdims=True)
    return (x - m) / jnp.sqrt(v + eps)

def _scatter_add(tgt, idx, src, axis=0):
    return tgt.at[idx].add(src)

def _segment_sum(src, seg, n):
    return jax.ops.segment_sum(src, seg, n)
kernel_name = 'mk_conv_attn_hybrid_d2_conv_nhwc256_r4_64897f'

def setup_inputs(seed: int=0):
    np.random.seed(seed)
    _w = jnp.asarray

    def _rec_inputs():
        import jax
        import jax.numpy as jnp
        _gk = jax.random.key(seed)
        x = 7.22e-05 + 1 * jax.random.normal(jax.random.fold_in(_gk, 1), (8, 16, 16, 64), jnp.float32)
        return x
    x = _rec_inputs()

    def _L0_conv_setup():
        import jax, jax.numpy as jnp
        import numpy as np
        N, H, W, C = (8, 16, 16, 64)
        GC = 8
        G = C // GC
        K = 3
        KK = K * K
        DK = 3

        def _dcnv4(x, dw_w, dw_b, om_w, om_b, vp_w, vp_b, op_w):
            n, h, w, c = x.shape
            xdw = jax.lax.conv_general_dilated(x, dw_w, window_strides=(1, 1), padding='SAME', dimension_numbers=('NHWC', 'HWIO', 'NHWC'), feature_group_count=c) + dw_b
            om = (xdw @ om_w + om_b).reshape(n, h, w, G, KK * 3)
            offset = om[..., :2 * KK].reshape(n, h, w, G, KK, 2)
            mask = om[..., 2 * KK:]
            value = (x @ vp_w + vp_b).reshape(n, h, w, G, GC)
            kg = (jnp.arange(K) - (K - 1) // 2).astype(jnp.float32)
            ky = jnp.repeat(kg, K)
            kx = jnp.tile(kg, K)
            base_y = jnp.arange(h, dtype=jnp.float32).reshape(1, h, 1, 1, 1)
            base_x = jnp.arange(w, dtype=jnp.float32).reshape(1, 1, w, 1, 1)
            py = base_y + ky + offset[..., 1]
            px = base_x + kx + offset[..., 0]
            y0 = jnp.floor(py)
            x0 = jnp.floor(px)
            ty = py - y0
            tx = px - x0
            n_idx = jnp.arange(n).reshape(n, 1, 1, 1, 1)
            g_idx = jnp.arange(G).reshape(1, 1, 1, G, 1)

            def gather(yi, xi):
                valid = (yi >= 0) & (yi <= h - 1) & (xi >= 0) & (xi <= w - 1)
                yc = jnp.clip(yi, 0, h - 1).astype(jnp.int32)
                xc = jnp.clip(xi, 0, w - 1).astype(jnp.int32)
                v = value[n_idx, yc, xc, g_idx]
                return v * valid[..., None].astype(value.dtype)
            v00 = gather(y0, x0)
            v01 = gather(y0, x0 + 1)
            v10 = gather(y0 + 1, x0)
            v11 = gather(y0 + 1, x0 + 1)
            sampled = ((1 - ty) * (1 - tx))[..., None] * v00 + ((1 - ty) * tx)[..., None] * v01 + (ty * (1 - tx))[..., None] * v10 + (ty * tx)[..., None] * v11
            out = jnp.einsum('nhwgkc,nhwgk->nhwgc', sampled, mask).reshape(n, h, w, c)
            return out @ op_w
        key = jax.random.key(seed)
        ks = jax.random.split(key, 6)
        s = 0.02
        return {'x': jax.random.normal(ks[0], (N, H, W, C), jnp.float32), 'dw_w': jax.random.normal(ks[1], (DK, DK, 1, C), jnp.float32) * s, 'dw_b': jnp.zeros((C,), jnp.float32), 'om_w': jax.random.normal(ks[2], (C, G * KK * 3), jnp.float32) * s, 'om_b': jnp.zeros((G * KK * 3,), jnp.float32), 'vp_w': jax.random.normal(ks[3], (C, C), jnp.float32) * s, 'vp_b': jnp.zeros((C,), jnp.float32), 'op_w': jax.random.normal(ks[4], (C, C), jnp.float32) * s}
    _L0_conv_all = _L0_conv_setup()
    _L0_conv_in = {k: v for k, v in _L0_conv_all.items() if k in ('dw_w', 'dw_b', 'om_w', 'om_b', 'vp_w', 'vp_b', 'op_w')}
    del _L0_conv_all

    def _L1_attn_setup():
        import jax, jax.numpy as jnp
        import numpy as np
        B, N, F = (4, 1024, 64)
        key = jax.random.key(seed)
        ks = jax.random.split(key, 7)
        s = 1.0 / np.sqrt(F)
        return {'x': jax.random.normal(ks[0], (B, N, F), dtype=jnp.float32), 'Wq': jax.random.normal(ks[1], (F, F), dtype=jnp.float32) * s, 'bq': jnp.zeros((F,), dtype=jnp.float32), 'Wk': jax.random.normal(ks[2], (F, F), dtype=jnp.float32) * s, 'bk': jnp.zeros((F,), dtype=jnp.float32), 'Wv': jax.random.normal(ks[3], (F, F), dtype=jnp.float32) * s, 'bv': jnp.zeros((F,), dtype=jnp.float32)}
    _L1_attn_all = _L1_attn_setup()
    _L1_attn_in = {k: v for k, v in _L1_attn_all.items() if k in ('Wq', 'bq', 'Wk', 'bk', 'Wv', 'bv')}
    del _L1_attn_all

    def _L1_ffn_setup():
        import jax, jax.numpy as jnp
        import numpy as np
        D_MODEL = 64
        N_EXPERTS = 16
        HIDDEN = 128
        SCALE = 0.02
        key = jax.random.key(seed)
        ks = jax.random.split(key, 5)
        x = jax.random.normal(ks[0], (4, 2048, D_MODEL), dtype=jnp.float32)
        gate_w = jax.random.normal(ks[1], (D_MODEL, N_EXPERTS), dtype=jnp.float32) * SCALE
        gate_b = jnp.zeros((N_EXPERTS,), dtype=jnp.float32)
        w1 = jax.random.normal(ks[2], (N_EXPERTS, D_MODEL, HIDDEN), dtype=jnp.float32) * SCALE
        w2 = jax.random.normal(ks[3], (N_EXPERTS, D_MODEL, HIDDEN), dtype=jnp.float32) * SCALE
        w3 = jax.random.normal(ks[4], (N_EXPERTS, HIDDEN, D_MODEL), dtype=jnp.float32) * SCALE
        return {'x': x, 'gate_w': gate_w, 'gate_b': gate_b, 'w1': w1, 'w2': w2, 'w3': w3}
    _L1_ffn_all = _L1_ffn_setup()
    _L1_ffn_in = {k: v for k, v in _L1_ffn_all.items() if k in ('gate_w', 'gate_b', 'w1', 'w2', 'w3')}
    del _L1_ffn_all
    return {'x': x, 'L0_conv_dw_w': _L0_conv_in['dw_w'], 'L0_conv_dw_b': _L0_conv_in['dw_b'], 'L0_conv_om_w': _L0_conv_in['om_w'], 'L0_conv_om_b': _L0_conv_in['om_b'], 'L0_conv_vp_w': _L0_conv_in['vp_w'], 'L0_conv_vp_b': _L0_conv_in['vp_b'], 'L0_conv_op_w': _L0_conv_in['op_w'], 'L1_attn_Wq': _L1_attn_in['Wq'], 'L1_attn_bq': _L1_attn_in['bq'], 'L1_attn_Wk': _L1_attn_in['Wk'], 'L1_attn_bk': _L1_attn_in['bk'], 'L1_attn_Wv': _L1_attn_in['Wv'], 'L1_attn_bv': _L1_attn_in['bv'], 'L1_ffn_gate_w': _L1_ffn_in['gate_w'], 'L1_ffn_gate_b': _L1_ffn_in['gate_b'], 'L1_ffn_w1': _L1_ffn_in['w1'], 'L1_ffn_w2': _L1_ffn_in['w2'], 'L1_ffn_w3': _L1_ffn_in['w3']}

def reference(x, L0_conv_dw_w, L0_conv_dw_b, L0_conv_om_w, L0_conv_om_b, L0_conv_vp_w, L0_conv_vp_b, L0_conv_op_w, L1_attn_Wq, L1_attn_bq, L1_attn_Wk, L1_attn_bk, L1_attn_Wv, L1_attn_bv, L1_ffn_gate_w, L1_ffn_gate_b, L1_ffn_w1, L1_ffn_w2, L1_ffn_w3):
    import jax
    import jax.numpy as jnp

    def _L0_conv_ref(x, dw_w, dw_b, om_w, om_b, vp_w, vp_b, op_w):
        import jax, jax.numpy as jnp
        import numpy as np
        N, H, W, C = (8, 16, 16, 64)
        GC = 8
        G = C // GC
        K = 3
        KK = K * K
        DK = 3

        def _dcnv4(x, dw_w, dw_b, om_w, om_b, vp_w, vp_b, op_w):
            n, h, w, c = x.shape
            xdw = jax.lax.conv_general_dilated(x, dw_w, window_strides=(1, 1), padding='SAME', dimension_numbers=('NHWC', 'HWIO', 'NHWC'), feature_group_count=c) + dw_b
            om = (xdw @ om_w + om_b).reshape(n, h, w, G, KK * 3)
            offset = om[..., :2 * KK].reshape(n, h, w, G, KK, 2)
            mask = om[..., 2 * KK:]
            value = (x @ vp_w + vp_b).reshape(n, h, w, G, GC)
            kg = (jnp.arange(K) - (K - 1) // 2).astype(jnp.float32)
            ky = jnp.repeat(kg, K)
            kx = jnp.tile(kg, K)
            base_y = jnp.arange(h, dtype=jnp.float32).reshape(1, h, 1, 1, 1)
            base_x = jnp.arange(w, dtype=jnp.float32).reshape(1, 1, w, 1, 1)
            py = base_y + ky + offset[..., 1]
            px = base_x + kx + offset[..., 0]
            y0 = jnp.floor(py)
            x0 = jnp.floor(px)
            ty = py - y0
            tx = px - x0
            n_idx = jnp.arange(n).reshape(n, 1, 1, 1, 1)
            g_idx = jnp.arange(G).reshape(1, 1, 1, G, 1)

            def gather(yi, xi):
                valid = (yi >= 0) & (yi <= h - 1) & (xi >= 0) & (xi <= w - 1)
                yc = jnp.clip(yi, 0, h - 1).astype(jnp.int32)
                xc = jnp.clip(xi, 0, w - 1).astype(jnp.int32)
                v = value[n_idx, yc, xc, g_idx]
                return v * valid[..., None].astype(value.dtype)
            v00 = gather(y0, x0)
            v01 = gather(y0, x0 + 1)
            v10 = gather(y0 + 1, x0)
            v11 = gather(y0 + 1, x0 + 1)
            sampled = ((1 - ty) * (1 - tx))[..., None] * v00 + ((1 - ty) * tx)[..., None] * v01 + (ty * (1 - tx))[..., None] * v10 + (ty * tx)[..., None] * v11
            out = jnp.einsum('nhwgkc,nhwgk->nhwgc', sampled, mask).reshape(n, h, w, c)
            return out @ op_w
        return _dcnv4(x, dw_w, dw_b, om_w, om_b, vp_w, vp_b, op_w)

    def _L1_attn_ref(x, Wq, bq, Wk, bk, Wv, bv):
        import jax, jax.numpy as jnp
        import numpy as np
        B, N, F = (4, 1024, 64)
        q = jnp.einsum('bnf,gf->bng', x, Wq) + bq
        k = jnp.einsum('bnf,gf->bng', x, Wk) + bk
        v = jnp.einsum('bnf,gf->bng', x, Wv) + bv
        scale = jnp.sqrt(jnp.asarray(F, dtype=jnp.float32))
        scores = jnp.einsum('bnd,bmd->bnm', q, k) / scale
        weights = jax.nn.softmax(scores, axis=-1)
        return jnp.einsum('bnm,bmd->bnd', weights, v)

    def _L1_ffn_ref(x, gate_w, gate_b, w1, w2, w3):
        import jax, jax.numpy as jnp
        import numpy as np
        D_MODEL = 64
        N_EXPERTS = 16
        HIDDEN = 128
        SCALE = 0.02
        n_experts = w1.shape[0]
        logits = jnp.einsum('bsd,de->bse', x, gate_w) + gate_b
        probs = jax.nn.softmax(logits, axis=-1)
        top_probs, top_idx = jax.lax.top_k(probs, 2)
        top_probs = top_probs / jnp.sum(top_probs, axis=-1, keepdims=True)
        dispatch = jnp.sum(jax.nn.one_hot(top_idx, n_experts, dtype=x.dtype) * top_probs[..., None], axis=-2)
        h1 = jnp.einsum('bsd,edh->bseh', x, w1)
        h2 = jnp.einsum('bsd,edh->bseh', x, w2)
        hidden = jax.nn.silu(h1) * h2
        expert_out = jnp.einsum('bseh,eho->bseo', hidden, w3)
        return jnp.einsum('bseo,bse->bso', expert_out, dispatch)

    def _gn(v, G=32, eps=1e-05):
        B_, H_, W_, C_ = v.shape
        g = v.reshape(B_, H_, W_, G, C_ // G)
        m = jnp.mean(g, axis=(1, 2, 4), keepdims=True)
        s = jnp.var(g, axis=(1, 2, 4), keepdims=True)
        return ((g - m) / jnp.sqrt(s + eps)).reshape(v.shape)

    def _ln_c(v, eps=1e-06):
        m = jnp.mean(v, axis=-1, keepdims=True)
        s = jnp.var(v, axis=-1, keepdims=True)
        return (v - m) / jnp.sqrt(s + eps)

    def _ln_t(v, eps=1e-05):
        m = jnp.mean(v, axis=-1, keepdims=True)
        s = jnp.var(v, axis=-1, keepdims=True)
        return (v - m) / jnp.sqrt(s + eps)

    def _to_tokens(v):
        B_, H_, W_, C_ = v.shape
        return v.reshape(B_, H_ * W_, C_)

    def _from_tokens(t, like):
        return t.reshape(like.shape)
    x = x + _L0_conv_ref(_gn(x), L0_conv_dw_w, L0_conv_dw_b, L0_conv_om_w, L0_conv_om_b, L0_conv_vp_w, L0_conv_vp_b, L0_conv_op_w)
    t = _to_tokens(x)
    t = t + _L1_attn_ref(_ln_t(t), L1_attn_Wq, L1_attn_bq, L1_attn_Wk, L1_attn_bk, L1_attn_Wv, L1_attn_bv)
    t = t + _L1_ffn_ref(_ln_t(t), L1_ffn_gate_w, L1_ffn_gate_b, L1_ffn_w1, L1_ffn_w2, L1_ffn_w3)
    x = _from_tokens(t, x)
    return x

_drawn_inputs = setup_inputs


def setup_inputs(seed=0):
    import zlib

    import numpy as np

    out = dict(_drawn_inputs(seed))
    spreads = {'L0_conv_dw_b': (0.0, 0.8),
     'L0_conv_om_b': (0.0, 0.8),
     'L0_conv_vp_b': (0.0, 0.8),
     'L1_attn_bq': (0.0, 0.538),
     'L1_attn_bk': (0.0, 0.8),
     'L1_attn_bv': (0.0, 0.1),
     'L1_ffn_gate_b': (0.0, 0.8)}
    factors = {'L0_conv_dw_w': 8.0,
     'L0_conv_om_w': 8.0,
     'L0_conv_vp_w': 8.0,
     'L0_conv_op_w': 7.552,
     'L1_ffn_gate_w': 8.0,
     'L1_ffn_w1': 8.0,
     'L1_ffn_w2': 8.0,
     'L1_ffn_w3': 8.0}
    for name, (base, spread) in spreads.items():
        noise = np.random.default_rng([zlib.crc32(name.encode()), seed]).standard_normal(out[name].shape)
        drawn = base * np.exp(spread * noise) if base else spread * noise
        out[name] = jnp.asarray(drawn.astype(out[name].dtype))
    for name, factor in factors.items():
        out[name] = (out[name] * factor).astype(out[name].dtype)
    return out
```

```python
from contextlib import ExitStack

import concourse.bass as bass
from concourse import mybir

F32 = mybir.dt.float32
F32R = mybir.dt.float32r
BF16 = mybir.dt.bfloat16
ALU = mybir.AluOpType
ACT = mybir.ActivationFunctionType
AX_X = mybir.AxisListType.X

P = 128
IMAGES, H, W, C = 8, 16, 16, 64
PIX = H * W
TT = IMAGES * PIX // P
TPI = PIX // P
GROUPS = 8
GC = C // GROUPS
TAPS = 9
OMJ = 3 * TAPS
QUART = 4
QUARTETS = GROUPS // QUART
COLS = TAPS * PIX
BANK = 512
UNIT = 2 * BANK
UPQ = QUART * COLS // UNIT
UPI = UPQ * QUARTETS
CHUNKS = (TAPS + 1) // 2
FILL = 16 * 2 * QUART
EXPERTS, HIDDEN = 16, 128
SCALE = float(C) ** -0.5
GN_EPS, LN_EPS = 1e-5, 1e-5


def positive(value):
    return not isinstance(value, int) or value > 0


def count(eng, value):
    return value if isinstance(value, int) else eng.snap(value)


def spread(ap, dim, n):
    ap = ap.unsqueeze(dim)
    return ap.broadcast_to([n if k == dim else size for k, size in enumerate(ap.shape)])


def conv_stage(nc, d, t_tok):
    with ExitStack() as ctx:
        def sb(name, shape, dt=F32, where=ctx):
            return where.enter_context(nc.sbuf_tensor(name, shape, dt))

        def sem(name):
            return ctx.enter_context(nc.semaphore(name))

        ident = sb("ident", [P, P])
        pair = sb("pair", [P, P])
        fold = sb("fold", [P, QUARTETS, 32])
        rep = sb("rep", [P, QUART, P], F32R)
        grid = sb("grid", [P, PIX], BF16)
        place = sb("place", [P, OMJ, GROUPS, 16], BF16)
        om_h = sb("om_h", [P, OMJ, GROUPS, 16], F32R)
        om_l = sb("om_l", [P, OMJ, GROUPS, 16], F32R)
        vp_f = sb("vp_f", [P, C])
        vp_h = sb("vp_h", [P, C], F32R)
        vp_l = sb("vp_l", [P, C], F32R)
        vp_bias = sb("vp_bias", [P, QUARTETS, GC])
        dw = sb("dw", [P, TAPS])
        dw_bias = sb("dw_bias", [P, 1])
        op_w = sb("op_w", [P, C])
        xpad = sb("xpad", [P, IMAGES, H + 2, W + 2])
        stats = sb("stats", [P, IMAGES, 6])
        chan = sb("chan", [P, IMAGES, 2])
        gmean = sb("gmean", [P, IMAGES])
        gdev = sb("gdev", [P, IMAGES])
        gsq = sb("gsq", [P, IMAGES])
        gvar = sb("gvar", [P, IMAGES])
        gvar_eps = sb("gvar_eps", [P, IMAGES])
        minus_half = sb("minus_half", [P, IMAGES])
        grstd = sb("grstd", [P, IMAGES])
        gshift = sb("gshift", [P, IMAGES])
        conv = sb("conv", [P, H, W])
        xd = [sb(f"xd{i}", [P, PIX], F32R) for i in range(2)]
        xrep = sb("xrep", [P, H // 2, 8, W], F32R)
        v_sb = sb("v_sb", [P, H, QUARTETS, GC])
        vt_h = sb("vt_h", [P, GROUPS, H, GC], F32R)
        vt_l = sb("vt_l", [P, GROUPS, H, GC], F32R)
        b_h = [sb(f"b_h{i}", [P, TAPS, PIX], F32R) for i in range(2)]
        b_l = [sb(f"b_l{i}", [P, TAPS, PIX], F32R) for i in range(2)]
        a_h = [sb(f"a_h{i}", [P, TAPS, PIX], F32R) for i in range(2)]
        a_l = [sb(f"a_l{i}", [P, TAPS, PIX], F32R) for i in range(2)]
        a_rep = [sb(f"a_rep{i}", [P, UNIT]) for i in range(2)]
        prod = [sb(f"prod{i}", [P, UNIT]) for i in range(3)]
        d_sb = sb("d_sb", [P, BANK])
        with ExitStack() as early:
            xdup = sb("xdup", [P, TT, 2, C], F32, early)
            om_f = sb("om_f", [P, GROUPS, OMJ], F32, early)
            om_lf = sb("om_lf", [P, GROUPS, OMJ], F32, early)
            om_hf = sb("om_hf", [P, GROUPS, OMJ], F32R, early)
            bias_f = sb("bias_f", [P, GROUPS, OMJ], F32, early)
            bias_s = sb("bias_s", [P, 3, GROUPS, OMJ], BF16, early)
            bias_sel = sb("bias_sel", [P, GROUPS, OMJ], BF16, early)
            rep_f = sb("rep_f", [P, QUART, P], F32, early)
            grid_f = sb("grid_f", [P, PIX], F32, early)
            place_f = sb("place_f", [P, OMJ * P], F32, early)
        mb = [sb(f"mb{q}", [P, TAPS, PIX], F32R) for q in range(QUARTETS)]
        ma = [sb(f"ma{q}", [P, TAPS, PIX], F32R) for q in range(QUARTETS)]

        ps_t = [ctx.enter_context(nc.psum_tensor(f"ps_t{i}", [P, UNIT], F32)) for i in range(2)]
        ps_a = [ctx.enter_context(nc.psum_tensor(f"ps_a{i}", [P, BANK], F32)) for i in range(2)]
        ps_d = ctx.enter_context(nc.psum_tensor("ps_d", [P, BANK], F32))
        ps_m = ctx.enter_context(nc.psum_tensor("ps_m", [P, BANK], F32))

        x_in = sem("x_in")
        consts_in = sem("consts_in")
        tokens_in = sem("tokens_in")
        zeroed = sem("zeroed")
        turned = sem("turned")
        bn_done = sem("bn_done")
        chan_stats = sem("chan_stats")
        pair_sums = sem("pair_sums")
        gn_steps = sem("gn_steps")
        gn_pow = sem("gn_pow")
        xn_ready = sem("xn_ready")
        bias_steps = sem("bias_steps")
        w_dve = sem("w_dve")
        w_act = sem("w_act")
        taps_done = sem("taps_done")
        xd_high = sem("xd_high")
        xd_ready = sem("xd_ready")
        y_pos = sem("y_pos")
        x_pos = sem("x_pos")
        mask_ps = sem("mask_ps")
        y_abs = sem("y_abs")
        x_abs = sem("x_abs")
        y_hat = sem("y_hat")
        x_hat = sem("x_hat")
        a_full = sem("a_full")
        a_high = sem("a_high")
        b_high = sem("b_high")
        a_low = sem("a_low")
        b_low = sem("b_low")
        mb_filled = [sem(f"mb_filled{q}") for q in range(QUARTETS)]
        ma_filled = [sem(f"ma_filled{q}") for q in range(QUARTETS)]
        xrep_high = sem("xrep_high")
        xrep_ready = sem("xrep_ready")
        v_ps = sem("v_ps")
        v_done = sem("v_done")
        vt_high = sem("vt_high")
        vt_ready = sem("vt_ready")
        t_ready = sem("t_ready")
        a_ready = sem("a_ready")
        a_copied = sem("a_copied")
        weighted = sem("weighted")
        reduced = sem("reduced")
        d_copied = sem("d_copied")
        out_ps = sem("out_ps")
        t_done = sem("t_done")

        xview = d["x"].rearrange("n h w c -> (n h w) c").rearrange("(t p) c -> p t c", p=P)
        inner = lambda n: xpad[:, n, 1:H + 1, 1:W + 1]

        def fma(k):
            return slice(2 * k, min(2 * k + 2, TAPS))

        block = ctx.enter_context(nc.Block())

        @block.sync
        def _(sp):
            for half in range(2):
                sp.dma_start(xdup[:, :, half, :], xview).then_inc(x_in, 16)
            sp.dma_start(t_tok[:, :, :], xview).then_inc(tokens_in, 16)
            for dst, src in (
                    (ident[:, :], d["ident"]), (pair[:, :], d["pair"]),
                    (dw[:, :], d["dw"]), (dw_bias[:, :], d["dw_bias"]),
                    (om_f[:, :, :], d["om_w"].rearrange("p (g j) -> p g j", g=GROUPS)),
                    (vp_f[:, :], d["vp_w"]),
                    (vp_bias[:, :, :], d["vp_bias"].rearrange("p (q c) -> p q c", q=QUARTETS)),
                    (op_w[:, :], d["op_w"]),
                    (fold[:, :, :], d["fold"].rearrange("p (q c) -> p q c", q=QUARTETS)),
                    (rep_f[:, :, :], d["rep"].rearrange("p (j c) -> p j c", j=QUART)),
                    (grid_f[:, :], d["grid"]), (place_f[96:99, :], d["place"])):
                sp.dma_start(dst, src).then_inc(consts_in, 16)
            sp.wait_ge(zeroed, 1)
            for r in (0, 32, 64):
                sp.dma_start(bias_f[r:r + 1, :, :],
                             d["om_b"].rearrange("(a g j) -> a g j", a=1, g=GROUPS)).then_inc(consts_in, 16)

            def fill(n, par):
                made = count(sp, CHUNKS * (n + 1))
                free = [count(sp, 2 * (UPI * (n - 1) + UPQ * (q + 1))) for q in range(QUARTETS)]
                sp.wait_ge(b_low, made)
                for q in range(QUARTETS):
                    if positive(free[q]):
                        sp.wait_ge(a_ready, free[q])
                    for moving, high, low, filled in ((mb[q], b_h[par], b_l[par], mb_filled[q]),
                                                      (ma[q], a_h[par], a_l[par], ma_filled[q])):
                        for j in range(QUART):
                            g = QUART * q + j
                            for part, src in enumerate((high, low)):
                                r = 32 * j + 16 * part
                                sp.dma_start(moving[r:r + 16, :, :].bitcast(F32),
                                             src[16 * g:16 * g + 16, :, :].bitcast(F32)).then_inc(filled, 16)

            fill(0, 0)
            fill(1, 1)
            with sp.Fori(1, IMAGES // 2) as it:
                for par in range(2):
                    fill(2 * it + par, par)

        @block.tensor
        def _(pe):
            pe.wait_ge(x_in, 32)
            pe.wait_ge(consts_in, 16 * 15)
            for t in range(TT):
                pe.transpose(ps_t[t // 8][:, (t % 8) * P:(t % 8 + 1) * P],
                             xdup[:, t, :, :].rearrange("p a c -> p (a c)"),
                             ident[:, :]).then_inc(turned, 1)
            pe.wait_ge(chan_stats, IMAGES)
            pe.matmul(ps_m[:, 0:IMAGES], pair[:, :], chan[:, :, 0], start=True, stop=True).then_inc(pair_sums, 1)
            pe.wait_ge(gn_steps, 4)
            pe.matmul(ps_m[:, IMAGES:2 * IMAGES], pair[:, :], gvar[:, :], start=True, stop=True)\
              .then_inc(pair_sums, 1)

            def positions(kind, k, n, par, signal):
                for c, tap in enumerate(range(2 * k, min(2 * k + 2, TAPS))):
                    j = 2 * TAPS + tap if kind == 2 else 2 * tap + kind
                    out = ps_m[:, c * PIX:(c + 1) * PIX]
                    pe.matmul(out, om_h[:, j, :, :].rearrange("p g x -> p (g x)"), xd[par][:, :],
                              start=True, stop=False)
                    pe.matmul(out, om_l[:, j, :, :].rearrange("p g x -> p (g x)"), xd[par][:, :],
                              start=False, stop=False)
                    mm = pe.matmul(out, place[:, j, :, :].rearrange("p g x -> p (g x)"), grid[:, :],
                                   start=False, stop=True)
                mm.then_inc(signal, 1)

            def job_y(k, n, par):
                if k == 0:
                    pe.wait_ge(xd_ready, n + 1)
                    if positive(2 * n):
                        pe.wait_ge(v_done, 2 * n)
                else:
                    pe.wait_ge(x_abs, CHUNKS * n + k)
                positions(1, k, n, par, y_pos)

            def job_m(k, n, par):
                pe.wait_ge(y_abs, CHUNKS * n + k + 1)
                positions(2, k, n, par, mask_ps)

            def job_x(k, n, par):
                pe.wait_ge(a_full, CHUNKS * n + k + 1)
                positions(0, k, n, par, x_pos)

            def job_v(half, n):
                if half:
                    pe.wait_ge(v_done, 2 * n + 1)
                else:
                    pe.wait_ge(x_abs, CHUNKS * (n + 1))
                    if positive(n - 1):
                        pe.wait_ge(t_done, n - 1)
                pe.wait_ge(xrep_ready, 2 * n + half + 1)
                for y in range(H // 2):
                    for w, first in ((vp_h, True), (vp_l, False)):
                        mm = pe.matmul(ps_m[:, y * C:(y + 1) * C],
                                       xrep[:, y, :, :].rearrange("p r x -> p (r x)"), w[:, :],
                                       start=first, stop=not first)
                mm.then_inc(v_ps, 1)

            def job_out(i, free_sem, free):
                pe.wait_ge(d_copied, i + 1)
                pe.wait_ge(free_sem, free)
                for t in range(TPI):
                    for h in range(2):
                        mm = pe.matmul(ps_m[:, t * C:(t + 1) * C],
                                       d_sb[:, h * PIX + t * P:h * PIX + (t + 1) * P], op_w[:, :],
                                       start=h == 0, stop=h == 1)
                mm.then_inc(out_ps, 1)

            def segments(u):
                v = u % UPQ
                if v < UPQ - 1:
                    return [(c, 0, 2 * (v % 2) + c, 2 * (v // 2), 2) for c in range(2)]
                return [(j // 2, PIX * (j % 2), j, TAPS - 1, 1) for j in range(QUART)]

            def sample_x(u, i):
                q = u // UPQ
                if u % UPQ == 0:
                    pe.wait_ge(mb_filled[q], FILL * (i + 1))
                    pe.wait_ge(vt_ready, QUARTETS * i + q + 1)
                if positive(UPI * i + u - 1):
                    pe.wait_ge(weighted, UPI * i + u - 1)
                for c, col, j, tap, n in segments(u):
                    out = ps_t[u % 2][:, c * BANK + col:c * BANK + col + n * PIX]
                    for vt, first in ((vt_h, True), (vt_l, False)):
                        mm = pe.matmul(out, vt[:, QUART * q + j, :, :].rearrange("p y c -> p (y c)"),
                                       mb[q][:, tap:tap + n, :].rearrange("p t x -> p (t x)"),
                                       start=first, stop=not first)
                mm.then_inc(t_ready, 1)

            def replicate_a(u, i):
                q = u // UPQ
                if u % UPQ == 0:
                    pe.wait_ge(ma_filled[q], FILL * (i + 1))
                segs = segments(u)
                for s, (c, col, j, tap, n) in enumerate(segs):
                    if col == 0:
                        if positive(2 * (UPI * i + u) + c - 1):
                            pe.wait_ge(a_copied, 2 * (UPI * i + u) + c - 1)
                    mm = pe.matmul(ps_a[c][:, col:col + n * PIX], rep[:, j, :],
                                   ma[q][:, tap:tap + n, :].rearrange("p t x -> p (t x)"),
                                   start=True, stop=True)
                    if s + 1 == len(segs) or segs[s + 1][0] != c:
                        mm.then_inc(a_ready, 1)

            def reduce_pair(r, i):
                pe.wait_ge(weighted, UPI * i + 2 * r + 2)
                if r == 0:
                    if positive(i):
                        pe.wait_ge(d_copied, i)
                for u in (2 * r, 2 * r + 1):
                    for c, col, j, tap, n in segments(u):
                        first = u < 2 and tap == 0
                        last = u == UPI - 1
                        mm = pe.matmul(ps_d[32 * j:32 * j + 32, 0:n * PIX],
                                       fold[:, u // UPQ, :],
                                       prod[u % 3][:, c * BANK + col:c * BANK + col + n * PIX],
                                       start=first, stop=last, skip_group_check=True)
                mm.then_inc(reduced, 1)

            def image(i, par, made):
                n, npar = i + 1, 1 - par
                for u in range(UPI):
                    sample_x(u, i)
                    if made and u < 2 * CHUNKS:
                        (job_m if u % 2 else job_y)(u // 2, n, npar)
                    if u == 10 and not (isinstance(i, int) and i == 0):
                        if made:
                            job_out(i - 1, x_abs, CHUNKS * (n + 1))
                        else:
                            job_out(i - 1, v_done, 2 * n)
                    if made and u in (12, 15):
                        job_v(u // 15, n)
                    replicate_a(u, i)
                    if u % 2:
                        if u >= 3:
                            reduce_pair((u - 3) // 2, i)
                        elif not (isinstance(i, int) and i == 0):
                            reduce_pair(UPI // 2 - 1, i - 1)
                        if made and u < 2 * CHUNKS:
                            job_x(u // 2, n, npar)

            pe.wait_ge(w_dve, 5)
            pe.wait_ge(w_act, 5)
            pe.wait_ge(gn_steps, 5)
            for k in range(CHUNKS):
                job_y(k, 0, 0)
                job_m(k, 0, 0)
                job_x(k, 0, 0)
            job_v(0, 0)
            job_v(1, 0)
            pe.wait_ge(xn_ready, IMAGES)
            image(0, 0, True)
            image(1, 1, True)
            with pe.Fori(1, IMAGES // 2 - 1) as it:
                for par in range(2):
                    image(2 * it + par, par, True)
            image(IMAGES - 2, 0, True)
            image(IMAGES - 1, 1, False)
            reduce_pair(UPI // 2 - 1, IMAGES - 1)
            job_out(IMAGES - 1, t_done, IMAGES - 1)

        @block.scalar
        def _(act):
            act.wait_ge(consts_in, 16 * 15)
            act.activation(om_hf[:, :, :], om_f[:, :, :], ACT.Copy).then_inc(w_act, 1)
            act.activation(vp_h[:, :], vp_f[:, :], ACT.Copy).then_inc(w_act, 1)
            act.activation(rep[:, :, :], rep_f[:, :, :], ACT.Copy).then_inc(w_act, 1)
            act.activation(grid[:, :], grid_f[:, :], ACT.Copy).then_inc(w_act, 1)
            act.activation(om_h[:, :, :, :],
                           spread(om_f[:, :, :].rearrange("p g j -> p j g"), 3, 16),
                           ACT.Copy).then_inc(w_act, 1)
            act.wait_ge(gn_steps, 6)
            act.wait_ge(gn_pow, 1)
            for n in range(IMAGES):
                act.activation(inner(n), ps_t[n // 4][:, (n % 4) * PIX:(n % 4 + 1) * PIX]
                               .rearrange("p (y x) -> p y x", y=H),
                               ACT.Identity, bias=gshift[:, n:n + 1], scale=grstd[:, n:n + 1])\
                   .then_inc(xn_ready, 1)

            def xd_split(n, par):
                act.wait_ge(taps_done, TAPS * (n + 1))
                if positive(CHUNKS * (n - 1)):
                    act.wait_ge(mask_ps, CHUNKS * (n - 1))
                if positive(CHUNKS * (n - 1)):
                    act.wait_ge(x_pos, CHUNKS * (n - 1))
                act.activation(xd[par][:, :], conv[:, :, :].rearrange("p y x -> p (y x)"), ACT.Copy)\
                   .then_inc(xd_high, 1)

            def x_rep(half, n):
                if positive(2 * n + half):
                    act.wait_ge(v_ps, 2 * n + half)
                act.activation(xrep[:, :, :, :],
                               spread(xpad[:, n, 1 + 8 * half:9 + 8 * half, 1:W + 1], 2, 8),
                               ACT.Copy).then_inc(xrep_high, 1)

            def abs_y(k, n, par):
                if k == 0:
                    for q in range(QUARTETS):
                        if positive(FILL * (n - 1)):
                            act.wait_ge(ma_filled[q], FILL * (n - 1))
                act.wait_ge(y_pos, CHUNKS * n + k + 1)
                w = min(2, TAPS - 2 * k) * PIX
                act.activation(a_l[par][:, fma(k), :].bitcast(F32).rearrange("p t x -> p (t x)"),
                               ps_m[:, 0:w], ACT.Abs).then_inc(y_abs, 1)

            def abs_x(k, n, par):
                if k == 0:
                    for q in range(QUARTETS):
                        if positive(FILL * (n - 1)):
                            act.wait_ge(mb_filled[q], FILL * (n - 1))
                act.wait_ge(x_pos, CHUNKS * n + k + 1)
                w = min(2, TAPS - 2 * k) * PIX
                act.activation(b_l[par][:, fma(k), :].bitcast(F32).rearrange("p t x -> p (t x)"),
                               ps_m[:, 0:w], ACT.Abs).then_inc(x_abs, 1)

            def high_parts(k, n, par):
                act.wait_ge(a_full, CHUNKS * n + k + 1)
                act.activation(a_h[par][:, fma(k), :], a_l[par][:, fma(k), :].bitcast(F32), ACT.Copy)\
                   .then_inc(a_high, 1)
                act.wait_ge(x_hat, CHUNKS * n + k + 1)
                act.activation(b_h[par][:, fma(k), :], b_l[par][:, fma(k), :].bitcast(F32), ACT.Copy)\
                   .then_inc(b_high, 1)

            def vt_split(q, n):
                act.wait_ge(v_done, 2 * n + 2)
                if positive(UPI * (n - 1) + UPQ * (q + 1)):
                    act.wait_ge(t_ready, UPI * (n - 1) + UPQ * (q + 1))
                if positive(QUARTETS * (n - 1) + q + 1):
                    act.wait_ge(vt_ready, QUARTETS * (n - 1) + q + 1)
                for j in range(QUART):
                    r = slice(32 * j, 32 * j + 32)
                    mm = act.activation(vt_h[r, QUART * q + j, :, :], v_sb[r, :, q, :], ACT.Copy)
                mm.then_inc(vt_high, 1)

            def copy_a(u, i):
                for c in range(2):
                    act.wait_ge(a_ready, 2 * (UPI * i + u) + c + 1)
                    if c == 0:
                        if positive(UPI * i + u - 1):
                            act.wait_ge(weighted, UPI * i + u - 1)
                    act.activation(a_rep[u % 2][:, c * BANK:(c + 1) * BANK], ps_a[c][:, :], ACT.Copy)\
                       .then_inc(a_copied, 1)

            def copy_d(i):
                act.wait_ge(reduced, UPI // 2 * (i + 1))
                if positive(i):
                    act.wait_ge(out_ps, i)
                act.activation(d_sb[:, :], ps_d[:, :], ACT.Copy).then_inc(d_copied, 1)

            def image(i, par, made, ahead):
                n, npar = i + 1, 1 - par
                for u in range(UPI):
                    if made and u < 2 * CHUNKS and u % 2 == 0:
                        abs_y(u // 2, n, npar)
                    copy_a(u, i)
                    if u == 2 and not (isinstance(i, int) and i == 0):
                        copy_d(i - 1)
                    if u == 2:
                        vt_split(1, i)
                    if made and u < 2 * CHUNKS and u % 2:
                        abs_x(u // 2, n, npar)
                    if made and 0 < u <= 2 * CHUNKS and u % 2 == 0:
                        high_parts(u // 2 - 1, n, npar)
                    if made and u in (10, 13):
                        x_rep(u // 13, n)
                    if made and u == 16:
                        vt_split(0, n)
                    if ahead and u == 17:
                        xd_split(i + 2, par)

            xd_split(0, 0)
            x_rep(0, 0)
            for k in range(CHUNKS):
                abs_y(k, 0, 0)
                abs_x(k, 0, 0)
                high_parts(k, 0, 0)
            x_rep(1, 0)
            vt_split(0, 0)
            xd_split(1, 1)
            image(0, 0, True, True)
            image(1, 1, True, True)
            with act.Fori(1, IMAGES // 2 - 1) as it:
                for par in range(2):
                    image(2 * it + par, par, True, True)
            image(IMAGES - 2, 0, True, False)
            image(IMAGES - 1, 1, False, False)
            copy_d(IMAGES - 1)

        @block.vector
        def _(dve):
            for n in range(IMAGES):
                dve.wait_ge(turned, 4 * (n // 2) + 4)
                dve.bn_stats(stats[:, n, :], ps_t[n // 4][:, (n % 4) * PIX:(n % 4 + 1) * PIX]).then_inc(bn_done, 1)
            for n in range(IMAGES):
                dve.wait_ge(bn_done, n + 1)
                dve.bn_aggr(chan[:, n, :], stats[:, n, :]).then_inc(chan_stats, 1)
            dve.wait_ge(pair_sums, 1)
            dve.tensor_copy(gmean[:, :], ps_m[:, 0:IMAGES]).then_inc(gn_steps, 1)
            dve.wait_ge(gn_steps, 1)
            dve.wait_ge(chan_stats, IMAGES)
            dve.tensor_tensor(gdev[:, :], chan[:, :, 0], gmean[:, :], ALU.subtract).then_inc(gn_steps, 1)
            dve.wait_ge(gn_steps, 2)
            dve.tensor_tensor(gsq[:, :], gdev[:, :], gdev[:, :], ALU.mult).then_inc(gn_steps, 1)
            dve.wait_ge(gn_steps, 3)
            dve.tensor_tensor(gvar[:, :], gsq[:, :], chan[:, :, 1], ALU.add).then_inc(gn_steps, 1)
            dve.wait_ge(pair_sums, 2)
            dve.tensor_scalar(gvar_eps[:, :], ps_m[:, IMAGES:2 * IMAGES], GN_EPS, None, ALU.add).then_inc(gn_steps, 1)
            dve.wait_ge(gn_pow, 1)
            dve.scalar_tensor_tensor(out=gshift[:, :], in0=gmean[:, :], scalar=-1.0, in1=grstd[:, :],
                                     op0=ALU.mult, op1=ALU.mult).then_inc(gn_steps, 1)
            dve.wait_ge(consts_in, 16 * 15)
            dve.tensor_copy(bias_s[:, 0, :, :], bias_f[:, :, :]).then_inc(bias_steps, 1)
            for part in range(2):
                dve.wait_ge(bias_steps, 2 * part + 1)
                dve.tensor_tensor(bias_f[:, :, :], bias_f[:, :, :], bias_s[:, part, :, :], ALU.subtract)\
                   .then_inc(bias_steps, 1)
                dve.wait_ge(bias_steps, 2 * part + 2)
                dve.tensor_copy(bias_s[:, part + 1, :, :], bias_f[:, :, :]).then_inc(bias_steps, 1)
            dve.wait_ge(bias_steps, 5)
            dve.wait_ge(zeroed, 6)
            for part in range(3):
                r = 32 * part
                dve.tensor_copy(bias_sel[r:r + 1, :, :], bias_s[r:r + 1, part, :, :]).then_inc(bias_steps, 1)
            dve.wait_ge(bias_steps, 8)
            dve.tensor_copy(place[:, :, :, :],
                            spread(bias_sel[:, :, :].rearrange("p g j -> p j g"), 3, 16))\
               .then_inc(w_dve, 1)
            dve.wait_ge(w_dve, 1)
            dve.tensor_copy(place[96:99, :, :, :].rearrange("p j g x -> p (j g x)"), place_f[96:99, :])\
               .then_inc(w_dve, 1)
            dve.wait_ge(w_act, 2)
            dve.tensor_tensor(om_lf[:, :, :], om_f[:, :, :], om_hf[:, :, :].bitcast(F32), ALU.subtract)\
               .then_inc(w_dve, 1)
            dve.tensor_tensor(vp_l[:, :], vp_f[:, :], vp_h[:, :].bitcast(F32), ALU.subtract).then_inc(w_dve, 1)
            dve.wait_ge(w_dve, 4)
            dve.tensor_copy(om_l[:, :, :, :],
                            spread(om_lf[:, :, :].rearrange("p g j -> p j g"), 3, 16))\
               .then_inc(w_dve, 1)

            def tap_step(tap, n):
                if tap == 0:
                    dve.wait_ge(xn_ready, IMAGES if not isinstance(n, int) else min(n + 1, IMAGES))
                    if positive(n):
                        dve.wait_ge(xd_high, n)
                    if positive(n):
                        dve.wait_ge(xd_ready, n)
                if positive(TAPS * n + tap):
                    dve.wait_ge(taps_done, TAPS * n + tap)
                src = xpad[:, n, tap // 3:tap // 3 + H, tap % 3:tap % 3 + W]
                if tap == 0:
                    dve.tensor_scalar(conv[:, :, :], src, dw[:, 0:1], dw_bias[:, 0:1],
                                      ALU.mult, ALU.add).then_inc(taps_done, 1)
                else:
                    dve.scalar_tensor_tensor(out=conv[:, :, :], in0=src, scalar=dw[:, tap:tap + 1],
                                             in1=conv[:, :, :], op0=ALU.mult, op1=ALU.add)\
                       .then_inc(taps_done, 1)

            def hat_y(k, n, par):
                dve.wait_ge(y_abs, CHUNKS * n + k + 1)
                v = a_l[par][:, fma(k), :].bitcast(F32)
                dve.tensor_scalar(v, v, 1.0, 1.0, ALU.min, ALU.subtract).then_inc(y_hat, 1)

            def masked(k, n, par):
                dve.wait_ge(y_hat, CHUNKS * n + k + 1)
                dve.wait_ge(mask_ps, CHUNKS * n + k + 1)
                w = min(2, TAPS - 2 * k) * PIX
                v = a_l[par][:, fma(k), :].bitcast(F32).rearrange("p t x -> p (t x)")
                dve.tensor_tensor(v, ps_m[:, 0:w], v, ALU.mult).then_inc(a_full, 1)

            def hat_x(k, n, par):
                dve.wait_ge(x_abs, CHUNKS * n + k + 1)
                v = b_l[par][:, fma(k), :].bitcast(F32)
                dve.tensor_scalar(v, v, 1.0, 1.0, ALU.min, ALU.subtract).then_inc(x_hat, 1)

            def x_rep_low(half, n):
                dve.wait_ge(xrep_high, 2 * n + half + 1)
                dve.tensor_tensor(xrep[64:P, :, :, :],
                                  spread(xpad[64:P, n, 1 + 8 * half:9 + 8 * half, 1:W + 1], 2, 8),
                                  xrep[64:P, :, :, :].bitcast(F32), ALU.subtract).then_inc(xrep_ready, 1)

            def v_out(half, n):
                dve.wait_ge(v_ps, 2 * n + half + 1)
                if positive(QUARTETS * n):
                    dve.wait_ge(vt_ready, QUARTETS * n)
                v = ps_m[:, :].rearrange("p (y q j c) -> p y q j c", y=8, q=QUARTETS, j=QUART)
                for j in range(QUART):
                    r = slice(32 * j, 32 * j + 32)
                    op = dve.tensor_tensor(v_sb[r, 8 * half:8 * half + 8, :, :], v[r, :, :, j, :],
                                           spread(vp_bias[r, :, :], 1, 8), ALU.add)
                op.then_inc(v_done, 1)

            def weight(u, i):
                dve.wait_ge(t_ready, UPI * i + u + 1)
                dve.wait_ge(a_copied, 2 * (UPI * i + u) + 2)
                if positive(UPI // 2 * i + (u - 3) // 2 + 1):
                    dve.wait_ge(reduced, UPI // 2 * i + (u - 3) // 2 + 1)
                dve.tensor_tensor(prod[u % 3][:, :], ps_t[u % 2][:, :], a_rep[u % 2][:, :], ALU.mult)\
                   .then_inc(weighted, 1)

            def residual(i):
                dve.wait_ge(out_ps, i + 1)
                t = t_tok[:, bass.ds(TPI * i, TPI), :].rearrange("p t c -> p (t c)")
                dve.tensor_tensor(t, ps_m[:, 0:TPI * C], t, ALU.add).then_inc(t_done, 1)

            def image(i, par, made, ahead):
                n, npar = i + 1, 1 - par
                for u in range(UPI):
                    if made and u < 2 * CHUNKS and u % 2:
                        masked(u // 2, n, npar)
                    weight(u, i)
                    if made and u < 2 * CHUNKS:
                        (hat_x if u % 2 else hat_y)(u // 2, n, npar)
                    if u == 10 and not (isinstance(i, int) and i == 0):
                        residual(i - 1)
                    if made and u in (10, 13):
                        x_rep_low(u // 13, n)
                    if made and u in (12, 15):
                        v_out(u // 15, n)
                    if ahead and 8 <= u < 8 + TAPS:
                        tap_step(u - 8, i + 2)

            dve.wait_ge(tokens_in, 16)
            for tap in range(TAPS):
                tap_step(tap, 0)
            x_rep_low(0, 0)
            for k in range(CHUNKS):
                hat_y(k, 0, 0)
                masked(k, 0, 0)
                hat_x(k, 0, 0)
            for tap in range(TAPS):
                tap_step(tap, 1)
            v_out(0, 0)
            x_rep_low(1, 0)
            v_out(1, 0)
            image(0, 0, True, True)
            image(1, 1, True, True)
            with dve.Fori(1, IMAGES // 2 - 1) as it:
                for par in range(2):
                    image(2 * it + par, par, True, True)
            image(IMAGES - 2, 0, True, False)
            image(IMAGES - 1, 1, False, False)
            residual(IMAGES - 1)

        @block.gpsimd
        def _(pool):
            pool.memset(bias_f[:, :, :], 0.0).then_inc(zeroed, 1)
            pool.memset(bias_sel[:, :, :], 0.0).then_inc(zeroed, 1)
            pool.memset(minus_half[:, :], -0.5).then_inc(zeroed, 1)
            pool.memset(xpad[:, :, :, :], 0.0).then_inc(zeroed, 1)
            pool.memset(vt_h[:, :, :, :].bitcast(F32), 0.0).then_inc(zeroed, 1)
            pool.memset(vt_l[:, :, :, :].bitcast(F32), 0.0).then_inc(zeroed, 1)
            pool.wait_ge(zeroed, 6)
            pool.wait_ge(gn_steps, 5)
            pool.tensor_tensor(grstd[:, :], gvar_eps[:, :], minus_half[:, :], ALU.pow).then_inc(gn_pow, 1)

            def xd_low(n, par):
                if isinstance(n, int) and n < 2:
                    if positive(n):
                        pool.wait_ge(vt_ready, n)
                else:
                    pool.wait_ge(vt_ready, QUARTETS * (n - 1) + 1)
                pool.wait_ge(xd_high, n + 1)
                pool.tensor_tensor(xd[par][64:P, :], conv[64:P, :, :].rearrange("p y x -> p (y x)"),
                                   xd[par][64:P, :].bitcast(F32), ALU.subtract).then_inc(xd_ready, 1)

            def low_parts(k, n, par):
                if k == 0:
                    if isinstance(n, int) and n == 0:
                        pool.wait_ge(xd_ready, 1)
                    else:
                        pool.wait_ge(vt_ready, QUARTETS * n)
                for full, high, high_done, low_done in ((a_l, a_h, a_high, a_low), (b_l, b_h, b_high, b_low)):
                    pool.wait_ge(high_done, CHUNKS * n + k + 1)
                    pool.tensor_tensor(full[par][:, fma(k), :], full[par][:, fma(k), :].bitcast(F32),
                                       high[par][:, fma(k), :].bitcast(F32), ALU.subtract).then_inc(low_done, 1)

            def vt_low(q, n):
                if q:
                    pool.wait_ge(xd_ready, n + 2 if not isinstance(n, int) else min(n + 2, IMAGES))
                    pool.wait_ge(vt_ready, QUARTETS * n + 1)
                else:
                    pool.wait_ge(b_low, CHUNKS * (n + 1))
                pool.wait_ge(vt_high, QUARTETS * n + q + 1)
                for j in range(QUART):
                    r = slice(32 * j, 32 * j + 32)
                    g = QUART * q + j
                    op = pool.tensor_tensor(vt_l[r, g, :, :], v_sb[r, :, q, :], vt_h[r, g, :, :].bitcast(F32),
                                            ALU.subtract)
                op.then_inc(vt_ready, 1)

            def image(i, par, made, ahead):
                n, npar = i + 1, 1 - par
                vt_low(1, i)
                if made:
                    for k in range(CHUNKS):
                        low_parts(k, n, npar)
                if made:
                    vt_low(0, n)
                if ahead:
                    xd_low(i + 2, par)

            xd_low(0, 0)
            for k in range(CHUNKS):
                low_parts(k, 0, 0)
            vt_low(0, 0)
            xd_low(1, 1)
            image(0, 0, True, True)
            image(1, 1, True, True)
            with pool.Fori(1, IMAGES // 2 - 1) as it:
                for par in range(2):
                    image(2 * it + par, par, True, True)
            image(IMAGES - 2, 0, True, False)
            image(IMAGES - 1, 1, False, False)


def attention_stage(nc, d, t_tok, xf, disp):
    with ExitStack() as ctx:
        def sb(name, shape, dt=F32):
            return ctx.enter_context(nc.sbuf_tensor(name, shape, dt))

        def ps(name):
            return ctx.enter_context(nc.psum_tensor(name, [P, BANK], F32))

        def sem(name):
            return ctx.enter_context(nc.semaphore(name))

        ident = sb("ident2", [P, P])
        wf = {n: sb(f"{n}_f", [P, w]) for n, w in (("q_w", P), ("k_w", P), ("v_w", C), ("gate_w", EXPERTS))}
        wh = {n: sb(f"{n}_h", list(t.shape), F32R) for n, t in wf.items()}
        wl = {n: sb(f"{n}_l", list(t.shape), F32R) for n, t in wf.items()}
        q_bias = sb("q_bias", [P, 1])
        k_bias = sb("k_bias", [P, 1])
        v_bias = sb("v_bias", [P, C])
        gate_bias = sb("gate_bias", [P, EXPERTS])
        minus_half = sb("minus_half2", [P, TPI])
        two = range(2)
        stats = [sb(f"ln_stats{s}", [P, TPI, 6]) for s in two]
        moments = [sb(f"ln_moments{s}", [P, TPI, 2]) for s in two]
        var_eps = [sb(f"ln_var{s}", [P, TPI]) for s in two]
        rstd = [sb(f"ln_rstd{s}", [P, TPI]) for s in two]
        normed = [sb(f"ln_out{s}", [P, TPI, 2, C]) for s in two]
        xs = [sb(f"xs{s}", [P, PIX], F32R) for s in two]
        q_s = sb("q_s", [P, PIX], F32R)
        k_h = sb("k_h", [P, PIX], F32R)
        k_l = sb("k_l", [P, PIX], F32R)
        v_sb = [sb(f"v_tok{s}", [P, TPI, C]) for s in two]
        top = sb("score_max", [P, TPI])
        ntop = sb("score_nmax", [P, TPI])
        prob = sb("prob", [P, TPI, PIX])
        psum_row = sb("prob_sum", [P, TPI])
        rsum = sb("prob_rsum", [P, TPI])
        prob_t = sb("prob_t", [P, TPI, PIX])
        logit = sb("logit", [P, TPI, EXPERTS])
        ltop = sb("logit_max", [P, TPI])
        nltop = sb("logit_nmax", [P, TPI])
        gexp = sb("gexp", [P, TPI, EXPERTS + 6])
        grest = sb("grest", [P, TPI, EXPERTS + 6])
        top8 = sb("top8", [P, TPI, 8])
        top2 = sb("top2", [P, TPI, 8])
        held = sb("held", [P, 1])
        gsel = sb("gsel", [P, TPI, EXPERTS])
        tsum = sb("tsum", [P, TPI])
        trec = sb("trec", [P, TPI])
        dwide = sb("dwide", [P, TPI, P])

        ps_x = [ps("ps_x0")[:, 0:PIX], ps("ps_x1")[:, 0:PIX]]
        ps_qk = ps("ps_qk")[:, :].rearrange("p (w x) -> p w x", w=2)
        ps_v = ps("ps_v")[:, 0:TPI * C].rearrange("p (t c) -> p t c", t=TPI)
        ps_s = ps("ps_s")[:, :].rearrange("p (t x) -> p t x", t=TPI)
        ps_p = ps("ps_p")[:, :].rearrange("p (t x) -> p t x", t=TPI)
        ps_o = ps("ps_o")[:, 0:TPI * C].rearrange("p (t c) -> p t c", t=TPI)
        ps_g = ps("ps_g")
        ps_logit = ps_g[:, 0:TPI * EXPERTS]
        ps_disp = ps_g[:, PIX:2 * PIX]

        weights_in = sem("weights_in2")
        cleared = sem("cleared2")
        w_high = sem("w_high")
        w_low = sem("w_low")
        ln_stat = [sem(f"ln_stat{s}") for s in two]
        ln_pow = [sem(f"ln_pow{s}") for s in two]
        ln_done = [sem(f"ln_done{s}") for s in two]
        x_ps = [sem(f"x_ps{s}") for s in two]
        x_high = [sem(f"x_high{s}") for s in two]
        x_low = [sem(f"x_low{s}") for s in two]
        qk_ps = sem("qk_ps")
        v_ps = sem("v_ps2")
        q_high = sem("q_high")
        k_high = sem("k_high")
        q_low = sem("q_low")
        k_low = sem("k_low")
        v_done = sem("v_done2")
        s_ps = sem("s_ps")
        max_step = sem("max_step")
        exp_done = sem("exp_done")
        p_ps = sem("p_ps")
        p_done = sem("p_done")
        rsum_done = sem("rsum_done")
        o_ps = sem("o_ps")
        res_done = sem("res_done")
        xf_done = sem("xf_done")
        g_ps = sem("g_ps")
        g_step = sem("g_step")
        g_exp = sem("g_exp")
        d_step = sem("d_step")
        d_ps = sem("d_ps")
        d_high = sem("d_high")
        d_low = sem("d_low")

        block = ctx.enter_context(nc.Block())

        def rounds(s1, s2, s3):
            def body(i, run1, run2, run3):
                for r in range(5):
                    if run1 and r < len(s1):
                        s1[r](i)
                    if run2 and r < len(s2):
                        s2[r](i - 1)
                    if run3 and r < len(s3):
                        s3[r](i - 2)
            return body

        @block.sync
        def _(sp):
            for dst, src in ((ident[:, :], d["ident"]), (wf["q_w"][:, :], d["q_w"]), (wf["k_w"][:, :], d["k_w"]),
                             (wf["v_w"][:, :], d["v_w"]), (wf["gate_w"][:, :], d["gate_w"]),
                             (q_bias[:, :], d["q_bias"]), (k_bias[:, :], d["k_bias"]),
                             (v_bias[:, :], d["v_bias"]), (gate_bias[:, :], d["gate_bias"])):
                sp.dma_start(dst, src).then_inc(weights_in, 16)

        def in_flight(eng, body):
            body(0, True, False, False)
            body(1, True, True, False)
            body(2, True, True, True)
            with eng.Fori(3, IMAGES) as i:
                body(i, True, True, True)
            body(IMAGES, False, True, True)
            body(IMAGES + 1, False, False, True)

        @block.vector
        def _(dve):
            def hold(s, value):
                dve.wait_ge(s, value)
                dve.memset(held[:, :], 0.0)

            def ln_stats(s, i, before):
                if before is not None:
                    hold(before, TPI * (i + 1))
                for t in range(TPI):
                    dve.bn_stats(stats[s][:, t, :], t_tok[:, TPI * i + t, :]).then_inc(ln_stat[s], 1)
                hold(ln_stat[s], 5 * i + 2)
                for t in range(TPI):
                    dve.bn_aggr(moments[s][:, t, :], stats[s][:, t, :]).then_inc(ln_stat[s], 1)
                dve.wait_ge(ln_stat[s], 5 * i + 4)
                dve.tensor_scalar(var_eps[s][:, :], moments[s][:, :, 1], LN_EPS, None, ALU.add)\
                   .then_inc(ln_stat[s], 1)

            def ln_apply(s, i):
                dve.wait_ge(ln_pow[s], i + 1)
                if positive(i):
                    dve.wait_ge(x_ps[s], i)
                for t in range(TPI):
                    op = dve.tensor_scalar(normed[s][:, t, :, :], spread(t_tok[:, TPI * i + t, :], 1, 2),
                                           moments[s][:, t, 0:1], rstd[s][:, t:t + 1],
                                           ALU.subtract, ALU.mult)
                op.then_inc(ln_done[s], 1)

            def x_split(s, i):
                dve.wait_ge(x_high[s], i + 1)
                dve.tensor_tensor(xs[s][64:P, :], ps_x[s][64:P, :], xs[s][64:P, :].bitcast(F32), ALU.subtract)\
                   .then_inc(x_low[s], 1)

            def qkv_low(i):
                dve.wait_ge(k_high, i + 1)
                dve.scalar_tensor_tensor(out=q_s[64:P, :], in0=ps_qk[64:P, 0, :], scalar=q_bias[64:P, 0:1],
                                         in1=q_s[64:P, :].bitcast(F32), op0=ALU.add, op1=ALU.subtract)\
                   .then_inc(q_low, 1)
                dve.scalar_tensor_tensor(out=k_l[:, :], in0=ps_qk[:, 1, :], scalar=k_bias[:, 0:1],
                                         in1=k_h[:, :].bitcast(F32), op0=ALU.add, op1=ALU.subtract)\
                   .then_inc(k_low, 1)
                dve.wait_ge(v_ps, i + 1)
                if positive(i):
                    dve.wait_ge(o_ps, i)
                dve.tensor_tensor(v_sb[0][:, :, :], ps_v[:, :, :], spread(v_bias[:, :], 1, TPI), ALU.add)\
                   .then_inc(v_done, 1)

            def score_max(i):
                dve.wait_ge(s_ps, i + 1)
                if positive(TPI * i):
                    dve.wait_ge(exp_done, TPI * i)
                dve.tensor_reduce(top[:, :], ps_s[:, :, :], AX_X, ALU.max).then_inc(max_step, 1)
                dve.wait_ge(max_step, 2 * i + 1)
                dve.tensor_scalar(ntop[:, :], top[:, :], -SCALE, None, ALU.mult).then_inc(max_step, 1)

            def add_values(i):
                dve.wait_ge(exp_done, TPI * (i + 1))
                dve.reciprocal(rsum[:, :], psum_row[:, :]).then_inc(rsum_done, 1)
                dve.wait_ge(rsum_done, i + 1)
                dve.wait_ge(o_ps, i + 1)
                for t in range(TPI):
                    tok = t_tok[:, TPI * i + t, :]
                    dve.scalar_tensor_tensor(out=tok, in0=ps_o[:, t, :], scalar=rsum[:, t:t + 1], in1=tok,
                                             op0=ALU.mult, op1=ALU.add).then_inc(res_done, 1)

            def gate_logits(i):
                x_split(1, i)
                dve.wait_ge(g_ps, i + 1)
                dve.tensor_tensor(logit[:, :, :], ps_logit.rearrange("p (t e) -> p t e", t=TPI),
                                  spread(gate_bias[:, :], 1, TPI), ALU.add).then_inc(g_step, 1)
                dve.wait_ge(g_step, 3 * i + 1)
                dve.tensor_reduce(ltop[:, :], logit[:, :, :], AX_X, ALU.max).then_inc(g_step, 1)
                dve.wait_ge(g_step, 3 * i + 2)
                dve.tensor_scalar(nltop[:, :], ltop[:, :], -1.0, None, ALU.mult).then_inc(g_step, 1)

            def top_two(i):
                hold(g_exp, TPI * (i + 1))
                base = 12 * i
                for t in range(TPI):
                    dve.max(top8[:, t, :], gexp[:, t, 0:EXPERTS]).then_inc(d_step, 1)
                dve.wait_ge(d_step, base + 2)
                dve.tensor_copy(top2[:, :, 0:2], top8[:, :, 0:2]).then_inc(d_step, 1)
                dve.tensor_tensor(tsum[:, :], top8[:, :, 0], top8[:, :, 1], ALU.add).then_inc(d_step, 1)
                hold(d_step, base + 4)
                for t in range(TPI):
                    dve.match_replace(grest[:, t, :], top2[:, t, :], gexp[:, t, :], 0.0).then_inc(d_step, 1)
                dve.reciprocal(trec[:, :], tsum[:, :]).then_inc(d_step, 1)
                dve.wait_ge(d_step, base + 7)
                dve.tensor_tensor(gsel[:, :, :], gexp[:, :, 0:EXPERTS], grest[:, :, 0:EXPERTS], ALU.subtract)\
                   .then_inc(d_step, 1)
                dve.wait_ge(d_step, base + 8)
                if positive(i):
                    dve.wait_ge(d_ps, i)
                for t in range(TPI):
                    for half in range(2):
                        dve.tensor_scalar(dwide[:, t, 32 * half:32 * half + EXPERTS], gsel[:, t, :],
                                          trec[:, t:t + 1], None, ALU.mult).then_inc(d_step, 1)

            def disp_low(i):
                dve.wait_ge(d_high, i + 1)
                rows = disp[32:32 + EXPERTS, bass.ds(PIX * i, PIX)]
                dve.tensor_tensor(rows, ps_disp[32:32 + EXPERTS, :], rows.bitcast(F32), ALU.subtract)\
                   .then_inc(d_low, 1)

            s1 = [lambda i: ln_stats(0, i, None), lambda i: ln_apply(0, i), lambda i: x_split(0, i), qkv_low]
            s2 = [score_max, lambda i: None, add_values, lambda i: ln_stats(1, i, res_done),
                  lambda i: ln_apply(1, i)]
            s3 = [gate_logits, top_two, disp_low]

            dve.wait_ge(weights_in, 16 * 9)
            dve.wait_ge(w_high, 4)
            for n in wf:
                dve.tensor_tensor(wl[n][:, :], wf[n][:, :], wh[n][:, :].bitcast(F32), ALU.subtract)\
                   .then_inc(w_low, 1)
            dve.wait_ge(cleared, 5)
            in_flight(dve, rounds(s1, s2, s3))

        @block.gpsimd
        def _(pool):
            pool.memset(minus_half[:, :], -0.5).then_inc(cleared, 1)
            pool.memset(gexp[:, :, EXPERTS:EXPERTS + 6], -1.0).then_inc(cleared, 1)
            pool.memset(top2[:, :, :], -1.0).then_inc(cleared, 1)
            pool.memset(dwide[:, :, :], 0.0).then_inc(cleared, 1)
            pool.memset(grest[:, :, :], 0.0).then_inc(cleared, 1)
            pool.wait_ge(cleared, 5)

            def power(s, i):
                pool.wait_ge(ln_stat[s], 5 * (i + 1))
                if positive(i):
                    pool.wait_ge(ln_done[s], i)
                pool.tensor_tensor(rstd[s][:, :], var_eps[s][:, :], minus_half[:, :], ALU.pow)\
                    .then_inc(ln_pow[s], 1)

            def keep_x(i):
                pool.wait_ge(x_low[1], i + 1)
                pool.tensor_copy(xf[:, bass.ds(PIX * i, PIX)], xs[1][:, :].bitcast(F32)).then_inc(xf_done, 1)

            skip = lambda i: None
            in_flight(pool, rounds([lambda i: power(0, i)], [skip, skip, skip, lambda i: power(1, i)],
                                   [keep_x]))

        @block.scalar
        def _(act):
            act.wait_ge(weights_in, 16 * 9)
            for n in wf:
                act.activation(wh[n][:, :], wf[n][:, :], ACT.Copy).then_inc(w_high, 1)

            def high(s, i):
                act.wait_ge(x_ps[s], i + 1)
                if s:
                    if positive(i):
                        act.wait_ge(xf_done, i)
                    if positive(i):
                        act.wait_ge(g_ps, i)
                else:
                    if positive(i):
                        act.wait_ge(v_ps, i)
                act.activation(xs[s][:, :], ps_x[s][:, :], ACT.Copy).then_inc(x_high[s], 1)

            def qk_high(i):
                act.wait_ge(qk_ps, i + 1)
                if positive(i):
                    act.wait_ge(s_ps, i)
                act.activation(q_s[:, :], ps_qk[:, 0, :], ACT.Identity, bias=q_bias[:, 0:1]).then_inc(q_high, 1)
                act.activation(k_h[:, :], ps_qk[:, 1, :], ACT.Identity, bias=k_bias[:, 0:1]).then_inc(k_high, 1)

            def exps(i):
                act.wait_ge(max_step, 2 * i + 2)
                if positive(i):
                    act.wait_ge(p_ps, i)
                if positive(i):
                    act.wait_ge(rsum_done, i)
                for t in range(TPI):
                    act.activation(prob[:, t, :], ps_s[:, t, :], ACT.Exp, bias=ntop[:, t:t + 1], scale=SCALE,
                                   accum_out=psum_row[:, t:t + 1]).then_inc(exp_done, 1)

            def copy_p(i):
                act.wait_ge(p_ps, i + 1)
                if positive(i):
                    act.wait_ge(o_ps, i)
                act.activation(prob_t[:, :, :], ps_p[:, :, :], ACT.Copy).then_inc(p_done, 1)

            def gate_exp(i):
                act.wait_ge(g_step, 3 * i + 3)
                if positive(12 * i):
                    act.wait_ge(d_step, 12 * i)
                for t in range(TPI):
                    act.activation(gexp[:, t, 0:EXPERTS], logit[:, t, :], ACT.Exp, bias=nltop[:, t:t + 1])\
                       .then_inc(g_exp, 1)

            def disp_high(i):
                act.wait_ge(d_ps, i + 1)
                act.activation(disp[:, bass.ds(PIX * i, PIX)], ps_disp, ACT.Copy).then_inc(d_high, 1)

            skip = lambda i: None
            in_flight(act, rounds([skip, lambda i: high(0, i), qk_high],
                                  [exps, copy_p, skip, skip, lambda i: high(1, i)],
                                  [skip, gate_exp, disp_high]))

        @block.tensor
        def _(pe):
            pe.wait_ge(weights_in, 16 * 9)
            pe.wait_ge(w_low, 4)
            pe.wait_ge(cleared, 5)

            def turn(s, i):
                pe.wait_ge(ln_done[s], i + 1)
                if positive(i):
                    pe.wait_ge(x_low[s], i)
                for t in range(TPI):
                    mm = pe.transpose(ps_x[s][:, t * P:(t + 1) * P],
                                      normed[s][:, t, :, :].rearrange("p a c -> p (a c)"), ident[:, :])
                mm.then_inc(x_ps[s], 1)

            def project(i):
                pe.wait_ge(x_low[0], i + 1)
                if positive(i):
                    pe.wait_ge(q_low, i)
                if positive(i):
                    pe.wait_ge(k_low, i)
                for c, n in enumerate(("q_w", "k_w")):
                    for w, first in ((wh[n], True), (wl[n], False)):
                        mm = pe.matmul(ps_qk[:, c, :], w[:, :], xs[0][:, :], start=first, stop=not first)
                mm.then_inc(qk_ps, 1)
                if positive(i):
                    pe.wait_ge(v_done, i)
                for t in range(TPI):
                    for w, first in ((wh["v_w"], True), (wl["v_w"], False)):
                        mm = pe.matmul(ps_v[:, t, :], xs[0][:, t * P:(t + 1) * P], w[:, :],
                                       start=first, stop=not first)
                mm.then_inc(v_ps, 1)

            def scores(i):
                pe.wait_ge(q_low, i + 1)
                pe.wait_ge(k_low, i + 1)
                if positive(TPI * i):
                    pe.wait_ge(exp_done, TPI * i)
                for t in range(TPI):
                    for k, first in ((k_h, True), (k_l, False)):
                        mm = pe.matmul(ps_s[:, t, :], q_s[:, t * P:(t + 1) * P], k[:, :],
                                       start=first, stop=not first)
                mm.then_inc(s_ps, 1)

            def turn_p(i):
                pe.wait_ge(exp_done, TPI * (i + 1))
                if positive(i):
                    pe.wait_ge(p_done, i)
                for t in range(TPI):
                    for k in range(TPI):
                        mm = pe.transpose(ps_p[:, k, t * P:(t + 1) * P], prob[:, t, k * P:(k + 1) * P],
                                          ident[:, :])
                mm.then_inc(p_ps, 1)

            def values(i):
                pe.wait_ge(p_done, i + 1)
                pe.wait_ge(v_done, i + 1)
                if positive(TPI * i):
                    pe.wait_ge(res_done, TPI * i)
                for t in range(TPI):
                    for k in range(TPI):
                        mm = pe.matmul(ps_o[:, t, :], prob_t[:, k, t * P:(t + 1) * P], v_sb[0][:, k, :],
                                       start=k == 0, stop=k == TPI - 1)
                mm.then_inc(o_ps, 1)

            def gate(i):
                pe.wait_ge(x_low[1], i + 1)
                if positive(i):
                    pe.wait_ge(d_low, i)
                for t in range(TPI):
                    for w, first in ((wh["gate_w"], True), (wl["gate_w"], False)):
                        mm = pe.matmul(ps_logit[:, t * EXPERTS:(t + 1) * EXPERTS],
                                       xs[1][:, t * P:(t + 1) * P], w[:, :], start=first, stop=not first)
                mm.then_inc(g_ps, 1)

            def turn_d(i):
                pe.wait_ge(d_step, 12 * (i + 1))
                if positive(i):
                    pe.wait_ge(d_low, i)
                for t in range(TPI):
                    mm = pe.transpose(ps_disp[:, t * P:(t + 1) * P], dwide[:, t, :], ident[:, :])
                mm.then_inc(d_ps, 1)

            skip = lambda i: None
            in_flight(pe, rounds([skip, lambda i: turn(0, i), project],
                                 [scores, turn_p, values, skip, lambda i: turn(1, i)],
                                 [gate, skip, turn_d]))


def expert_stage(nc, d, out, t_tok, xf, disp):
    PAIRS, CH = IMAGES * PIX // (2 * BANK), 2
    UNITS = EXPERTS * CH
    with ExitStack() as ctx:
        def sb(name, shape, dt=F32):
            return ctx.enter_context(nc.sbuf_tensor(name, shape, dt))

        def sem(name):
            return ctx.enter_context(nc.semaphore(name))

        ident = sb("ident3", [P, P])
        w_f = [sb(f"w{k}_f", [P, EXPERTS, HIDDEN]) for k in (1, 2)]
        w_h = [sb(f"w{k}_h", [P, EXPERTS, HIDDEN], F32R) for k in (1, 2)]
        w_l = [sb(f"w{k}_l", [P, EXPERTS, HIDDEN], F32R) for k in (1, 2)]
        w3 = sb("w3", [P, EXPERTS, C])
        sel_f = sb("sel_f", [P, EXPERTS, P])
        sel = sb("sel", [P, EXPERTS, P], F32R)
        gated = [sb(f"gated{c}", [P, BANK]) for c in range(CH)]
        scaled = [sb(f"scaled{c}", [P, BANK]) for c in range(CH)]
        hidden = [sb(f"hidden{c}", [P, BANK]) for c in range(2 * CH)]
        y_sb = sb("y_sb", [P, BANK])

        def bank(name):
            return ctx.enter_context(nc.psum_tensor(name, [P, BANK], F32))

        ps_h1 = [bank(f"ps_h1{c}") for c in range(CH)]
        ps_h2 = [bank(f"ps_h2{c}") for c in range(CH)]
        ps_w = [bank(f"ps_w{c}") for c in range(CH)]
        ps_y = bank("ps_y")
        ps_z = bank("ps_z")

        weights_in = sem("weights_in3")
        w_high = sem("w_high3")
        w_low = sem("w_low3")
        h1_ps = sem("h1_ps")
        h2_ps = sem("h2_ps")
        w_ps = sem("w_ps")
        silu_done = sem("silu_done")
        scaled_done = sem("scaled_done")
        hidden_done = sem("hidden_done")
        y_ps = sem("y_ps")
        y_copied = sem("y_copied")
        z_ps = sem("z_ps")
        added = sem("added")
        stored = sem("stored")

        out_view = out.rearrange("n h w c -> (n h w) c").rearrange("(t p) c -> p t c", p=P)
        TPP = 2 * BANK // P

        block = ctx.enter_context(nc.Block())

        @block.sync
        def _(sp):
            for dst, src in ((w_f[0][:, :, :], d["w1"].rearrange("p (e h) -> p e h", e=EXPERTS)),
                             (w_f[1][:, :, :], d["w2"].rearrange("p (e h) -> p e h", e=EXPERTS)),
                             (sel_f[:, :, :], d["sel"].rearrange("p (e h) -> p e h", e=EXPERTS)),
                             (w3[:, :, :], d["w3"].rearrange("p (e c) -> p e c", e=EXPERTS)),
                             (ident[:, :], d["ident"])):
                sp.dma_start(dst, src).then_inc(weights_in, 16)
            for pair in range(PAIRS):
                sp.wait_ge(added, pair + 1)
                sp.dma_start(out_view[:, TPP * pair:TPP * (pair + 1), :],
                             t_tok[:, TPP * pair:TPP * (pair + 1), :]).then_inc(stored, 16)
            sp.wait_ge(stored, 16 * PAIRS)

        @block.tensor
        def _(pe):
            pe.wait_ge(weights_in, 16 * 5)
            pe.wait_ge(w_low, 2)
            pe.wait_ge(w_high, 3)

            def output(e, pair):
                pe.wait_ge(hidden_done, UNITS * pair + CH * (e + 1))
                for c in range(CH):
                    mm = pe.matmul(ps_y[64 * c:64 * c + 64, :], w3[:, e, :], hidden[CH * (e % 2) + c][:, :],
                                   start=e == 0, stop=e == EXPERTS - 1)
                mm.then_inc(y_ps, 1)

            for pair in range(PAIRS):
                if positive(pair):
                    pe.wait_ge(y_copied, pair)
                if positive(pair):
                    pe.wait_ge(added, pair)
                for e in range(EXPERTS):
                    for c in range(CH):
                        u = CH * e + c
                        cols = bass.ds(BANK * (2 * pair + c), BANK)
                        if positive(UNITS * pair + max(u - CH + 1, 0)):
                            pe.wait_ge(hidden_done, UNITS * pair + max(u - CH + 1, 0))
                        for k, (out_ps, signal) in enumerate(((ps_h1[c], h1_ps), (ps_h2[c], h2_ps))):
                            for w, first in ((w_h[k], True), (w_l[k], False)):
                                mm = pe.matmul(out_ps[:, :], w[:, e, :], xf[:, cols], start=first, stop=not first)
                            mm.then_inc(signal, 1)
                        pe.matmul(ps_w[c][:, :], sel[:, e, :], disp[:, cols], start=True, stop=True)\
                          .then_inc(w_ps, 1)
                    if e:
                        output(e - 1, pair)
                output(EXPERTS - 1, pair)
                pe.wait_ge(y_copied, pair + 1)
                for t in range(TPP // 2):
                    mm = pe.transpose(ps_z[:, t * P:(t + 1) * P], y_sb[:, t * P:(t + 1) * P], ident[:, :])
                mm.then_inc(z_ps, 1)

        @block.scalar
        def _(act):
            act.wait_ge(weights_in, 16 * 5)
            for k in range(2):
                act.activation(w_h[k][:, :, :], w_f[k][:, :, :], ACT.Copy).then_inc(w_high, 1)
            act.activation(sel[:, :, :], sel_f[:, :, :], ACT.Copy).then_inc(w_high, 1)
            for pair in range(PAIRS):
                for u in range(UNITS):
                    c = u % CH
                    act.wait_ge(h1_ps, UNITS * pair + u + 1)
                    if positive(UNITS * pair + max(u - CH + 1, 0)):
                        act.wait_ge(scaled_done, UNITS * pair + max(u - CH + 1, 0))
                    act.activation(gated[c][:, :], ps_h1[c][:, :], ACT.Silu).then_inc(silu_done, 1)
                act.wait_ge(y_ps, EXPERTS * (pair + 1))
                if positive(pair):
                    act.wait_ge(z_ps, pair)
                act.activation(y_sb[:, :], ps_y[:, :], ACT.Copy).then_inc(y_copied, 1)

        @block.vector
        def _(dve):
            for k in range(2):
                dve.wait_ge(w_high, k + 1)
                dve.tensor_tensor(w_l[k][:, :, :], w_f[k][:, :, :], w_h[k][:, :, :].bitcast(F32), ALU.subtract)\
                   .then_inc(w_low, 1)
            for pair in range(PAIRS):
                for u in range(UNITS):
                    c, e = u % CH, u // CH
                    dve.wait_ge(silu_done, UNITS * pair + u + 1)
                    dve.wait_ge(w_ps, UNITS * pair + u + 1)
                    if positive(UNITS * pair + max(u - CH + 1, 0)):
                        dve.wait_ge(hidden_done, UNITS * pair + max(u - CH + 1, 0))
                    dve.tensor_tensor(scaled[c][:, :], ps_w[c][:, :], gated[c][:, :], ALU.mult)\
                       .then_inc(scaled_done, 1)
                    dve.wait_ge(scaled_done, UNITS * pair + u + 1)
                    dve.wait_ge(h2_ps, UNITS * pair + u + 1)
                    if positive(EXPERTS * pair + max(e - 1, 0)):
                        dve.wait_ge(y_ps, EXPERTS * pair + max(e - 1, 0))
                    dve.tensor_tensor(hidden[CH * (e % 2) + c][:, :], ps_h2[c][:, :], scaled[c][:, :], ALU.mult)\
                       .then_inc(hidden_done, 1)
                dve.wait_ge(z_ps, pair + 1)
                tok = t_tok[:, bass.ds(TPP * pair, TPP), :].rearrange("p (c t) o -> p c t o", c=CH)
                dve.tensor_tensor(tok, ps_z[:, :].rearrange("p (t c o) -> p c t o", c=CH, o=C), tok, ALU.add)\
                   .then_inc(added, 1)


def shape_arrays(np):
    ident = np.eye(P, dtype=np.float32)
    pair = np.zeros((P, P), np.float32)
    for r in range(P):
        pair[r, r] = pair[r, r ^ 1] = 0.5
    fold = np.zeros((P, QUARTETS, 32), np.float32)
    for q in range(QUARTETS):
        for c in range(GC):
            fold[c::GC, q, GC * q + c] = 1.0
    rep = np.zeros((P, QUART, P), np.float32)
    for j in range(QUART):
        for y in range(16):
            rep[32 * j + y, j, GC * y:GC * y + GC] = rep[32 * j + 16 + y, j, GC * y:GC * y + GC] = 1.0
    grid = np.zeros((P, H, W), np.float32)
    grid[[0, 32, 64, 96]] = 1.0
    grid[97] = np.arange(H)[:, None]
    grid[98] = np.arange(W)[None, :]
    place = np.zeros((3, OMJ, GROUPS, 16), np.float32)
    at = np.arange(16)
    for tap in range(TAPS):
        place[0, 2 * tap] = tap % 3 - 1 - at
        place[2, 2 * tap] = 1.0
        place[0, 2 * tap + 1] = tap // 3 - 1 - at
        place[1, 2 * tap + 1] = 1.0
    sel = np.zeros((P, EXPERTS, P), np.float32)
    for e in range(EXPERTS):
        sel[[e, 32 + e], e] = 1.0
    return {"ident": ident, "sel": sel.reshape(P, -1), "pair": pair, "fold": fold.reshape(P, -1), "rep": rep.reshape(P, -1),
            "grid": grid.reshape(P, -1), "place": place.reshape(3, -1)}


def laid_out(inputs, np):
    f = {k: np.asarray(v) for k, v in inputs.items()}
    twice = lambda a: np.ascontiguousarray(np.concatenate([a, a], 0))
    op = f["L0_conv_op_w"].reshape(QUARTETS, QUART, GC, C)
    op_w = np.zeros((QUART, 32, C), op.dtype)
    for q in range(QUARTETS):
        op_w[:, GC * q:GC * q + GC] = op[q]
    vb = f["L0_conv_vp_b"].reshape(QUARTETS, QUART, GC).transpose(1, 0, 2).reshape(QUART, 1, -1)
    rows = lambda v: np.ascontiguousarray(np.repeat(v.reshape(1, -1), P, 0))
    four = lambda m: np.ascontiguousarray(np.tile(m, (2, 2)))
    return {
        "q_w": four(f["L1_attn_Wq"].T), "k_w": four(f["L1_attn_Wk"].T), "v_w": twice(f["L1_attn_Wv"].T),
        "q_bias": twice(f["L1_attn_bq"].reshape(C, 1)), "k_bias": twice(f["L1_attn_bk"].reshape(C, 1)),
        "v_bias": rows(f["L1_attn_bv"]), "gate_w": twice(f["L1_ffn_gate_w"]), "gate_bias": rows(f["L1_ffn_gate_b"]),
        "w1": twice(f["L1_ffn_w1"].transpose(1, 0, 2).reshape(C, -1)),
        "w2": twice(f["L1_ffn_w2"].transpose(1, 0, 2).reshape(C, -1)),
        "w3": np.ascontiguousarray(f["L1_ffn_w3"].transpose(1, 0, 2).reshape(HIDDEN, -1)),
        "x": f["x"],
        "dw": twice(f["L0_conv_dw_w"].reshape(TAPS, C).T), "dw_bias": twice(f["L0_conv_dw_b"].reshape(C, 1)),
        "om_w": twice(f["L0_conv_om_w"]), "om_b": f["L0_conv_om_b"], "vp_w": twice(f["L0_conv_vp_w"]),
        "vp_bias": np.ascontiguousarray(np.repeat(vb, 32, 1).reshape(P, -1)),
        "op_w": np.ascontiguousarray(op_w.reshape(P, C)),
    }


def program(nc, d, out, until=3):
    with ExitStack() as ctx:
        t_tok = ctx.enter_context(nc.sbuf_tensor("t_tok", [P, TT, C], F32))
        conv_stage(nc, d, t_tok)
        if until > 1:
            xf = ctx.enter_context(nc.sbuf_tensor("xf", [P, IMAGES * PIX], F32R))
            disp = ctx.enter_context(nc.sbuf_tensor("disp", [P, IMAGES * PIX], F32R))
            attention_stage(nc, d, t_tok, xf, disp)
        if until > 2:
            expert_stage(nc, d, out, t_tok, xf, disp)
            return
        stored = ctx.enter_context(nc.semaphore("stored_debug"))
        block = ctx.enter_context(nc.Block())

        @block.sync
        def _(sp):
            sp.dma_start(out.rearrange("n h w c -> (n h w) c").rearrange("(t p) c -> p t c", p=P),
                         t_tok[:, :, :]).then_inc(stored, 16)
            sp.wait_ge(stored, 16)


def kernel(**inputs):
    import numpy as np
    import concourse.bacc as bacc
    from concourse.bass_utils import run_bass_kernel_spmd

    arrays = {**laid_out(inputs, np), **shape_arrays(np)}
    nc = bacc.Bacc("TRN2", target_bir_lowering=False, num_devices=1)
    d = {name: nc.dram_tensor(f"in_{name}", a.shape, mybir.dt.from_np(a.dtype), kind="ExternalInput").ap()
         for name, a in arrays.items()}
    out = nc.dram_tensor("out", (IMAGES, H, W, C), F32, kind="ExternalOutput").ap()
    program(nc, d, out)
    result = run_bass_kernel_spmd(nc, [{f"in_{name}": a for name, a in arrays.items()}], core_ids=[0])
    return result.results[0]["out"]
```

```python
from contextlib import ExitStack

import concourse.bass as bass
from concourse import mybir

F32 = mybir.dt.float32
F32R = mybir.dt.float32r
BF16 = mybir.dt.bfloat16
ALU = mybir.AluOpType
ACT = mybir.ActivationFunctionType
AX_X = mybir.AxisListType.X

P = 128
IMAGES, H, W, C = 8, 16, 16, 64
PIX = H * W
TT = IMAGES * PIX // P
TPI = PIX // P
GROUPS = 8
GC = C // GROUPS
TAPS = 9
OMJ = 3 * TAPS
QUART = 4
QUARTETS = GROUPS // QUART
COLS = TAPS * PIX
BANK = 512
PAIRS = (TAPS + 1) // 2
CPQ = QUART * COLS // BANK
CPI = CPQ * QUARTETS
SUM = 4
SPI = CPI // SUM
TRING, AREP, PROD = 3, 3, 8
FILL = 16 * 2 * QUART
EXPERTS, HIDDEN = 16, 128
SCALE = float(C) ** -0.5
GN_EPS, LN_EPS = 1e-5, 1e-5


def positive(value):
    return not isinstance(value, int) or value > 0


def count(eng, value):
    return value if isinstance(value, int) else eng.snap(value)


def spread(ap, dim, n):
    ap = ap.unsqueeze(dim)
    return ap.broadcast_to([n if k == dim else size for k, size in enumerate(ap.shape)])


KEEP = {"pair": P, "fold": QUARTETS * 32, "vp_w": C, "vp_bias": QUARTETS * GC, "op_w": C, "dw": TAPS, "dw_bias": 1}
START = {"om_w": GROUPS * OMJ, "om_b": GROUPS * OMJ, "rep": QUART * P, "grid": PIX}
KEEP_COLS, START_COLS = sum(KEEP.values()), sum(START.values())


def columns(pack):
    ends, end = [], 0
    for width in pack.values():
        ends.append(slice(end, end + width))
        end += width
    return ends


def conv_stage(nc, d, t_tok):
    with ExitStack() as ctx:
        def sb(name, shape, dt=F32, where=ctx):
            return where.enter_context(nc.sbuf_tensor(name, shape, dt))

        def sem(name):
            return ctx.enter_context(nc.semaphore(name))

        keep = sb("keep", [P, KEEP_COLS])
        at = dict(zip(KEEP, columns(KEEP)))
        pair = keep[:, at["pair"]]
        fold = keep[:, at["fold"]].rearrange("p (q c) -> p q c", q=QUARTETS)
        vp_f = keep[:, at["vp_w"]]
        vp_bias = keep[:, at["vp_bias"]].rearrange("p (q c) -> p q c", q=QUARTETS)
        op_w = keep[:, at["op_w"]]
        dw = keep[:, at["dw"]]
        dw_bias = keep[:, at["dw_bias"]]
        rep = sb("rep", [P, QUART, P], F32R)
        grid = sb("grid", [P, PIX], BF16)
        place = sb("place", [P, OMJ, GROUPS, 16], BF16)
        om_h = sb("om_h", [P, OMJ, GROUPS, 16], F32R)
        om_l = sb("om_l", [P, OMJ, GROUPS, 16], F32R)
        vp_h = sb("vp_h", [P, C], F32R)
        vp_l = sb("vp_l", [P, C], F32R)
        xpad = sb("xpad", [P, IMAGES, H + 2, W + 2])
        stats = sb("stats", [P, IMAGES, 6])
        chan = sb("chan", [P, IMAGES, 2])
        gmean = sb("gmean", [P, IMAGES])
        gdev = sb("gdev", [P, IMAGES])
        gsq = sb("gsq", [P, IMAGES])
        gvar = sb("gvar", [P, IMAGES])
        gvar_eps = sb("gvar_eps", [P, IMAGES])
        minus_half = sb("minus_half", [P, IMAGES])
        grstd = sb("grstd", [P, IMAGES])
        gshift = sb("gshift", [P, IMAGES])
        conv = sb("conv", [P, H, W])
        xd = [sb(f"xd{i}", [P, PIX], F32R) for i in range(2)]
        xrep = sb("xrep", [P, H // 2, 8, W], F32R)
        v_sb = sb("v_sb", [P, H, QUARTETS, GC])
        vt_h = sb("vt_h", [P, GROUPS, H, GC], F32R)
        vt_l = sb("vt_l", [P, GROUPS, H, GC], F32R)
        b_h = [sb(f"b_h{i}", [P, TAPS, PIX], F32R) for i in range(2)]
        b_l = [sb(f"b_l{i}", [P, TAPS, PIX], F32R) for i in range(2)]
        a_h = [sb(f"a_h{i}", [P, TAPS, PIX], F32R) for i in range(2)]
        a_l = [sb(f"a_l{i}", [P, TAPS, PIX], F32R) for i in range(2)]
        a_rep = [sb(f"a_rep{i}", [P, BANK]) for i in range(AREP)]
        prod = [sb(f"prod{i}", [P, BANK]) for i in range(PROD)]
        d_sb = sb("d_sb", [P, BANK])
        with ExitStack() as early:
            x_turned = sb("x_turned", [P, IMAGES, H, W], F32, early)
            start = sb("start", [P, START_COLS], F32, early)
            om_lf = sb("om_lf", [P, GROUPS, OMJ], F32, early)
            om_hf = sb("om_hf", [P, GROUPS, OMJ], F32R, early)
            bias_s = sb("bias_s", [P, 3, GROUPS, OMJ], BF16, early)
            bias_sel = sb("bias_sel", [P, GROUPS, OMJ], BF16, early)
            place_f = sb("place_f", [P, OMJ * P], F32, early)
        ahead = dict(zip(START, columns(START)))
        om_f = start[:, ahead["om_w"]].rearrange("p (g j) -> p g j", g=GROUPS)
        bias_f = start[:, ahead["om_b"]].rearrange("p (g j) -> p g j", g=GROUPS)
        rep_f = start[:, ahead["rep"]].rearrange("p (j c) -> p j c", j=QUART)
        grid_f = start[:, ahead["grid"]]
        mb = [sb(f"mb{q}", [P, TAPS, PIX], F32R) for q in range(QUARTETS)]
        ma = [sb(f"ma{q}", [P, TAPS, PIX], F32R) for q in range(QUARTETS)]

        ps_t = [ctx.enter_context(nc.psum_tensor(f"ps_t{i}", [P, BANK], F32)) for i in range(TRING)]
        ps_a = [ctx.enter_context(nc.psum_tensor(f"ps_a{i}", [P, BANK], F32)) for i in range(2)]
        ps_d = ctx.enter_context(nc.psum_tensor("ps_d", [P, BANK], F32))
        ps_m = [ctx.enter_context(nc.psum_tensor(f"ps_m{i}", [P, BANK], F32)) for i in range(2)]

        x_in = [sem(f"x_in{half}") for half in range(2)]
        keep_in = sem("keep_in")
        start_in = sem("start_in")
        place_in = sem("place_in")
        tokens_in = sem("tokens_in")
        zeroed = sem("zeroed")
        bn_done = sem("bn_done")
        chan_stats = sem("chan_stats")
        pair_sums = sem("pair_sums")
        gn_steps = sem("gn_steps")
        gn_pow = sem("gn_pow")
        xn_ready = sem("xn_ready")
        bias_steps = sem("bias_steps")
        place_done = sem("place_done")
        w_dve = sem("w_dve")
        w_act = sem("w_act")
        taps_done = sem("taps_done")
        xd_high = sem("xd_high")
        xd_ready = sem("xd_ready")
        y_pos = sem("y_pos")
        x_pos = sem("x_pos")
        mask_ps = sem("mask_ps")
        y_abs = sem("y_abs")
        x_abs = sem("x_abs")
        y_hat = sem("y_hat")
        x_hat = sem("x_hat")
        a_full = sem("a_full")
        a_high = sem("a_high")
        b_high = sem("b_high")
        a_low = sem("a_low")
        b_low = sem("b_low")
        mb_filled = [sem(f"mb_filled{q}") for q in range(QUARTETS)]
        ma_filled = [sem(f"ma_filled{q}") for q in range(QUARTETS)]
        xrep_high = sem("xrep_high")
        xrep_ready = sem("xrep_ready")
        v_ps = sem("v_ps")
        v_done = sem("v_done")
        vt_high = sem("vt_high")
        vt_ready = sem("vt_ready")
        t_ready = sem("t_ready")
        a_ready = sem("a_ready")
        a_copied = sem("a_copied")
        weighted = sem("weighted")
        reduced = sem("reduced")
        d_copied = sem("d_copied")
        out_ps = sem("out_ps")
        t_done = sem("t_done")

        xview = d["x"].rearrange("n h w c -> (n h w) c").rearrange("(t p) c -> p t c", p=P)
        inner = lambda n: xpad[:, n, 1:H + 1, 1:W + 1]

        def pair_cols(k):
            return slice(2 * k, min(2 * k + 2, TAPS))

        MADE_AT = [4 * b // 3 for b in range(3 * PAIRS)]
        OUT_AT, V_AT = 20, (22, 28)

        def product(c, par):
            return prod[(CPI * par + c) % PROD]

        def job_at(c):
            return divmod(MADE_AT.index(c), 3) if c in MADE_AT else (None, None)

        block = ctx.enter_context(nc.Block())

        @block.sync
        def _(sp):
            for half in range(2):
                n = slice(half * IMAGES // 2, (half + 1) * IMAGES // 2)
                sp.dma_start(x_turned[:, n, :, :],
                             d["x_turned"].rearrange("c (n y x) -> c n y x", y=H, x=W)[:, n, :, :])\
                  .then_inc(x_in[half], 16)
            sp.dma_start(keep[:, :], d["keep"]).then_inc(keep_in, 16)
            sp.dma_start(start[:, :], d["start"]).then_inc(start_in, 16)
            sp.dma_start(place_f[96:99, :], d["place"]).then_inc(place_in, 16)
            sp.dma_start(t_tok[:, :, :], xview).then_inc(tokens_in, 16)

            def fill(n, par):
                made = count(sp, PAIRS * (n + 1))
                free = [count(sp, CPI * (n - 1) + CPQ * (q + 1)) for q in range(QUARTETS)]
                sp.wait_ge(b_low, made)
                for q in range(QUARTETS):
                    if positive(free[q]):
                        sp.wait_ge(a_ready, free[q])
                    for moving, high, low, filled in ((mb[q], b_h[par], b_l[par], mb_filled[q]),
                                                      (ma[q], a_h[par], a_l[par], ma_filled[q])):
                        for j in range(QUART):
                            g = QUART * q + j
                            for part, src in enumerate((high, low)):
                                r = 32 * j + 16 * part
                                sp.dma_start(moving[r:r + 16, :, :].bitcast(F32),
                                             src[16 * g:16 * g + 16, :, :].bitcast(F32)).then_inc(filled, 16)

            fill(0, 0)
            fill(1, 1)
            with sp.Fori(1, IMAGES // 2) as it:
                for par in range(2):
                    fill(2 * it + par, par)

        @block.tensor
        def _(pe):
            pe.wait_ge(keep_in, 16)
            pe.wait_ge(chan_stats, IMAGES)
            pe.matmul(ps_m[0][:, 0:IMAGES], pair, chan[:, :, 0], start=True, stop=True).then_inc(pair_sums, 1)
            pe.wait_ge(gn_steps, 4)
            pe.matmul(ps_m[0][:, IMAGES:2 * IMAGES], pair, gvar[:, :], start=True, stop=True)\
              .then_inc(pair_sums, 1)

            def positions(k, kind, par, signal):
                for c, tap in enumerate(range(2 * k, min(2 * k + 2, TAPS))):
                    j = (2 * tap + 1, 2 * TAPS + tap, 2 * tap)[kind]
                    out = ps_m[(3 * k + kind) % 2][:, c * PIX:(c + 1) * PIX]
                    pe.matmul(out, om_h[:, j, :, :].rearrange("p g x -> p (g x)"), xd[par][:, :],
                              start=True, stop=False)
                    pe.matmul(out, om_l[:, j, :, :].rearrange("p g x -> p (g x)"), xd[par][:, :],
                              start=False, stop=False)
                    mm = pe.matmul(out, place[0:99, j, :, :].rearrange("p g x -> p (g x)"), grid[0:99, :],
                                   start=False, stop=True)
                mm.then_inc(signal, 1)

            def job(k, kind, n, par):
                if kind == 0:
                    if k == 0:
                        pe.wait_ge(xd_ready, n + 1)
                        if positive(2 * n - 1):
                            pe.wait_ge(v_done, 2 * n - 1)
                    else:
                        pe.wait_ge(a_full, PAIRS * n + k)
                    positions(k, kind, par, y_pos)
                elif kind == 1:
                    if k == 0:
                        if positive(2 * n):
                            pe.wait_ge(v_done, 2 * n)
                    else:
                        pe.wait_ge(x_abs, PAIRS * n + k)
                    positions(k, kind, par, mask_ps)
                else:
                    pe.wait_ge(y_abs, PAIRS * n + k + 1)
                    positions(k, kind, par, x_pos)

            def job_v(half, n):
                if half == 0:
                    pe.wait_ge(x_abs, PAIRS * (n + 1))
                elif isinstance(n, int) and n < 2:
                    pe.wait_ge(a_full, PAIRS * (n + 1))
                else:
                    pe.wait_ge(t_done, n - 1)
                pe.wait_ge(xrep_ready, 2 * n + half + 1)
                for y in range(H // 2):
                    for w, first in ((vp_h, True), (vp_l, False)):
                        mm = pe.matmul(ps_m[half][:, y * C:(y + 1) * C],
                                       xrep[:, y, :, :].rearrange("p r x -> p (r x)"), w[:, :],
                                       start=first, stop=not first)
                mm.then_inc(v_ps, 1)

            def job_out(i, free_sem, free):
                pe.wait_ge(d_copied, i + 1)
                pe.wait_ge(free_sem, free)
                for t in range(TPI):
                    for h in range(2):
                        mm = pe.matmul(ps_m[1][:, t * C:(t + 1) * C],
                                       d_sb[:, h * PIX + t * P:h * PIX + (t + 1) * P], op_w,
                                       start=h == 0, stop=h == 1)
                mm.then_inc(out_ps, 1)

            def segments(c):
                v = c % CPQ
                if v < CPQ - 2:
                    return [(0, v % QUART, 2 * (v // QUART), 2)]
                return [(PIX * s, 2 * (v % 2) + s, TAPS - 1, 1) for s in range(2)]

            def sample_x(c, i):
                q = c // CPQ
                if c % CPQ == 0:
                    pe.wait_ge(mb_filled[q], FILL * (i + 1))
                    pe.wait_ge(vt_ready, QUARTETS * i + q + 1)
                if positive(CPI * i + c - TRING + 1):
                    pe.wait_ge(weighted, CPI * i + c - TRING + 1)
                for col, j, tap, n in segments(c):
                    out = ps_t[c % TRING][:, col:col + n * PIX]
                    for vt, first in ((vt_h, True), (vt_l, False)):
                        mm = pe.matmul(out, vt[:, QUART * q + j, :, :].rearrange("p y c -> p (y c)"),
                                       mb[q][:, tap:tap + n, :].rearrange("p t x -> p (t x)"),
                                       start=first, stop=not first)
                mm.then_inc(t_ready, 1)

            def replicate_a(c, i):
                q = c // CPQ
                if c % CPQ == 0:
                    pe.wait_ge(ma_filled[q], FILL * (i + 1))
                if positive(CPI * i + c - 1):
                    pe.wait_ge(a_copied, CPI * i + c - 1)
                for col, j, tap, n in segments(c):
                    mm = pe.matmul(ps_a[c % 2][:, col:col + n * PIX], rep[:, j, :],
                                   ma[q][:, tap:tap + n, :].rearrange("p t x -> p (t x)"),
                                   start=True, stop=True)
                mm.then_inc(a_ready, 1)

            def reduce_chunks(r, i, par):
                pe.wait_ge(weighted, CPI * i + SUM * (r + 1))
                if r == 0:
                    if positive(i):
                        pe.wait_ge(d_copied, i)
                for c in range(SUM * r, SUM * (r + 1)):
                    for col, j, tap, n in segments(c):
                        mm = pe.matmul(ps_d[32 * j:32 * j + 32, 0:n * PIX],
                                       fold[:, c // CPQ, :], product(c, par)[:, col:col + n * PIX],
                                       start=c < QUART, stop=c >= CPI - 2, skip_group_check=True)
                mm.then_inc(reduced, 1)

            def image(i, par, made):
                n, npar = i + 1, 1 - par
                first_image = isinstance(i, int) and i == 0
                for c in range(CPI):
                    sample_x(c, i)
                    replicate_a(c, i)
                    k, kind = job_at(c)
                    if made and k is not None:
                        job(k, kind, n, npar)
                    if c == OUT_AT and not first_image:
                        if made:
                            job_out(i - 1, a_full, PAIRS * (n + 1))
                        else:
                            job_out(i - 1, v_done, 2 * n)
                    if made and c in V_AT:
                        job_v(V_AT.index(c), n)
                    if c % SUM == SUM - 1 and c > SUM:
                        reduce_chunks(c // SUM - 1, i, par)
                    if c == SUM - 1 and not first_image:
                        reduce_chunks(SPI - 1, i - 1, 1 - par)

            pe.wait_ge(place_done, 2)
            pe.wait_ge(w_dve, 2)
            pe.wait_ge(w_act, 6)
            pe.wait_ge(gn_steps, 5)
            for k in range(PAIRS):
                for kind in range(3):
                    job(k, kind, 0, 0)
            job_v(0, 0)
            job_v(1, 0)
            image(0, 0, True)
            image(1, 1, True)
            with pe.Fori(1, IMAGES // 2 - 1) as it:
                for par in range(2):
                    image(2 * it + par, par, True)
            image(IMAGES - 2, 0, True)
            image(IMAGES - 1, 1, False)
            reduce_chunks(SPI - 1, IMAGES - 1, 1)
            job_out(IMAGES - 1, t_done, IMAGES - 1)

        @block.scalar
        def _(act):
            replicated = lambda t: spread(t[:, :, :].rearrange("p g j -> p j g"), 3, 16)
            act.wait_ge(keep_in, 16)
            act.activation(vp_h[:, :], vp_f, ACT.Copy).then_inc(w_act, 1)
            act.wait_ge(start_in, 16)
            act.activation(om_hf[:, :, :], om_f, ACT.Copy).then_inc(w_act, 1)
            act.activation(om_h[:, :, :, :], replicated(om_f), ACT.Copy).then_inc(w_act, 1)
            act.activation(grid[:, :], grid_f, ACT.Copy).then_inc(w_act, 1)
            act.wait_ge(w_dve, 1)
            act.activation(om_l[:, :, :, :], replicated(om_lf), ACT.Copy).then_inc(w_act, 1)

            def normalise(n):
                act.wait_ge(x_in[n // (IMAGES // 2)], 16)
                act.wait_ge(zeroed, 4)
                act.activation(inner(n), x_turned[:, n, :, :], ACT.Identity, bias=gshift[:, n:n + 1],
                               scale=grstd[:, n:n + 1]).then_inc(xn_ready, 1)

            act.wait_ge(gn_steps, 6)
            normalise(0)
            act.wait_ge(place_in, 16)
            act.activation(place[96:99, :, :, :].rearrange("p j g x -> p (j g x)"), place_f[96:99, :],
                           ACT.Copy).then_inc(place_done, 1)
            act.activation(rep[:, :, :], rep_f, ACT.Copy).then_inc(w_act, 1)

            def xd_split(n, par):
                act.wait_ge(taps_done, TAPS * (n + 1))
                if positive(PAIRS * (n - 1)):
                    act.wait_ge(mask_ps, PAIRS * (n - 1))
                if positive(PAIRS * (n - 1)):
                    act.wait_ge(x_pos, PAIRS * (n - 1))
                act.activation(xd[par][:, :], conv[:, :, :].rearrange("p y x -> p (y x)"), ACT.Copy)\
                   .then_inc(xd_high, 1)

            def x_rep(half, n, quarters=(0, 1)):
                if positive(2 * n + half):
                    act.wait_ge(v_ps, 2 * n + half)
                for s in quarters:
                    y = 1 + 8 * half + 4 * s
                    act.activation(xrep[:, 4 * s:4 * s + 4, :, :],
                                   spread(xpad[:, n, y:y + 4, 1:W + 1], 2, 8), ACT.Copy).then_inc(xrep_high, 1)

            def abs_y(k, n, par):
                if k == 0:
                    for q in range(QUARTETS):
                        if positive(FILL * (n - 1)):
                            act.wait_ge(ma_filled[q], FILL * (n - 1))
                act.wait_ge(y_pos, PAIRS * n + k + 1)
                w = min(2, TAPS - 2 * k) * PIX
                act.activation(a_l[par][:, pair_cols(k), :].bitcast(F32).rearrange("p t x -> p (t x)"),
                               ps_m[3 * k % 2][:, 0:w], ACT.Abs).then_inc(y_abs, 1)

            def abs_x(k, n, par):
                if k == 0:
                    for q in range(QUARTETS):
                        if positive(FILL * (n - 1)):
                            act.wait_ge(mb_filled[q], FILL * (n - 1))
                act.wait_ge(x_pos, PAIRS * n + k + 1)
                w = min(2, TAPS - 2 * k) * PIX
                act.activation(b_l[par][:, pair_cols(k), :].bitcast(F32).rearrange("p t x -> p (t x)"),
                               ps_m[3 * k % 2][:, 0:w], ACT.Abs).then_inc(x_abs, 1)

            def high_part_a(k, n, par):
                act.wait_ge(a_full, PAIRS * n + k + 1)
                act.activation(a_h[par][:, pair_cols(k), :], a_l[par][:, pair_cols(k), :].bitcast(F32), ACT.Copy)\
                   .then_inc(a_high, 1)

            def high_part_b(k, n, par):
                act.wait_ge(x_hat, PAIRS * n + k + 1)
                act.activation(b_h[par][:, pair_cols(k), :], b_l[par][:, pair_cols(k), :].bitcast(F32), ACT.Copy)\
                   .then_inc(b_high, 1)

            def vt_split(q, n):
                act.wait_ge(v_done, 2 * n + 2)
                if positive(CPI * (n - 1) + CPQ * (q + 1)):
                    act.wait_ge(t_ready, CPI * (n - 1) + CPQ * (q + 1))
                if positive(QUARTETS * (n - 1) + q + 1):
                    act.wait_ge(vt_ready, QUARTETS * (n - 1) + q + 1)
                for j in range(QUART):
                    r = slice(32 * j, 32 * j + 32)
                    mm = act.activation(vt_h[r, QUART * q + j, :, :], v_sb[r, :, q, :], ACT.Copy)
                mm.then_inc(vt_high, 1)

            def copy_a(c, i):
                act.wait_ge(a_ready, CPI * i + c + 1)
                if positive(CPI * i + c - AREP + 1):
                    act.wait_ge(weighted, CPI * i + c - AREP + 1)
                act.activation(a_rep[c % AREP][:, :], ps_a[c % 2][:, :], ACT.Copy).then_inc(a_copied, 1)

            def copy_d(i):
                act.wait_ge(reduced, SPI * (i + 1))
                if positive(i):
                    act.wait_ge(out_ps, i)
                act.activation(d_sb[:, :], ps_d[:, :], ACT.Copy).then_inc(d_copied, 1)

            def image(i, par, made, ahead):
                n, npar = i + 1, 1 - par
                for c in range(CPI):
                    copy_a(c, i)
                    k, kind = job_at(c)
                    if made and kind == 0:
                        abs_y(k, n, npar)
                    if made and kind == 2:
                        abs_x(k, n, npar)
                    if made and c % 4 == 3 and c < 4 * PAIRS:
                        high_part_a(c // 4, n, npar)
                    if made and c % 4 == 1 and 1 < c <= 4 * PAIRS + 1:
                        high_part_b(c // 4 - 1, n, npar)
                    if c == 1:
                        vt_split(1, i)
                    if c == 5 and not (isinstance(i, int) and i == 0):
                        copy_d(i - 1)
                    for half, quarter, at in ((0, 0, 16), (0, 1, 17), (1, 0, 23), (1, 1, 24)):
                        if made and c == at:
                            x_rep(half, n, (quarter,))
                    if made and c == 30:
                        vt_split(0, n)
                    if ahead and c == 35:
                        xd_split(i + 2, par)

            xd_split(0, 0)
            x_rep(0, 0)
            abs_y(0, 0, 0)
            for k in range(PAIRS):
                abs_x(k, 0, 0)
                if k + 1 < PAIRS:
                    abs_y(k + 1, 0, 0)
                high_part_a(k, 0, 0)
                high_part_b(k, 0, 0)
                for n in range(2 * k + 1, min(2 * k + 3, IMAGES)):
                    normalise(n)
            x_rep(1, 0)
            vt_split(0, 0)
            xd_split(1, 1)
            image(0, 0, True, True)
            image(1, 1, True, True)
            with act.Fori(1, IMAGES // 2 - 1) as it:
                for par in range(2):
                    image(2 * it + par, par, True, True)
            image(IMAGES - 2, 0, True, False)
            image(IMAGES - 1, 1, False, False)
            copy_d(IMAGES - 1)

        @block.vector
        def _(dve):
            for n in range(IMAGES):
                dve.wait_ge(x_in[n // (IMAGES // 2)], 16)
                dve.bn_stats(stats[:, n, :], x_turned[:, n, :, :].rearrange("p y x -> p (y x)"))\
                   .then_inc(bn_done, 1)
            for n in range(IMAGES):
                dve.wait_ge(bn_done, n + 1)
                dve.bn_aggr(chan[:, n, :], stats[:, n, :]).then_inc(chan_stats, 1)
            dve.wait_ge(pair_sums, 1)
            dve.tensor_copy(gmean[:, :], ps_m[0][:, 0:IMAGES]).then_inc(gn_steps, 1)
            dve.wait_ge(gn_steps, 1)
            dve.wait_ge(chan_stats, IMAGES)
            dve.tensor_tensor(gdev[:, :], chan[:, :, 0], gmean[:, :], ALU.subtract).then_inc(gn_steps, 1)
            dve.wait_ge(gn_steps, 2)
            dve.tensor_tensor(gsq[:, :], gdev[:, :], gdev[:, :], ALU.mult).then_inc(gn_steps, 1)
            dve.wait_ge(gn_steps, 3)
            dve.tensor_tensor(gvar[:, :], gsq[:, :], chan[:, :, 1], ALU.add).then_inc(gn_steps, 1)
            dve.wait_ge(pair_sums, 2)
            dve.tensor_scalar(gvar_eps[:, :], ps_m[0][:, IMAGES:2 * IMAGES], GN_EPS, None, ALU.add).then_inc(gn_steps, 1)
            dve.wait_ge(w_act, 2)
            dve.tensor_tensor(om_lf[:, :, :], om_f, om_hf[:, :, :].bitcast(F32), ALU.subtract).then_inc(w_dve, 1)
            dve.tensor_tensor(vp_l[:, :], vp_f, vp_h[:, :].bitcast(F32), ALU.subtract).then_inc(w_dve, 1)
            dve.wait_ge(start_in, 16)
            dve.tensor_copy(bias_s[:, 0, :, :], bias_f).then_inc(bias_steps, 1)
            for part in range(2):
                dve.wait_ge(bias_steps, 2 * part + 1)
                dve.tensor_tensor(bias_f, bias_f, bias_s[:, part, :, :], ALU.subtract)\
                   .then_inc(bias_steps, 1)
                dve.wait_ge(bias_steps, 2 * part + 2)
                dve.tensor_copy(bias_s[:, part + 1, :, :], bias_f).then_inc(bias_steps, 1)
            dve.wait_ge(bias_steps, 5)
            for part in range(3):
                r = slice(32 * part, 32 * part + 32)
                dve.tensor_copy(bias_sel[r, :, :], bias_s[r, part, :, :]).then_inc(bias_steps, 1)
            dve.wait_ge(gn_pow, 1)
            dve.scalar_tensor_tensor(out=gshift[:, :], in0=gmean[:, :], scalar=-1.0, in1=grstd[:, :],
                                     op0=ALU.mult, op1=ALU.mult).then_inc(gn_steps, 1)
            dve.wait_ge(bias_steps, 8)
            dve.tensor_copy(place[0:96, :, :, :],
                            spread(bias_sel[0:96, :, :].rearrange("p g j -> p j g"), 3, 16))\
               .then_inc(place_done, 1)

            def tap_step(tap, n):
                if tap == 0:
                    dve.wait_ge(xn_ready, n + 1)
                    if positive(n):
                        dve.wait_ge(xd_high, n)
                    if positive(n):
                        dve.wait_ge(xd_ready, n)
                if positive(TAPS * n + tap):
                    dve.wait_ge(taps_done, TAPS * n + tap)
                src = xpad[:, n, tap // 3:tap // 3 + H, tap % 3:tap % 3 + W]
                if tap == 0:
                    dve.tensor_scalar(conv[:, :, :], src, dw[:, 0:1], dw_bias[:, 0:1],
                                      ALU.mult, ALU.add).then_inc(taps_done, 1)
                else:
                    dve.scalar_tensor_tensor(out=conv[:, :, :], in0=src, scalar=dw[:, tap:tap + 1],
                                             in1=conv[:, :, :], op0=ALU.mult, op1=ALU.add)\
                       .then_inc(taps_done, 1)

            def hat_y(k, n, par):
                dve.wait_ge(y_abs, PAIRS * n + k + 1)
                v = a_l[par][:, pair_cols(k), :].bitcast(F32)
                dve.tensor_scalar(v, v, 1.0, 1.0, ALU.min, ALU.subtract).then_inc(y_hat, 1)

            def masked(k, n, par):
                dve.wait_ge(y_hat, PAIRS * n + k + 1)
                dve.wait_ge(mask_ps, PAIRS * n + k + 1)
                w = min(2, TAPS - 2 * k) * PIX
                v = a_l[par][:, pair_cols(k), :].bitcast(F32).rearrange("p t x -> p (t x)")
                dve.tensor_tensor(v, ps_m[(3 * k + 1) % 2][:, 0:w], v, ALU.mult).then_inc(a_full, 1)

            def hat_x(k, n, par):
                dve.wait_ge(x_abs, PAIRS * n + k + 1)
                v = b_l[par][:, pair_cols(k), :].bitcast(F32)
                dve.tensor_scalar(v, v, 1.0, 1.0, ALU.min, ALU.subtract).then_inc(x_hat, 1)

            def x_rep_low(half, n):
                dve.wait_ge(xrep_high, 4 * n + 2 * half + 2)
                dve.tensor_tensor(xrep[64:P, :, :, :],
                                  spread(xpad[64:P, n, 1 + 8 * half:9 + 8 * half, 1:W + 1], 2, 8),
                                  xrep[64:P, :, :, :].bitcast(F32), ALU.subtract).then_inc(xrep_ready, 1)

            def v_out(half, n):
                dve.wait_ge(v_ps, 2 * n + half + 1)
                if positive(QUARTETS * n):
                    dve.wait_ge(vt_ready, QUARTETS * n)
                v = ps_m[half][:, :].rearrange("p (y q j c) -> p y q j c", y=8, q=QUARTETS, j=QUART)
                for j in range(QUART):
                    r = slice(32 * j, 32 * j + 32)
                    op = dve.tensor_tensor(v_sb[r, 8 * half:8 * half + 8, :, :], v[r, :, :, j, :],
                                           spread(vp_bias[r, :, :], 1, 8), ALU.add)
                op.then_inc(v_done, 1)

            def weight(c, i, par):
                dve.wait_ge(t_ready, CPI * i + c + 1)
                dve.wait_ge(a_copied, CPI * i + c + 1)
                if positive(SPI * i + (c - PROD) // SUM + 1):
                    dve.wait_ge(reduced, SPI * i + (c - PROD) // SUM + 1)
                dve.tensor_tensor(product(c, par)[:, :], ps_t[c % TRING][:, :], a_rep[c % AREP][:, :], ALU.mult)\
                   .then_inc(weighted, 1)

            def residual(i):
                dve.wait_ge(out_ps, i + 1)
                t = t_tok[:, bass.ds(TPI * i, TPI), :].rearrange("p t c -> p (t c)")
                dve.tensor_tensor(t, ps_m[1][:, 0:TPI * C], t, ALU.add).then_inc(t_done, 1)

            def image(i, par, made, ahead):
                n, npar = i + 1, 1 - par
                for c in range(CPI):
                    weight(c, i, par)
                    if made and c < 4 * PAIRS and c % 4 == 1:
                        hat_y(c // 4, n, npar)
                    if made and c < 4 * PAIRS and c % 4 == 2:
                        masked(c // 4, n, npar)
                    if made and c < 4 * PAIRS and c % 4 == 3:
                        hat_x(c // 4, n, npar)
                    if c == OUT_AT + 1 and not (isinstance(i, int) and i == 0):
                        residual(i - 1)
                    if made and c - 1 in V_AT:
                        v_out(V_AT.index(c - 1), n)
                    if ahead and c % 2 == 0 and 14 <= c < 14 + 2 * TAPS:
                        tap_step((c - 14) // 2, i + 2)

            dve.wait_ge(tokens_in, 16)
            for tap in range(TAPS):
                tap_step(tap, 0)
            x_rep_low(0, 0)
            for k in range(PAIRS):
                hat_y(k, 0, 0)
                masked(k, 0, 0)
                hat_x(k, 0, 0)
            for tap in range(TAPS):
                tap_step(tap, 1)
            v_out(0, 0)
            x_rep_low(1, 0)
            v_out(1, 0)
            image(0, 0, True, True)
            image(1, 1, True, True)
            with dve.Fori(1, IMAGES // 2 - 1) as it:
                for par in range(2):
                    image(2 * it + par, par, True, True)
            image(IMAGES - 2, 0, True, False)
            image(IMAGES - 1, 1, False, False)
            residual(IMAGES - 1)

        @block.gpsimd
        def _(pool):
            pool.memset(minus_half[:, :], -0.5).then_inc(zeroed, 1)
            pool.memset(xpad[:, :, :, :], 0.0).then_inc(zeroed, 1)
            pool.memset(vt_h[:, :, :, :].bitcast(F32), 0.0).then_inc(zeroed, 1)
            pool.memset(vt_l[:, :, :, :].bitcast(F32), 0.0).then_inc(zeroed, 1)
            pool.wait_ge(zeroed, 4)
            pool.wait_ge(gn_steps, 5)
            pool.tensor_tensor(grstd[:, :], gvar_eps[:, :], minus_half[:, :], ALU.pow).then_inc(gn_pow, 1)

            def xd_low(n, par):
                if isinstance(n, int) and n < 2:
                    if positive(n):
                        pool.wait_ge(vt_ready, n)
                else:
                    pool.wait_ge(vt_ready, QUARTETS * (n - 1) + 1)
                pool.wait_ge(xd_high, n + 1)
                pool.tensor_tensor(xd[par][64:P, :], conv[64:P, :, :].rearrange("p y x -> p (y x)"),
                                   xd[par][64:P, :].bitcast(F32), ALU.subtract).then_inc(xd_ready, 1)

            def low_parts(k, n, par):
                if k == 0:
                    if isinstance(n, int) and n == 0:
                        pool.wait_ge(xd_ready, 1)
                    else:
                        pool.wait_ge(vt_ready, QUARTETS * n)
                if k == PAIRS - 1:
                    pool.wait_ge(xrep_ready, 2 * n + 1)
                for full, high, high_done, low_done in ((a_l, a_h, a_high, a_low), (b_l, b_h, b_high, b_low)):
                    pool.wait_ge(high_done, PAIRS * n + k + 1)
                    pool.tensor_tensor(full[par][:, pair_cols(k), :], full[par][:, pair_cols(k), :].bitcast(F32),
                                       high[par][:, pair_cols(k), :].bitcast(F32), ALU.subtract).then_inc(low_done, 1)

            def x_rep_low(half, n):
                pool.wait_ge(b_low, PAIRS * (n + 1) - (1 - half))
                pool.wait_ge(xrep_high, 4 * n + 2 * half + 2)
                pool.tensor_tensor(xrep[64:P, :, :, :],
                                   spread(xpad[64:P, n, 1 + 8 * half:9 + 8 * half, 1:W + 1], 2, 8),
                                   xrep[64:P, :, :, :].bitcast(F32), ALU.subtract).then_inc(xrep_ready, 1)

            def vt_low(q, n):
                if q:
                    pool.wait_ge(xd_ready, n + 2 if not isinstance(n, int) else min(n + 2, IMAGES))
                    pool.wait_ge(vt_ready, QUARTETS * n + 1)
                else:
                    pool.wait_ge(b_low, PAIRS * (n + 1))
                    pool.wait_ge(xrep_ready, 2 * n + 2)
                pool.wait_ge(vt_high, QUARTETS * n + q + 1)
                for j in range(QUART):
                    r = slice(32 * j, 32 * j + 32)
                    g = QUART * q + j
                    op = pool.tensor_tensor(vt_l[r, g, :, :], v_sb[r, :, q, :], vt_h[r, g, :, :].bitcast(F32),
                                            ALU.subtract)
                op.then_inc(vt_ready, 1)

            def image(i, par, made, ahead):
                n, npar = i + 1, 1 - par
                vt_low(1, i)
                if made:
                    for k in range(PAIRS):
                        if k == PAIRS - 1:
                            x_rep_low(0, n)
                        low_parts(k, n, npar)
                if made:
                    x_rep_low(1, n)
                    vt_low(0, n)
                if ahead:
                    xd_low(i + 2, par)

            xd_low(0, 0)
            for k in range(PAIRS):
                low_parts(k, 0, 0)
            vt_low(0, 0)
            xd_low(1, 1)
            image(0, 0, True, True)
            image(1, 1, True, True)
            with pool.Fori(1, IMAGES // 2 - 1) as it:
                for par in range(2):
                    image(2 * it + par, par, True, True)
            image(IMAGES - 2, 0, True, False)
            image(IMAGES - 1, 1, False, False)


ATTENTION = {"q_w": P, "k_w": P, "v_w": C, "gate_w": EXPERTS, "ident": P, "q_bias": 1, "k_bias": 1,
             "v_bias": C, "gate_bias": EXPERTS}
ATTENTION_COLS = sum(ATTENTION.values())


def token_stage(nc, d, out, t_tok):
    SLOTS = 8
    CHUNK = BANK // P
    CHUNKS = TT // CHUNK
    UNITS = EXPERTS * CHUNKS
    FIRST = 4
    ROUNDS = FIRST + UNITS // SLOTS
    PIECE = EXPERTS // 4

    with ExitStack() as ctx:
        def sb(name, shape, dt=F32):
            return ctx.enter_context(nc.sbuf_tensor(name, shape, dt))

        def ps(name):
            return ctx.enter_context(nc.psum_tensor(name, [P, BANK], F32))

        def sem(name):
            return ctx.enter_context(nc.semaphore(name))

        two = range(2)
        pack = sb("attention_pack", [P, ATTENTION_COLS])
        at = {n: pack[:, cols] for n, cols in zip(ATTENTION, columns(ATTENTION))}
        ident, q_bias, k_bias = at["ident"], at["q_bias"], at["k_bias"]
        SPLIT = ("q_w", "k_w", "v_w", "gate_w")
        split_cols = sum(ATTENTION[n] for n in SPLIT)
        pack_h = sb("attention_high", [P, split_cols], F32R)
        pack_l = sb("attention_low", [P, split_cols], F32R)
        wh = {n: pack_h[:, cols] for n, cols in zip(SPLIT, columns(ATTENTION))}
        wl = {n: pack_l[:, cols] for n, cols in zip(SPLIT, columns(ATTENTION))}
        minus_half = sb("minus_half2", [P, TPI])
        stats = [sb(f"ln_stats{s}", [P, TPI, 6]) for s in two]
        moments = [sb(f"ln_moments{s}", [P, TPI, 2]) for s in two]
        var_eps = [sb(f"ln_var{s}", [P, TPI]) for s in two]
        rstd = [sb(f"ln_rstd{s}", [P, TPI]) for s in two]
        normed = [sb(f"ln_out{s}", [P, TPI, 2, C]) for s in two]
        xs = [sb(f"xs{s}", [P, PIX], F32R) for s in two]
        q_s = sb("q_s", [P, PIX], F32R)
        k_h = sb("k_h", [P, PIX], F32R)
        k_l = sb("k_l", [P, PIX], F32R)
        v_sb = sb("v_tok", [P, TPI, C])
        top = sb("score_max", [P, TPI])
        ntop = sb("score_nmax", [P, TPI])
        prob = sb("prob", [P, TPI, PIX])
        psum_row = sb("prob_sum", [P, TPI])
        rsum = sb("prob_rsum", [P, TPI])
        prob_t = sb("prob_t", [P, TPI, PIX])
        logit = sb("logit", [P, TPI, EXPERTS])
        ltop = sb("logit_max", [P, TPI])
        nltop = sb("logit_nmax", [P, TPI])
        gexp = sb("gexp", [P, TPI, EXPERTS + 6])
        grest = sb("grest", [P, TPI, EXPERTS + 6])
        top8 = sb("top8", [P, TPI, 8])
        top2 = sb("top2", [P, TPI, 8])
        gsel = sb("gsel", [P, TPI, EXPERTS])
        tsum = sb("tsum", [P, TPI])
        trec = sb("trec", [P, TPI])
        xf = sb("xf", [P, IMAGES * PIX], F32R)
        dispatch = sb("dispatch", [P, TT, EXPERTS])
        w_f = [sb(f"w{k}_f", [P, EXPERTS, HIDDEN]) for k in (1, 2)]
        w_h = [sb(f"w{k}_h", [P, EXPERTS, HIDDEN], F32R) for k in (1, 2)]
        w_l = [sb(f"w{k}_l", [P, EXPERTS, HIDDEN], F32R) for k in (1, 2)]
        w3 = sb("w3", [P, EXPERTS, C])
        gated = [sb(f"gated{b}", [P, BANK]) for b in two]
        hidden = [sb(f"hidden{b}", [P, BANK]) for b in two]
        share = [sb(f"share{b}", [P, CHUNK, C]) for b in two]

        ps_xv = ps("ps_xv")
        ps_x = [ps_xv[:, 0:PIX], None]
        ps_v = ps_xv[:, PIX:PIX + TPI * C].rearrange("p (t c) -> p t c", t=TPI)
        ps_qk = ps("ps_qk")[:, :].rearrange("p (w x) -> p w x", w=2)
        ps_s = ps("ps_s")[:, :].rearrange("p (t x) -> p t x", t=TPI)
        ps_p = ps_s
        ps_oxg = ps("ps_oxg")
        ps_x[1] = ps_oxg[:, 0:PIX]
        ps_o = ps_oxg[:, PIX:PIX + TPI * C].rearrange("p (t c) -> p t c", t=TPI)
        ps_logit = ps_oxg[:, PIX + TPI * C:PIX + TPI * (C + EXPERTS)]
        ps_h1 = ps("ps_h1")
        ps_h2 = [ps(f"ps_h2{b}") for b in two]
        ps_y = ps("ps_y")[:, 0:CHUNK * C].rearrange("p (t c) -> p t c", t=CHUNK)

        pack_in = sem("pack_in")
        w1_in = sem("w1_in")
        w2_in = sem("w2_in")
        w3_in = sem("w3_in")
        cleared = sem("cleared2")
        w_high = sem("w_high")
        w_low = sem("w_low")
        piece_high = sem("piece_high")
        piece_low = sem("piece_low")
        ln_stat = [sem(f"ln_stat{s}") for s in two]
        ln_pow = [sem(f"ln_pow{s}") for s in two]
        ln_done = [sem(f"ln_done{s}") for s in two]
        x_ps = [sem(f"x_ps{s}") for s in two]
        x_high = [sem(f"x_high{s}") for s in two]
        x_low = [sem(f"x_low{s}") for s in two]
        qk_ps = sem("qk_ps")
        v_ps = sem("v_ps2")
        q_high = sem("q_high")
        k_high = sem("k_high")
        q_low = sem("q_low")
        k_low = sem("k_low")
        v_done = sem("v_done2")
        s_ps = sem("s_ps")
        max_step = sem("max_step")
        exp_done = sem("exp_done")
        p_ps = sem("p_ps")
        p_done = sem("p_done")
        rsum_done = sem("rsum_done")
        o_ps = sem("o_ps")
        res_done = sem("res_done")
        xf_done = sem("xf_done")
        g_ps = sem("g_ps")
        g_step = sem("g_step")
        g_exp = sem("g_exp")
        d_step = sem("d_step")
        h1_ps = sem("h1_ps")
        h2_ps = sem("h2_ps")
        silu_done = sem("silu_done")
        hidden_done = sem("hidden_done")
        y_ps = sem("y_ps")
        weighed = sem("weighed")
        added = sem("added")
        stored = sem("stored")
        TOP_STEPS = 9

        out_view = out.rearrange("n h w c -> (n h w) c").rearrange("(t p) c -> p t c", p=P)

        def unit_at(r, slot):
            u = SLOTS * (r - FIRST) + slot
            return u if 0 <= u < UNITS else None

        def stages(r):
            return [n if 0 <= n < IMAGES else None for n in (r, r - 1, r - 2)]

        def piece_at(r, slot):
            places = [(a, b) for a in (1, 2) for b in (2, 3, 6, 7)]
            return places.index((r, slot)) if (r, slot) in places else None

        block = ctx.enter_context(nc.Block())

        @block.sync
        def _(sp):
            sp.dma_start(pack[:, :], d["attention"]).then_inc(pack_in, 16)
            for w, name, arrived in ((w_f[0], "w1", w1_in), (w_f[1], "w2", w2_in), (w3, "w3", w3_in)):
                sp.dma_start(w[:, :, :], d[name].rearrange("p (e h) -> p e h", e=EXPERTS)).then_inc(arrived, 16)
            for c in range(CHUNKS):
                sp.wait_ge(added, EXPERTS * (c + 1))
                sp.dma_start(out_view[:, CHUNK * c:CHUNK * (c + 1), :],
                             t_tok[:, CHUNK * c:CHUNK * (c + 1), :]).then_inc(stored, 16)
            sp.wait_ge(stored, 16 * CHUNKS)

        @block.vector
        def _(dve):
            def ln_stats(s, i):
                if s:
                    dve.wait_ge(res_done, TPI * (i + 1))
                for t in range(TPI):
                    dve.bn_stats(stats[s][:, t, :], t_tok[:, TPI * i + t, :]).then_inc(ln_stat[s], 1)
                dve.wait_ge(ln_stat[s], 5 * i + 2)
                for t in range(TPI):
                    dve.bn_aggr(moments[s][:, t, :], stats[s][:, t, :]).then_inc(ln_stat[s], 1)
                dve.wait_ge(ln_stat[s], 5 * i + 4)
                dve.tensor_scalar(var_eps[s][:, :], moments[s][:, :, 1], LN_EPS, None, ALU.add)\
                   .then_inc(ln_stat[s], 1)

            def ln_apply(s, i):
                dve.wait_ge(ln_pow[s], i + 1)
                if positive(i):
                    dve.wait_ge(x_ps[s], i)
                for t in range(TPI):
                    op = dve.tensor_scalar(normed[s][:, t, :, :], spread(t_tok[:, TPI * i + t, :], 1, 2),
                                           moments[s][:, t, 0:1], rstd[s][:, t:t + 1],
                                           ALU.subtract, ALU.mult)
                op.then_inc(ln_done[s], 1)

            def x_split(s, i):
                dve.wait_ge(x_high[s], i + 1)
                dve.tensor_tensor(xs[s][64:P, :], ps_x[s][64:P, :], xs[s][64:P, :].bitcast(F32), ALU.subtract)\
                   .then_inc(x_low[s], 1)

            def qkv_low(i):
                dve.wait_ge(k_high, i + 1)
                dve.scalar_tensor_tensor(out=q_s[64:P, :], in0=ps_qk[64:P, 0, :], scalar=q_bias[64:P, :],
                                         in1=q_s[64:P, :].bitcast(F32), op0=ALU.add, op1=ALU.subtract)\
                   .then_inc(q_low, 1)
                dve.scalar_tensor_tensor(out=k_l[:, :], in0=ps_qk[:, 1, :], scalar=k_bias,
                                         in1=k_h[:, :].bitcast(F32), op0=ALU.add, op1=ALU.subtract)\
                   .then_inc(k_low, 1)
                dve.wait_ge(v_ps, i + 1)
                if positive(i):
                    dve.wait_ge(o_ps, i)
                dve.tensor_tensor(v_sb[:, :, :], ps_v, spread(at["v_bias"], 1, TPI), ALU.add).then_inc(v_done, 1)

            def score_max(i):
                dve.wait_ge(s_ps, i + 1)
                if positive(TPI * i):
                    dve.wait_ge(exp_done, TPI * i)
                dve.tensor_reduce(top[:, :], ps_s, AX_X, ALU.max).then_inc(max_step, 1)
                dve.wait_ge(max_step, 2 * i + 1)
                dve.tensor_scalar(ntop[:, :], top[:, :], -SCALE, None, ALU.mult).then_inc(max_step, 1)

            def add_values(i):
                dve.wait_ge(exp_done, TPI * (i + 1))
                dve.reciprocal(rsum[:, :], psum_row[:, :]).then_inc(rsum_done, 1)
                dve.wait_ge(rsum_done, i + 1)
                dve.wait_ge(o_ps, i + 1)
                for t in range(TPI):
                    tok = t_tok[:, TPI * i + t, :]
                    dve.scalar_tensor_tensor(out=tok, in0=ps_o[:, t, :], scalar=rsum[:, t:t + 1], in1=tok,
                                             op0=ALU.mult, op1=ALU.add).then_inc(res_done, 1)

            def gate_logits(i):
                dve.wait_ge(g_ps, i + 1)
                dve.tensor_tensor(logit[:, :, :], ps_logit.rearrange("p (t e) -> p t e", t=TPI),
                                  spread(at["gate_bias"], 1, TPI), ALU.add).then_inc(g_step, 1)
                dve.wait_ge(g_step, 3 * i + 1)
                dve.tensor_reduce(ltop[:, :], logit[:, :, :], AX_X, ALU.max).then_inc(g_step, 1)
                dve.wait_ge(g_step, 3 * i + 2)
                dve.tensor_scalar(nltop[:, :], ltop[:, :], -1.0, None, ALU.mult).then_inc(g_step, 1)

            def top_two(i):
                dve.wait_ge(g_exp, TPI * (i + 1))
                base = TOP_STEPS * i
                for t in range(TPI):
                    dve.max(top8[:, t, :], gexp[:, t, 0:EXPERTS]).then_inc(d_step, 1)
                dve.wait_ge(d_step, base + 2)
                dve.tensor_copy(top2[:, :, 0:2], top8[:, :, 0:2]).then_inc(d_step, 1)
                dve.tensor_tensor(tsum[:, :], top8[:, :, 0], top8[:, :, 1], ALU.add).then_inc(d_step, 1)
                dve.wait_ge(d_step, base + 4)
                for t in range(TPI):
                    dve.match_replace(grest[:, t, :], top2[:, t, :], gexp[:, t, :], 0.0).then_inc(d_step, 1)
                dve.reciprocal(trec[:, :], tsum[:, :]).then_inc(d_step, 1)
                dve.wait_ge(d_step, base + 7)
                dve.tensor_tensor(gsel[:, :, :], gexp[:, :, 0:EXPERTS], grest[:, :, 0:EXPERTS], ALU.subtract)\
                   .then_inc(d_step, 1)
                dve.wait_ge(d_step, base + 8)
                dve.tensor_tensor(dispatch[:, TPI * i:TPI * (i + 1), :], gsel[:, :, :],
                                  spread(trec[:, :], 2, EXPERTS), ALU.mult).then_inc(d_step, 1)

            def hide(u):
                dve.wait_ge(silu_done, u + 1)
                dve.wait_ge(h2_ps, u + 1)
                if positive(u - 1):
                    dve.wait_ge(y_ps, u - 1)
                dve.tensor_tensor(hidden[u % 2][:, :], ps_h2[u % 2][:, :], gated[u % 2][:, :], ALU.mult)\
                   .then_inc(hidden_done, 1)

            def weigh(u):
                c, e = u // EXPERTS, u % EXPERTS
                if e == 0:
                    dve.wait_ge(d_step, TOP_STEPS * IMAGES // CHUNKS * (c + 1))
                dve.wait_ge(y_ps, u + 1)
                if positive(u - 1):
                    dve.wait_ge(added, u - 1)
                dve.tensor_tensor(share[u % 2][:, :, :], ps_y,
                                  spread(dispatch[:, CHUNK * c:CHUNK * (c + 1), e], 2, C), ALU.mult)\
                   .then_inc(weighed, 1)

            dve.wait_ge(pack_in, 16)
            dve.wait_ge(w_high, 1)
            dve.tensor_tensor(pack_l[:, :], pack[:, 0:split_cols], pack_h[:, :].bitcast(F32), ALU.subtract)\
               .then_inc(w_low, 1)
            dve.wait_ge(cleared, 4)
            for r in range(ROUNDS):
                project, attend, gate = stages(r)
                for slot in range(SLOTS):
                    u = unit_at(r, slot)
                    if u is not None:
                        if u >= 2:
                            weigh(u - 2)
                        hide(u)
                    if slot == 0 and gate is not None:
                        x_split(1, gate)
                    if slot == 0 and project is not None:
                        ln_stats(0, project)
                    if slot == 1 and attend is not None:
                        score_max(attend)
                    if slot == 1 and gate is not None:
                        gate_logits(gate)
                    if slot == 2 and project is not None:
                        ln_apply(0, project)
                    if slot == 4 and project is not None:
                        x_split(0, project)
                    if slot == 4 and gate is not None:
                        top_two(gate)
                    if slot == 5 and attend is not None:
                        add_values(attend)
                        ln_stats(1, attend)
                    if slot == 6 and project is not None:
                        qkv_low(project)
                    if slot == 7 and attend is not None:
                        ln_apply(1, attend)
            weigh(UNITS - 2)
            weigh(UNITS - 1)

        @block.gpsimd
        def _(pool):
            pool.memset(minus_half[:, :], -0.5).then_inc(cleared, 1)
            pool.memset(gexp[:, :, EXPERTS:EXPERTS + 6], -1.0).then_inc(cleared, 1)
            pool.memset(top2[:, :, :], -1.0).then_inc(cleared, 1)
            pool.memset(grest[:, :, :], 0.0).then_inc(cleared, 1)
            pool.wait_ge(cleared, 4)

            def power(s, i):
                pool.wait_ge(ln_stat[s], 5 * (i + 1))
                if positive(i):
                    pool.wait_ge(ln_done[s], i)
                pool.tensor_tensor(rstd[s][:, :], var_eps[s][:, :], minus_half[:, :], ALU.pow)\
                    .then_inc(ln_pow[s], 1)

            def keep_x(i):
                pool.wait_ge(x_low[1], i + 1)
                pool.tensor_copy(xf[:, PIX * i:PIX * (i + 1)], xs[1][:, :].bitcast(F32)).then_inc(xf_done, 1)

            def add(u):
                c = u // EXPERTS
                tokens = t_tok[:, CHUNK * c:CHUNK * (c + 1), :]
                pool.wait_ge(weighed, u + 1)
                if positive(u):
                    pool.wait_ge(added, u)
                pool.tensor_tensor(tokens, tokens, share[u % 2][:, :, :], ALU.add).then_inc(added, 1)

            def low_piece(k):
                w, e = k // 4, PIECE * (k % 4)
                pool.wait_ge(piece_high, k + 1)
                pool.tensor_tensor(w_l[w][:, e:e + PIECE, :], w_f[w][:, e:e + PIECE, :],
                                   w_h[w][:, e:e + PIECE, :].bitcast(F32), ALU.subtract).then_inc(piece_low, 1)

            for r in range(ROUNDS):
                project, attend, gate = stages(r)
                for slot in range(SLOTS):
                    u = unit_at(r, slot)
                    if u is not None and u >= 2:
                        add(u - 2)
                    if slot == 0 and gate is not None:
                        keep_x(gate)
                    if slot == 0 and project is not None:
                        power(0, project)
                    if slot == 5 and attend is not None:
                        power(1, attend)
                    if piece_at(r, slot) is not None:
                        low_piece(piece_at(r, slot))
            add(UNITS - 2)
            add(UNITS - 1)

        @block.scalar
        def _(act):
            act.wait_ge(pack_in, 16)
            act.activation(pack_h[:, :], pack[:, 0:split_cols], ACT.Copy).then_inc(w_high, 1)

            def high(s, i):
                act.wait_ge(x_ps[s], i + 1)
                if s:
                    if positive(i):
                        act.wait_ge(xf_done, i)
                    if positive(i):
                        act.wait_ge(g_ps, i)
                else:
                    if positive(i):
                        act.wait_ge(v_ps, i)
                act.activation(xs[s][:, :], ps_x[s][:, :], ACT.Copy).then_inc(x_high[s], 1)

            def qk_high(i):
                act.wait_ge(qk_ps, i + 1)
                if positive(i):
                    act.wait_ge(s_ps, i)
                act.activation(q_s[:, :], ps_qk[:, 0, :], ACT.Identity, bias=q_bias).then_inc(q_high, 1)
                act.activation(k_h[:, :], ps_qk[:, 1, :], ACT.Identity, bias=k_bias).then_inc(k_high, 1)

            def exps(i):
                act.wait_ge(max_step, 2 * i + 2)
                if positive(i):
                    act.wait_ge(p_ps, i)
                if positive(i):
                    act.wait_ge(rsum_done, i)
                for t in range(TPI):
                    act.activation(prob[:, t, :], ps_s[:, t, :], ACT.Exp, bias=ntop[:, t:t + 1], scale=SCALE,
                                   accum_out=psum_row[:, t:t + 1]).then_inc(exp_done, 1)

            def copy_p(i):
                act.wait_ge(p_ps, i + 1)
                if positive(i):
                    act.wait_ge(o_ps, i)
                act.activation(prob_t[:, :, :], ps_p, ACT.Copy).then_inc(p_done, 1)

            def gate_exp(i):
                act.wait_ge(g_step, 3 * i + 3)
                if positive(TOP_STEPS * i):
                    act.wait_ge(d_step, TOP_STEPS * i)
                for t in range(TPI):
                    act.activation(gexp[:, t, 0:EXPERTS], logit[:, t, :], ACT.Exp, bias=nltop[:, t:t + 1])\
                       .then_inc(g_exp, 1)

            def high_piece(k):
                w, e = k // 4, PIECE * (k % 4)
                act.wait_ge((w1_in, w2_in)[w], 16)
                act.activation(w_h[w][:, e:e + PIECE, :], w_f[w][:, e:e + PIECE, :], ACT.Copy)\
                   .then_inc(piece_high, 1)

            def silu(u):
                act.wait_ge(h1_ps, u + 1)
                if positive(u - 1):
                    act.wait_ge(hidden_done, u - 1)
                act.activation(gated[u % 2][:, :], ps_h1[:, :], ACT.Silu).then_inc(silu_done, 1)

            for r in range(ROUNDS):
                project, attend, gate = stages(r)
                for slot in range(SLOTS):
                    u = unit_at(r, slot)
                    if slot == 0 and gate is not None:
                        high(1, gate)
                    if u is not None:
                        silu(u)
                    if slot == 2 and attend is not None:
                        exps(attend)
                    if slot == 2 and gate is not None:
                        gate_exp(gate)
                    if slot == 3 and attend is not None:
                        copy_p(attend)
                    if slot == 4 and project is not None:
                        high(0, project)
                    if slot == 6 and project is not None:
                        qk_high(project)
                    if piece_at(r, slot) is not None:
                        high_piece(piece_at(r, slot))

        @block.tensor
        def _(pe):
            pe.wait_ge(pack_in, 16)
            pe.wait_ge(w_low, 1)
            pe.wait_ge(cleared, 4)

            def turn(s, i):
                pe.wait_ge(ln_done[s], i + 1)
                if s == 0:
                    if positive(i):
                        pe.wait_ge(v_done, i)
                for t in range(TPI):
                    mm = pe.transpose(ps_x[s][:, t * P:(t + 1) * P],
                                      normed[s][:, t, :, :].rearrange("p a c -> p (a c)"), ident)
                mm.then_inc(x_ps[s], 1)

            def project_qkv(i):
                pe.wait_ge(x_low[0], i + 1)
                if positive(i):
                    pe.wait_ge(q_low, i)
                if positive(i):
                    pe.wait_ge(k_low, i)
                for c, n in enumerate(("q_w", "k_w")):
                    for w, first in ((wh[n], True), (wl[n], False)):
                        mm = pe.matmul(ps_qk[:, c, :], w, xs[0][:, :], start=first, stop=not first)
                mm.then_inc(qk_ps, 1)
                for t in range(TPI):
                    for w, first in ((wh["v_w"], True), (wl["v_w"], False)):
                        mm = pe.matmul(ps_v[:, t, :], xs[0][:, t * P:(t + 1) * P], w,
                                       start=first, stop=not first)
                mm.then_inc(v_ps, 1)

            def scores(i):
                pe.wait_ge(q_low, i + 1)
                pe.wait_ge(k_low, i + 1)
                if positive(i):
                    pe.wait_ge(p_done, i)
                for t in range(TPI):
                    for k, first in ((k_h, True), (k_l, False)):
                        mm = pe.matmul(ps_s[:, t, :], q_s[:, t * P:(t + 1) * P], k[:, :],
                                       start=first, stop=not first)
                mm.then_inc(s_ps, 1)

            def turn_p(i):
                pe.wait_ge(exp_done, TPI * (i + 1))
                for t in range(TPI):
                    for k in range(TPI):
                        mm = pe.transpose(ps_p[:, k, t * P:(t + 1) * P], prob[:, t, k * P:(k + 1) * P], ident)
                mm.then_inc(p_ps, 1)

            def values(i):
                pe.wait_ge(p_done, i + 1)
                pe.wait_ge(v_done, i + 1)
                if positive(3 * i - 2):
                    pe.wait_ge(g_step, 3 * i - 2)
                for t in range(TPI):
                    for k in range(TPI):
                        mm = pe.matmul(ps_o[:, t, :], prob_t[:, k, t * P:(t + 1) * P], v_sb[:, k, :],
                                       start=k == 0, stop=k == TPI - 1)
                mm.then_inc(o_ps, 1)

            def gate_product(i):
                pe.wait_ge(x_low[1], i + 1)
                for t in range(TPI):
                    for w, first in ((wh["gate_w"], True), (wl["gate_w"], False)):
                        mm = pe.matmul(ps_logit[:, t * EXPERTS:(t + 1) * EXPERTS],
                                       xs[1][:, t * P:(t + 1) * P], w, start=first, stop=not first)
                mm.then_inc(g_ps, 1)

            def hidden_products(u):
                c, e = u // EXPERTS, u % EXPERTS
                tokens = xf[:, BANK * c:BANK * (c + 1)]
                if e == 0:
                    pe.wait_ge(xf_done, IMAGES // CHUNKS * (c + 1))
                if u < EXPERTS and u % PIECE == 0:
                    pe.wait_ge(piece_low, 4 + u // PIECE + 1)
                if positive(u):
                    pe.wait_ge(silu_done, u)
                for w, first in ((w_h[0], True), (w_l[0], False)):
                    mm = pe.matmul(ps_h1[:, :], w[:, e, :], tokens, start=first, stop=not first)
                mm.then_inc(h1_ps, 1)
                if positive(u - 1):
                    pe.wait_ge(hidden_done, u - 1)
                for w, first in ((w_h[1], True), (w_l[1], False)):
                    mm = pe.matmul(ps_h2[u % 2][:, :], w[:, e, :], tokens, start=first, stop=not first)
                mm.then_inc(h2_ps, 1)

            def output(u):
                if u == 0:
                    pe.wait_ge(w3_in, 16)
                pe.wait_ge(hidden_done, u + 1)
                if positive(u):
                    pe.wait_ge(weighed, u)
                for t in range(CHUNK):
                    mm = pe.matmul(ps_y[:, t, :], hidden[u % 2][:, t * P:(t + 1) * P], w3[:, u % EXPERTS, :],
                                   start=True, stop=True)
                mm.then_inc(y_ps, 1)

            for r in range(ROUNDS):
                project, attend, gate = stages(r)
                for slot in range(SLOTS):
                    u = unit_at(r, slot)
                    if u is not None:
                        hidden_products(u)
                    if slot == 0 and attend is not None:
                        scores(attend)
                    if slot == 0 and gate is not None:
                        gate_product(gate)
                    if slot == 3 and attend is not None:
                        turn_p(attend)
                    if slot == 3 and project is not None:
                        turn(0, project)
                    if slot == 4 and attend is not None:
                        values(attend)
                    if slot == 5 and project is not None:
                        project_qkv(project)
                    if slot == 7 and attend is not None:
                        turn(1, attend)
                    if u is not None and u:
                        output(u - 1)
            output(UNITS - 1)


def shape_arrays(np):
    ident = np.eye(P, dtype=np.float32)
    pair = np.zeros((P, P), np.float32)
    for r in range(P):
        pair[r, r] = pair[r, r ^ 1] = 0.5
    fold = np.zeros((P, QUARTETS, 32), np.float32)
    for q in range(QUARTETS):
        for c in range(GC):
            fold[c::GC, q, GC * q + c] = 1.0
    rep = np.zeros((P, QUART, P), np.float32)
    for j in range(QUART):
        for y in range(16):
            rep[32 * j + y, j, GC * y:GC * y + GC] = rep[32 * j + 16 + y, j, GC * y:GC * y + GC] = 1.0
    grid = np.zeros((P, H, W), np.float32)
    grid[[0, 32, 64, 96]] = 1.0
    grid[97] = np.arange(H)[:, None]
    grid[98] = np.arange(W)[None, :]
    place = np.zeros((3, OMJ, GROUPS, 16), np.float32)
    at = np.arange(16)
    for tap in range(TAPS):
        place[0, 2 * tap] = tap % 3 - 1 - at
        place[2, 2 * tap] = 1.0
        place[0, 2 * tap + 1] = tap // 3 - 1 - at
        place[1, 2 * tap + 1] = 1.0
    return {"ident": ident, "pair": pair, "fold": fold.reshape(P, -1), "rep": rep.reshape(P, -1),
            "grid": grid.reshape(P, -1), "place": place.reshape(3, -1)}


def laid_out(inputs, np):
    f = {k: np.asarray(v) for k, v in inputs.items()}
    twice = lambda a: np.ascontiguousarray(np.concatenate([a, a], 0))
    op = f["L0_conv_op_w"].reshape(QUARTETS, QUART, GC, C)
    op_w = np.zeros((QUART, 32, C), op.dtype)
    for q in range(QUARTETS):
        op_w[:, GC * q:GC * q + GC] = op[q]
    om_b = np.zeros((P, GROUPS * OMJ), f["L0_conv_om_b"].dtype)
    om_b[[0, 32, 64]] = f["L0_conv_om_b"]
    vb = f["L0_conv_vp_b"].reshape(QUARTETS, QUART, GC).transpose(1, 0, 2).reshape(QUART, 1, -1)
    rows = lambda v: np.ascontiguousarray(np.repeat(v.reshape(1, -1), P, 0))
    four = lambda m: np.ascontiguousarray(np.tile(m, (2, 2)))
    return {
        "q_w": four(f["L1_attn_Wq"].T), "k_w": four(f["L1_attn_Wk"].T), "v_w": twice(f["L1_attn_Wv"].T),
        "q_bias": twice(f["L1_attn_bq"].reshape(C, 1)), "k_bias": twice(f["L1_attn_bk"].reshape(C, 1)),
        "v_bias": rows(f["L1_attn_bv"]), "gate_w": twice(f["L1_ffn_gate_w"]), "gate_bias": rows(f["L1_ffn_gate_b"]),
        "w1": twice(f["L1_ffn_w1"].transpose(1, 0, 2).reshape(C, -1)),
        "w2": twice(f["L1_ffn_w2"].transpose(1, 0, 2).reshape(C, -1)),
        "w3": np.ascontiguousarray(f["L1_ffn_w3"].transpose(1, 0, 2).reshape(HIDDEN, -1)),
        "x": f["x"], "x_turned": twice(f["x"].reshape(-1, C).T),
        "dw": twice(f["L0_conv_dw_w"].reshape(TAPS, C).T), "dw_bias": twice(f["L0_conv_dw_b"].reshape(C, 1)),
        "om_w": twice(f["L0_conv_om_w"]), "om_b": om_b, "vp_w": twice(f["L0_conv_vp_w"]),
        "vp_bias": np.repeat(vb, 32, 1).reshape(P, -1), "op_w": op_w.reshape(P, C),
    }


def packed(arrays, np):
    packs = {"keep": KEEP, "start": START, "attention": ATTENTION}
    members = {name for pack in packs.values() for name in pack}
    side = {p: np.ascontiguousarray(np.concatenate([arrays[n] for n in pack], 1)) for p, pack in packs.items()}
    return {**{n: a for n, a in arrays.items() if n not in members}, **side}


def program(nc, d, out, until=3):
    with ExitStack() as ctx:
        t_tok = ctx.enter_context(nc.sbuf_tensor("t_tok", [P, TT, C], F32))
        conv_stage(nc, d, t_tok)
        if until > 1:
            token_stage(nc, d, out, t_tok)
            return
        stored = ctx.enter_context(nc.semaphore("stored_debug"))
        block = ctx.enter_context(nc.Block())

        @block.sync
        def _(sp):
            sp.dma_start(out.rearrange("n h w c -> (n h w) c").rearrange("(t p) c -> p t c", p=P),
                         t_tok[:, :, :]).then_inc(stored, 16)
            sp.wait_ge(stored, 16)


def kernel(**inputs):
    import numpy as np
    import concourse.bacc as bacc
    from concourse.bass_utils import run_bass_kernel_spmd

    arrays = packed({**laid_out(inputs, np), **shape_arrays(np)}, np)
    nc = bacc.Bacc("TRN2", target_bir_lowering=False, num_devices=1)
    d = {name: nc.dram_tensor(f"in_{name}", a.shape, mybir.dt.from_np(a.dtype), kind="ExternalInput").ap()
         for name, a in arrays.items()}
    out = nc.dram_tensor("out", (IMAGES, H, W, C), F32, kind="ExternalOutput").ap()
    program(nc, d, out)
    result = run_bass_kernel_spmd(nc, [{f"in_{name}": a for name, a in arrays.items()}], core_ids=[0])
    return result.results[0]["out"]
```

```python
from contextlib import ExitStack

import concourse.bass as bass
from concourse import mybir

F32 = mybir.dt.float32
F32R = mybir.dt.float32r
BF16 = mybir.dt.bfloat16
ALU = mybir.AluOpType
ACT = mybir.ActivationFunctionType
AX_X = mybir.AxisListType.X

P = 128
IMAGES, H, W, C = 8, 16, 16, 64
PIX = H * W
TT = IMAGES * PIX // P
TPI = PIX // P
GROUPS = 8
GC = C // GROUPS
TAPS = 9
OFFSETS = 2 * TAPS
OMJ = 3 * TAPS
QUART = 4
DUO = 2
DUOS = GROUPS // DUO
QUARTETS = GROUPS // QUART
COLS = TAPS * PIX
BANK = 512
PAIRS = (TAPS + 1) // 2
CPQ = QUART * COLS // BANK
CPI = CPQ * QUARTETS
SUM = 4
SPI = CPI // SUM
TRING, AREP, PROD = 3, 3, 8
FILL_X, FILL_Y = 16 * 4, 16 * 2
EXPERTS, HIDDEN = 16, 128
SCALE = float(C) ** -0.5
GN_EPS, LN_EPS = 1e-5, 1e-5


def positive(value):
    return not isinstance(value, int) or value > 0


def count(eng, value):
    return value if isinstance(value, int) else eng.snap(value)


def spread(ap, dim, n):
    ap = ap.unsqueeze(dim)
    return ap.broadcast_to([n if k == dim else size for k, size in enumerate(ap.shape)])


KEEP = {"pair": P, "fold": QUARTETS * 32, "vp_w": C, "vp_bias": C, "rows": DUO, "op_w": C, "dw": TAPS, "dw_bias": 1,
        "mask_bias": TAPS}
START = {"om_w": GROUPS * OMJ, "om_b": GROUPS * OMJ, "rep": QUART * P, "grid": PIX}
KEEP_COLS, START_COLS = sum(KEEP.values()), sum(START.values())


def columns(pack):
    ends, end = [], 0
    for width in pack.values():
        ends.append(slice(end, end + width))
        end += width
    return ends


def conv_stage(nc, d, t_tok, pack, pack_in):
    with ExitStack() as ctx:
        def sb(name, shape, dt=F32, where=ctx):
            return where.enter_context(nc.sbuf_tensor(name, shape, dt))

        def sem(name):
            return ctx.enter_context(nc.semaphore(name))

        keep = sb("keep", [P, KEEP_COLS])
        at = dict(zip(KEEP, columns(KEEP)))
        pair = keep[:, at["pair"]]
        fold = keep[:, at["fold"]].rearrange("p (q c) -> p q c", q=QUARTETS)
        vp_f = keep[:, at["vp_w"]]
        vp_bias = keep[:, at["vp_bias"]]
        rows = keep[:, at["rows"]]
        op_w = keep[:, at["op_w"]]
        dw = keep[:, at["dw"]]
        dw_bias = keep[:, at["dw_bias"]]
        mask_bias = keep[:, at["mask_bias"]]
        rep = sb("rep", [P, QUART, P], F32R)
        grid = sb("grid", [P, PIX], BF16)
        place = sb("place", [P, OFFSETS, GROUPS, 16], BF16)
        om_h = sb("om_h", [P, OMJ, GROUPS, 16], F32R)
        om_l = sb("om_l", [P, OMJ, GROUPS, 16], F32R)
        vp_h = sb("vp_h", [P, C], F32R)
        vp_l = sb("vp_l", [P, C], F32R)
        xpad = sb("xpad", [P, IMAGES, H + 2, W + 2])
        stats = sb("stats", [P, IMAGES, 6])
        chan = sb("chan", [P, IMAGES, 2])
        gmean = sb("gmean", [P, IMAGES])
        gdev = sb("gdev", [P, IMAGES])
        gsq = sb("gsq", [P, IMAGES])
        gvar = sb("gvar", [P, IMAGES])
        gvar_eps = sb("gvar_eps", [P, IMAGES])
        minus_half = sb("minus_half", [P, IMAGES])
        grstd = sb("grstd", [P, IMAGES])
        gshift = sb("gshift", [P, IMAGES])
        conv = sb("conv", [P, H, W])
        xd = [sb(f"xd{i}", [P, PIX], F32R) for i in range(2)]
        x_parts = sb("x_parts", [P, H, W], F32R)
        xrep = sb("xrep", [P, H // 2, 8, W], F32R)
        v_sb = sb("v_sb", [P, H // 2, C])
        v_parts = sb("v_parts", [P, H, GROUPS, GC], F32R)
        vt = sb("vt", [P, GROUPS, H, GC], F32R)
        b_h = [sb(f"b_h{i}", [P, TAPS, PIX], F32R) for i in range(2)]
        b_l = [sb(f"b_l{i}", [P, TAPS, PIX], F32R) for i in range(2)]
        a_h = sb("a_h", [P, TAPS, PIX], F32R)
        a_l = sb("a_l", [P, TAPS, PIX], F32R)
        a_rep = [sb(f"a_rep{i}", [P, BANK]) for i in range(AREP)]
        prod = [sb(f"prod{i}", [P, BANK]) for i in range(PROD)]
        d_sb = sb("d_sb", [P, BANK])
        with ExitStack() as early:
            x_turned = sb("x_turned", [P, IMAGES, H, W], F32, early)
            start = sb("start", [P, START_COLS], F32, early)
            om_lf = sb("om_lf", [P, GROUPS, OMJ], F32, early)
            om_hf = sb("om_hf", [P, GROUPS, OMJ], F32R, early)
            bias_s = sb("bias_s", [P, 3, GROUPS, OMJ], BF16, early)
            bias_sel = sb("bias_sel", [P, GROUPS, OMJ], BF16, early)
            place_f = sb("place_f", [P, OFFSETS * P], F32, early)
        ahead = dict(zip(START, columns(START)))
        om_f = start[:, ahead["om_w"]].rearrange("p (g j) -> p g j", g=GROUPS)
        bias_f = start[:, ahead["om_b"]].rearrange("p (g j) -> p g j", g=GROUPS)
        rep_f = start[:, ahead["rep"]].rearrange("p (j c) -> p j c", j=QUART)
        grid_f = start[:, ahead["grid"]]
        mb = [sb(f"mb{m}", [P, TAPS, PIX], F32R) for m in range(DUOS)]
        ma = [sb(f"ma{q}", [P, TAPS, PIX], F32R) for q in range(QUARTETS)]

        ps_t = [ctx.enter_context(nc.psum_tensor(f"ps_t{i}", [P, BANK], F32)) for i in range(TRING)]
        ps_a = [ctx.enter_context(nc.psum_tensor(f"ps_a{i}", [P, BANK], F32)) for i in range(2)]
        ps_d = ctx.enter_context(nc.psum_tensor("ps_d", [P, BANK], F32))
        ps_m = [ctx.enter_context(nc.psum_tensor(f"ps_m{i}", [P, BANK], F32)) for i in range(2)]

        x_in = [sem(f"x_in{half}") for half in range(2)]
        keep_in = sem("keep_in")
        start_in = sem("start_in")
        place_in = sem("place_in")
        tokens_in = sem("tokens_in")
        zeroed = sem("zeroed")
        bn_done = sem("bn_done")
        chan_stats = sem("chan_stats")
        pair_sums = sem("pair_sums")
        gn_steps = sem("gn_steps")
        gn_pow = sem("gn_pow")
        xn_ready = sem("xn_ready")
        bias_steps = sem("bias_steps")
        place_done = sem("place_done")
        w_dve = sem("w_dve")
        w_act = sem("w_act")
        taps_done = sem("taps_done")
        xd_high = sem("xd_high")
        xd_ready = sem("xd_ready")
        y_pos = sem("y_pos")
        x_pos = sem("x_pos")
        mask_ps = sem("mask_ps")
        y_abs = sem("y_abs")
        x_abs = sem("x_abs")
        y_hat = sem("y_hat")
        x_hat = sem("x_hat")
        a_full = sem("a_full")
        a_high = sem("a_high")
        b_high = sem("b_high")
        a_low = sem("a_low")
        b_low = sem("b_low")
        mb_filled = [sem(f"mb_filled{m}") for m in range(DUOS)]
        ma_filled = [sem(f"ma_filled{q}") for q in range(QUARTETS)]
        x_high = sem("x_high")
        x_low = sem("x_low")
        xrep_ready = sem("xrep_ready")
        v_ps = sem("v_ps")
        v_done = sem("v_done")
        v_high = sem("v_high")
        v_low = sem("v_low")
        vt_ready = sem("vt_ready")
        t_ready = sem("t_ready")
        a_ready = sem("a_ready")
        a_copied = sem("a_copied")
        weighted = sem("weighted")
        reduced = sem("reduced")
        d_copied = sem("d_copied")
        out_ps = sem("out_ps")
        t_done = sem("t_done")

        xview = d["x"].rearrange("n h w c -> (n h w) c").rearrange("(t p) c -> p t c", p=P)
        inner = lambda n: xpad[:, n, 1:H + 1, 1:W + 1]

        def pair_cols(k):
            return slice(2 * k, min(2 * k + 2, TAPS))

        MADE_AT = [4 + b for b in range(3 * PAIRS)]
        OUT_AT, V_AT = 21, (20, 25)
        X_SPLIT_AT, X_REP_AT = 1, (11, 15, 21, 22)
        V_SPLIT_AT = (24, 30)
        TABLES_AT = (32, 2)
        SUM_AT, XD_SPLIT_AT = 5, 35
        TAPS_AT = (1, 2, 6, 9, 12, 15, 20, 24, 30)

        def product(c, par):
            return prod[(CPI * par + c) % PROD]

        def job_at(c):
            return divmod(MADE_AT.index(c), 3) if c in MADE_AT else (None, None)

        block = ctx.enter_context(nc.Block())

        @block.sync
        def _(sp):
            sp.dma_start(start[:, :], d["start"]).then_inc(start_in, 16)
            sp.dma_start(place_f[96:99, :], d["place"]).then_inc(place_in, 16)
            for half in range(2):
                n = slice(half * IMAGES // 2, (half + 1) * IMAGES // 2)
                sp.dma_start(x_turned[:, n, :, :],
                             d["x_turned"].rearrange("c (n y x) -> c n y x", y=H, x=W)[:, n, :, :])\
                  .then_inc(x_in[half], 16)
            sp.dma_start(keep[:, :], d["keep"]).then_inc(keep_in, 16)
            sp.dma_start(t_tok[:, :, :], xview).then_inc(tokens_in, 16)
            sp.dma_start(pack[:, :], d["attention"]).then_inc(pack_in, 16)

            def fill(n, par):
                made = count(sp, PAIRS * (n + 1))
                free = [count(sp, CPI * (n - 1) + CPQ * (q + 1)) for q in range(QUARTETS)]
                sp.wait_ge(b_low, made)
                for q in range(QUARTETS):
                    if positive(free[q]):
                        sp.wait_ge(t_ready, free[q])
                    for part, src in enumerate((a_h, a_l)):
                        sp.dma_start(ma[q][64 * part:64 * part + 64, :, :].bitcast(F32),
                                     src[64 * q:64 * q + 64, :, :].bitcast(F32)).then_inc(ma_filled[q], 16)
                    for m in (2 * q, 2 * q + 1):
                        for r in range(4):
                            src = (b_h, b_l)[r % 2][par]
                            sp.dma_start(mb[m][32 * r:32 * r + 32, :, :].bitcast(F32),
                                         src[32 * m:32 * m + 32, :, :].bitcast(F32)).then_inc(mb_filled[m], 16)

            fill(0, 0)
            fill(1, 1)
            with sp.Fori(1, IMAGES // 2) as it:
                for par in range(2):
                    fill(2 * it + par, par)

        @block.tensor
        def _(pe):
            pe.wait_ge(keep_in, 16)
            pe.wait_ge(chan_stats, IMAGES)
            pe.matmul(ps_m[0][:, 0:IMAGES], pair, chan[:, :, 0], start=True, stop=True).then_inc(pair_sums, 1)
            pe.wait_ge(gn_steps, 4)
            pe.matmul(ps_m[0][:, IMAGES:2 * IMAGES], pair, gvar[:, :], start=True, stop=True)\
              .then_inc(pair_sums, 1)

            def positions(k, kind, par, signal):
                for c, tap in enumerate(range(2 * k, min(2 * k + 2, TAPS))):
                    j = (2 * tap + 1, 2 * TAPS + tap, 2 * tap)[kind]
                    out = ps_m[(3 * k + kind) % 2][:, c * PIX:(c + 1) * PIX]
                    pe.matmul(out, om_h[:, j, :, :].rearrange("p g x -> p (g x)"), xd[par][:, :],
                              start=True, stop=False)
                    mm = pe.matmul(out, om_l[:, j, :, :].rearrange("p g x -> p (g x)"), xd[par][:, :],
                                   start=False, stop=kind == 1)
                    if kind != 1:
                        mm = pe.matmul(out, place[0:99, j, :, :].rearrange("p g x -> p (g x)"), grid[0:99, :],
                                       start=False, stop=True)
                mm.then_inc(signal, 1)

            def job(k, kind, n, par):
                if kind == 0:
                    if k == 0:
                        pe.wait_ge(xd_ready, n + 1)
                        if positive(2 * n - 1):
                            pe.wait_ge(v_done, 2 * n - 1)
                    else:
                        pe.wait_ge(a_full, PAIRS * n + k)
                    positions(k, kind, par, y_pos)
                elif kind == 1:
                    if k == 0:
                        if positive(2 * n):
                            pe.wait_ge(v_done, 2 * n)
                    else:
                        pe.wait_ge(x_abs, PAIRS * n + k)
                    positions(k, kind, par, mask_ps)
                else:
                    pe.wait_ge(y_abs, PAIRS * n + k + 1)
                    positions(k, kind, par, x_pos)

            def job_v(half, n):
                if half == 0:
                    pe.wait_ge(x_abs, PAIRS * (n + 1))
                elif isinstance(n, int) and n < 2:
                    pe.wait_ge(a_full, PAIRS * (n + 1))
                else:
                    pe.wait_ge(t_done, n - 1)
                pe.wait_ge(xrep_ready, 4 * n + 2 * half + 2)
                for y in range(H // 2):
                    for w, first in ((vp_h, True), (vp_l, False)):
                        mm = pe.matmul(ps_m[half][:, y * C:(y + 1) * C],
                                       xrep[:, y, :, :].rearrange("p r x -> p (r x)"), w[:, :],
                                       start=first, stop=not first)
                mm.then_inc(v_ps, 1)

            def job_out(i, free_sem, free):
                pe.wait_ge(d_copied, i + 1)
                pe.wait_ge(free_sem, free)
                for t in range(TPI):
                    for h in range(2):
                        mm = pe.matmul(ps_m[1][:, t * C:(t + 1) * C],
                                       d_sb[:, h * PIX + t * P:h * PIX + (t + 1) * P], op_w,
                                       start=h == 0, stop=h == 1)
                mm.then_inc(out_ps, 1)

            def segments(c):
                v = c % CPQ
                if v < CPQ - 2:
                    return [(0, v % QUART, 2 * (v // QUART), 2)]
                return [(PIX * s, 2 * (v % 2) + s, TAPS - 1, 1) for s in range(2)]

            def sample_x(c, i):
                q = c // CPQ
                if c % CPQ == 0:
                    pe.wait_ge(vt_ready, 4 * i + 2 * q + 2)
                if c % CPQ in (0, DUO):
                    m = 2 * q + c % CPQ // DUO
                    pe.wait_ge(mb_filled[m], FILL_X * (i + 1))
                if positive(CPI * i + c - TRING + 1):
                    pe.wait_ge(weighted, CPI * i + c - TRING + 1)
                for col, j, tap, n in segments(c):
                    out = ps_t[c % TRING][:, col:col + n * PIX]
                    mm = pe.matmul(out, vt[:, QUART * q + j, :, :].rearrange("p y c -> p (y c)"),
                                   mb[2 * q + j // DUO][:, tap:tap + n, :].rearrange("p t x -> p (t x)"),
                                   start=True, stop=True)
                mm.then_inc(t_ready, 1)

            def replicate_a(c, i):
                q = c // CPQ
                if c % CPQ == 0:
                    pe.wait_ge(ma_filled[q], FILL_Y * (i + 1))
                if positive(CPI * i + c - 1):
                    pe.wait_ge(a_copied, CPI * i + c - 1)
                for col, j, tap, n in segments(c):
                    mm = pe.matmul(ps_a[c % 2][:, col:col + n * PIX], rep[:, j, :],
                                   ma[q][:, tap:tap + n, :].rearrange("p t x -> p (t x)"),
                                   start=True, stop=True)
                mm.then_inc(a_ready, 1)

            def reduce_chunks(r, i, par):
                pe.wait_ge(weighted, CPI * i + SUM * (r + 1))
                if r == 0:
                    if positive(i):
                        pe.wait_ge(d_copied, i)
                for c in range(SUM * r, SUM * (r + 1)):
                    for col, j, tap, n in segments(c):
                        mm = pe.matmul(ps_d[32 * j:32 * j + 32, 0:n * PIX],
                                       fold[:, c // CPQ, :], product(c, par)[:, col:col + n * PIX],
                                       start=c < QUART, stop=c >= CPI - 2, skip_group_check=True)
                mm.then_inc(reduced, 1)

            def image(i, par, made):
                n, npar = i + 1, 1 - par
                first_image = isinstance(i, int) and i == 0
                for c in range(CPI):
                    if c == 0:
                        replicate_a(0, i)
                    sample_x(c, i)
                    if c + 1 < CPI:
                        replicate_a(c + 1, i)
                    k, kind = job_at(c)
                    if made and k is not None:
                        job(k, kind, n, npar)
                    if c == OUT_AT and not first_image:
                        if made:
                            job_out(i - 1, a_full, PAIRS * (n + 1))
                        else:
                            job_out(i - 1, v_done, 2 * n)
                    if made and c in V_AT:
                        job_v(V_AT.index(c), n)
                    if c % SUM == SUM - 1 and c > SUM:
                        reduce_chunks(c // SUM - 1, i, par)
                    if c == SUM - 1 and not first_image:
                        reduce_chunks(SPI - 1, i - 1, 1 - par)

            pe.wait_ge(place_done, 2)
            pe.wait_ge(w_act, 5)
            pe.wait_ge(gn_steps, 5)
            for k in range(PAIRS):
                for kind in range(3):
                    if (k, kind) == (0, 1):
                        pe.wait_ge(place_done, 3)
                    job(k, kind, 0, 0)
            pe.wait_ge(w_dve, 2)
            job_v(0, 0)
            job_v(1, 0)
            pe.wait_ge(w_act, 6)
            image(0, 0, True)
            image(1, 1, True)
            with pe.Fori(1, IMAGES // 2 - 1) as it:
                for par in range(2):
                    image(2 * it + par, par, True)
            image(IMAGES - 2, 0, True)
            image(IMAGES - 1, 1, False)
            reduce_chunks(SPI - 1, IMAGES - 1, 1)
            job_out(IMAGES - 1, t_done, IMAGES - 1)

        @block.scalar
        def _(act):
            replicated = lambda t: spread(t[:, :, :].rearrange("p g j -> p j g"), 3, 16)
            act.wait_ge(start_in, 16)
            act.activation(om_hf[:, :, :], om_f, ACT.Copy).then_inc(w_act, 1)
            act.activation(om_h[:, :, :, :], replicated(om_f), ACT.Copy).then_inc(w_act, 1)
            act.wait_ge(w_dve, 1)
            act.activation(om_l[:, :, :, :], replicated(om_lf), ACT.Copy).then_inc(w_act, 1)
            act.wait_ge(place_in, 16)
            act.activation(place[96:99, :, :, :].rearrange("p j g x -> p (j g x)"), place_f[96:99, :],
                           ACT.Copy).then_inc(place_done, 1)
            act.activation(grid[:, :], grid_f, ACT.Copy).then_inc(w_act, 1)
            act.wait_ge(keep_in, 16)
            act.activation(vp_h[:, :], vp_f, ACT.Copy).then_inc(w_act, 1)
            act.wait_ge(zeroed, 2)
            act.wait_ge(gn_steps, 6)
            for n in range(IMAGES):
                act.wait_ge(x_in[n // (IMAGES // 2)], 16)
                act.activation(inner(n), x_turned[:, n, :, :], ACT.Identity, bias=gshift[:, n:n + 1],
                               scale=grstd[:, n:n + 1]).then_inc(xn_ready, 1)
            act.activation(rep[:, :, :], rep_f, ACT.Copy).then_inc(w_act, 1)

            def xd_split(n, par):
                act.wait_ge(taps_done, TAPS * (n + 1))
                if positive(PAIRS * (n - 1)):
                    act.wait_ge(mask_ps, PAIRS * (n - 1))
                if positive(PAIRS * (n - 1)):
                    act.wait_ge(x_pos, PAIRS * (n - 1))
                act.activation(xd[par][:, :], conv[:, :, :].rearrange("p y x -> p (y x)"), ACT.Copy)\
                   .then_inc(xd_high, 1)

            def x_split(n):
                if positive(2 * n):
                    act.wait_ge(v_ps, 2 * n)
                act.activation(x_parts[:, :, :], inner(n), ACT.Copy).then_inc(x_high, 1)

            def x_rep(half, n, quarters=(0, 1)):
                act.wait_ge(x_low, n + 1)
                if positive(2 * n + half):
                    act.wait_ge(v_ps, 2 * n + half)
                for s in quarters:
                    y = 8 * half + 4 * s
                    act.activation(xrep[:, 4 * s:4 * s + 4, :, :],
                                   spread(x_parts[:, y:y + 4, :].bitcast(F32), 2, 8), ACT.Copy)\
                       .then_inc(xrep_ready, 1)

            def abs_y(k, n, par):
                if k == 0:
                    for q in range(QUARTETS):
                        if positive(FILL_Y * n):
                            act.wait_ge(ma_filled[q], FILL_Y * n)
                act.wait_ge(y_pos, PAIRS * n + k + 1)
                w = min(2, TAPS - 2 * k) * PIX
                act.activation(a_l[:, pair_cols(k), :].bitcast(F32).rearrange("p t x -> p (t x)"),
                               ps_m[3 * k % 2][:, 0:w], ACT.Abs).then_inc(y_abs, 1)

            def abs_x(k, n, par):
                if k == 0:
                    for m in range(DUOS):
                        if positive(FILL_X * (n - 1)):
                            act.wait_ge(mb_filled[m], FILL_X * (n - 1))
                act.wait_ge(x_pos, PAIRS * n + k + 1)
                w = min(2, TAPS - 2 * k) * PIX
                act.activation(b_l[par][:, pair_cols(k), :].bitcast(F32).rearrange("p t x -> p (t x)"),
                               ps_m[3 * k % 2][:, 0:w], ACT.Abs).then_inc(x_abs, 1)

            def high_part_a(k, n, par):
                act.wait_ge(a_full, PAIRS * n + k + 1)
                act.activation(a_h[:, pair_cols(k), :], a_l[:, pair_cols(k), :].bitcast(F32), ACT.Copy)\
                   .then_inc(a_high, 1)

            def high_part_b(k, n, par):
                act.wait_ge(x_hat, PAIRS * n + k + 1)
                act.activation(b_h[par][:, pair_cols(k), :], b_l[par][:, pair_cols(k), :].bitcast(F32), ACT.Copy)\
                   .then_inc(b_high, 1)

            def v_split(half, n):
                act.wait_ge(v_done, 2 * n + half + 1)
                if positive(4 * n):
                    act.wait_ge(vt_ready, 4 * n)
                act.activation(v_parts[:, 8 * half:8 * half + 8, :, :].rearrange("p y g c -> p y (g c)"),
                               v_sb[:, :, :], ACT.Copy).then_inc(v_high, 1)

            def tables(q, n):
                act.wait_ge(v_low, 2 * n + 2)
                if positive(CPI * (n - 1) + CPQ * (q + 1)):
                    act.wait_ge(t_ready, CPI * (n - 1) + CPQ * (q + 1))
                for g in range(DUO):
                    groups = slice(QUART * q + g, QUART * (q + 1), DUO)
                    act.activation(vt[:, groups, :, :],
                                   v_parts[:, :, groups, :].bitcast(F32).rearrange("p y g c -> p g y c"),
                                   ACT.Copy, scale=rows[:, g:g + 1]).then_inc(vt_ready, 1)

            def copy_a(c, i):
                act.wait_ge(a_ready, CPI * i + c + 1)
                if positive(CPI * i + c - AREP + 1):
                    act.wait_ge(weighted, CPI * i + c - AREP + 1)
                act.activation(a_rep[c % AREP][:, :], ps_a[c % 2][:, :], ACT.Copy).then_inc(a_copied, 1)

            def copy_d(i):
                act.wait_ge(reduced, SPI * (i + 1))
                if positive(i):
                    act.wait_ge(out_ps, i)
                act.activation(d_sb[:, :], ps_d[:, :], ACT.Copy).then_inc(d_copied, 1)

            def image(i, par, made, ahead):
                n, npar = i + 1, 1 - par
                for c in range(CPI):
                    if c == 0:
                        copy_a(0, i)
                    if c + 1 < CPI:
                        copy_a(c + 1, i)
                    k, kind = job_at(c)
                    if made and kind == 0:
                        abs_y(k, n, npar)
                    if made and kind == 2:
                        abs_x(k, n, npar)
                    k, kind = job_at(c - 3)
                    if made and kind == 1:
                        high_part_a(k, n, npar)
                        high_part_b(k, n, npar)
                    if c == TABLES_AT[1]:
                        tables(1, i)
                    if made and c == X_SPLIT_AT:
                        x_split(n)
                    if made and c == TABLES_AT[0]:
                        tables(0, n)
                    if c == SUM_AT and not (isinstance(i, int) and i == 0):
                        copy_d(i - 1)
                    if made and c in X_REP_AT:
                        half, quarter = divmod(X_REP_AT.index(c), 2)
                        x_rep(half, n, (quarter,))
                    if made and c in V_SPLIT_AT:
                        v_split(V_SPLIT_AT.index(c), n)
                    if ahead and c == XD_SPLIT_AT:
                        xd_split(i + 2, par)

            xd_split(0, 0)
            x_split(0)
            abs_y(0, 0, 0)
            x_rep(0, 0)
            for k in range(PAIRS):
                abs_x(k, 0, 0)
                if k + 1 < PAIRS:
                    abs_y(k + 1, 0, 0)
                high_part_a(k, 0, 0)
                high_part_b(k, 0, 0)
            x_rep(1, 0)
            v_split(0, 0)
            v_split(1, 0)
            tables(0, 0)
            xd_split(1, 1)
            image(0, 0, True, True)
            image(1, 1, True, True)
            with act.Fori(1, IMAGES // 2 - 1) as it:
                for par in range(2):
                    image(2 * it + par, par, True, True)
            image(IMAGES - 2, 0, True, False)
            image(IMAGES - 1, 1, False, False)
            copy_d(IMAGES - 1)

        @block.vector
        def _(dve):
            dve.wait_ge(start_in, 16)
            dve.tensor_copy(bias_s[:, 0, :, :], bias_f).then_inc(bias_steps, 1)
            for part in range(2):
                dve.wait_ge(bias_steps, 2 * part + 1)
                dve.tensor_tensor(bias_f, bias_f, bias_s[:, part, :, :], ALU.subtract)\
                   .then_inc(bias_steps, 1)
                dve.wait_ge(bias_steps, 2 * part + 2)
                dve.tensor_copy(bias_s[:, part + 1, :, :], bias_f).then_inc(bias_steps, 1)
            dve.wait_ge(bias_steps, 5)
            for part in range(3):
                r = slice(32 * part, 32 * part + 32)
                dve.tensor_copy(bias_sel[r, :, :], bias_s[r, part, :, :]).then_inc(bias_steps, 1)
            dve.wait_ge(w_act, 1)
            dve.tensor_tensor(om_lf[:, :, :], om_f, om_hf[:, :, :].bitcast(F32), ALU.subtract).then_inc(w_dve, 1)

            def place_bias(first, last):
                dve.wait_ge(bias_steps, 8)
                dve.tensor_copy(place[0:96, first:last, :, :],
                                spread(bias_sel[0:96, :, first:last].rearrange("p g j -> p j g"), 3, 16))\
                   .then_inc(place_done, 1)

            for n in range(IMAGES):
                dve.wait_ge(x_in[n // (IMAGES // 2)], 16)
                dve.bn_stats(stats[:, n, :], x_turned[:, n, :, :].rearrange("p y x -> p (y x)"))\
                   .then_inc(bn_done, 1)
            for n in range(IMAGES):
                dve.wait_ge(bn_done, n + 1)
                dve.bn_aggr(chan[:, n, :], stats[:, n, :]).then_inc(chan_stats, 1)
            dve.wait_ge(pair_sums, 1)
            dve.tensor_copy(gmean[:, :], ps_m[0][:, 0:IMAGES]).then_inc(gn_steps, 1)
            dve.wait_ge(gn_steps, 1)
            dve.wait_ge(chan_stats, IMAGES)
            dve.tensor_tensor(gdev[:, :], chan[:, :, 0], gmean[:, :], ALU.subtract).then_inc(gn_steps, 1)
            dve.wait_ge(gn_steps, 2)
            dve.tensor_tensor(gsq[:, :], gdev[:, :], gdev[:, :], ALU.mult).then_inc(gn_steps, 1)
            dve.wait_ge(gn_steps, 3)
            dve.tensor_tensor(gvar[:, :], gsq[:, :], chan[:, :, 1], ALU.add).then_inc(gn_steps, 1)
            dve.wait_ge(pair_sums, 2)
            dve.tensor_scalar(gvar_eps[:, :], ps_m[0][:, IMAGES:2 * IMAGES], GN_EPS, None, ALU.add)\
               .then_inc(gn_steps, 1)
            place_bias(0, 10)
            dve.wait_ge(gn_pow, 1)
            dve.scalar_tensor_tensor(out=gshift[:, :], in0=gmean[:, :], scalar=-1.0, in1=grstd[:, :],
                                     op0=ALU.mult, op1=ALU.mult).then_inc(gn_steps, 1)

            def tap_step(tap, n):
                if tap == 0:
                    dve.wait_ge(xn_ready, n + 1)
                    if positive(n):
                        dve.wait_ge(xd_high, n)
                    if positive(n):
                        dve.wait_ge(xd_ready, n)
                if positive(TAPS * n + tap):
                    dve.wait_ge(taps_done, TAPS * n + tap)
                src = xpad[:, n, tap // 3:tap // 3 + H, tap % 3:tap % 3 + W]
                if tap == 0:
                    dve.tensor_scalar(conv[:, :, :], src, dw[:, 0:1], dw_bias[:, 0:1],
                                      ALU.mult, ALU.add).then_inc(taps_done, 1)
                else:
                    dve.scalar_tensor_tensor(out=conv[:, :, :], in0=src, scalar=dw[:, tap:tap + 1],
                                             in1=conv[:, :, :], op0=ALU.mult, op1=ALU.add)\
                       .then_inc(taps_done, 1)

            def hat_y(k, n, par):
                dve.wait_ge(y_abs, PAIRS * n + k + 1)
                v = a_l[:, pair_cols(k), :].bitcast(F32)
                dve.tensor_scalar(v, v, 1.0, 1.0, ALU.min, ALU.subtract).then_inc(y_hat, 1)

            def masked(k, n, par):
                dve.wait_ge(y_hat, PAIRS * n + k + 1)
                dve.wait_ge(mask_ps, PAIRS * n + k + 1)
                taps = range(2 * k, min(2 * k + 2, TAPS))
                for c, tap in enumerate(taps):
                    v = a_l[:, tap, :].bitcast(F32)
                    op = dve.scalar_tensor_tensor(out=v, in0=ps_m[(3 * k + 1) % 2][:, c * PIX:(c + 1) * PIX],
                                                  scalar=mask_bias[:, tap:tap + 1], in1=v,
                                                  op0=ALU.add, op1=ALU.mult)
                op.then_inc(a_full, 1)

            def hat_x(k, n, par):
                dve.wait_ge(x_abs, PAIRS * n + k + 1)
                v = b_l[par][:, pair_cols(k), :].bitcast(F32)
                dve.tensor_scalar(v, v, 1.0, 1.0, ALU.min, ALU.subtract).then_inc(x_hat, 1)

            def v_out(half, n):
                dve.wait_ge(v_ps, 2 * n + half + 1)
                if positive(2 * n + half):
                    dve.wait_ge(v_low, 2 * n + half)
                dve.tensor_tensor(v_sb[:, :, :], ps_m[half][:, :].rearrange("p (y c) -> p y c", c=C),
                                  spread(vp_bias, 1, 8), ALU.add).then_inc(v_done, 1)

            def weight(c, i, par):
                dve.wait_ge(t_ready, CPI * i + c + 1)
                dve.wait_ge(a_copied, CPI * i + c + 1)
                if positive(SPI * i + (c - PROD) // SUM + 1):
                    dve.wait_ge(reduced, SPI * i + (c - PROD) // SUM + 1)
                dve.tensor_tensor(product(c, par)[:, :], ps_t[c % TRING][:, :], a_rep[c % AREP][:, :], ALU.mult)\
                   .then_inc(weighted, 1)

            def residual(i):
                if isinstance(i, int) and i == 0:
                    dve.wait_ge(tokens_in, 16)
                dve.wait_ge(out_ps, i + 1)
                t = t_tok[:, bass.ds(TPI * i, TPI), :].rearrange("p t c -> p (t c)")
                dve.tensor_tensor(t, ps_m[1][:, 0:TPI * C], t, ALU.add).then_inc(t_done, 1)

            def image(i, par, made, ahead):
                n, npar = i + 1, 1 - par
                for c in range(CPI):
                    weight(c, i, par)
                    k, kind = job_at(c)
                    if made and k is not None:
                        (hat_y, masked, hat_x)[kind](k, n, npar)
                    if c == OUT_AT + 1 and not (isinstance(i, int) and i == 0):
                        residual(i - 1)
                    if made and c - 1 in V_AT:
                        v_out(V_AT.index(c - 1), n)
                    if ahead and c in TAPS_AT:
                        tap_step(TAPS_AT.index(c), i + 2)

            for tap in range(TAPS):
                tap_step(tap, 0)
            place_bias(10, OFFSETS)
            dve.wait_ge(w_act, 5)
            dve.tensor_tensor(vp_l[:, :], vp_f, vp_h[:, :].bitcast(F32), ALU.subtract).then_inc(w_dve, 1)
            for k in range(PAIRS):
                hat_y(k, 0, 0)
                masked(k, 0, 0)
                hat_x(k, 0, 0)
            v_out(0, 0)
            v_out(1, 0)
            for tap in range(TAPS):
                tap_step(tap, 1)
            image(0, 0, True, True)
            image(1, 1, True, True)
            with dve.Fori(1, IMAGES // 2 - 1) as it:
                for par in range(2):
                    image(2 * it + par, par, True, True)
            image(IMAGES - 2, 0, True, False)
            image(IMAGES - 1, 1, False, False)
            residual(IMAGES - 1)

        @block.gpsimd
        def _(pool):
            pool.memset(minus_half[:, :], -0.5).then_inc(zeroed, 1)
            pool.memset(xpad[:, :, :, :], 0.0).then_inc(zeroed, 1)
            pool.wait_ge(zeroed, 2)
            pool.wait_ge(gn_steps, 5)
            pool.tensor_tensor(grstd[:, :], gvar_eps[:, :], minus_half[:, :], ALU.pow).then_inc(gn_pow, 1)

            def xd_low(n, par):
                if positive(2 * n):
                    pool.wait_ge(v_low, 2 * n)
                pool.wait_ge(xd_high, n + 1)
                pool.tensor_tensor(xd[par][64:P, :], conv[64:P, :, :].rearrange("p y x -> p (y x)"),
                                   xd[par][64:P, :].bitcast(F32), ALU.subtract).then_inc(xd_ready, 1)

            def low_parts(k, n, par):
                if k == 0:
                    pool.wait_ge(xd_ready, n + 1)
                    pool.wait_ge(x_low, n + 1)
                for full, high, high_done, low_done in ((a_l, a_h, a_high, a_low),
                                                        (b_l[par], b_h[par], b_high, b_low)):
                    pool.wait_ge(high_done, PAIRS * n + k + 1)
                    pool.tensor_tensor(full[:, pair_cols(k), :], full[:, pair_cols(k), :].bitcast(F32),
                                       high[:, pair_cols(k), :].bitcast(F32), ALU.subtract).then_inc(low_done, 1)

            def x_rest(n):
                pool.wait_ge(xd_ready, min(n + 1, IMAGES) if isinstance(n, int) else n + 1)
                pool.wait_ge(x_high, n + 1)
                pool.tensor_tensor(x_parts[64:P, :, :], inner(n)[64:P, :, :],
                                   x_parts[64:P, :, :].bitcast(F32), ALU.subtract).then_inc(x_low, 1)

            def v_rest(half, n):
                if half == 0:
                    pool.wait_ge(b_low, PAIRS * (n + 1))
                if positive(2 * n + half):
                    pool.wait_ge(v_low, 2 * n + half)
                pool.wait_ge(v_high, 2 * n + half + 1)
                parts = v_parts[64:P, 8 * half:8 * half + 8, :, :].rearrange("p y g c -> p y (g c)")
                pool.tensor_tensor(parts, v_sb[64:P, :, :], parts.bitcast(F32), ALU.subtract).then_inc(v_low, 1)

            def image(i, par, made, ahead):
                n, npar = i + 1, 1 - par
                if made:
                    x_rest(n)
                    for k in range(PAIRS):
                        low_parts(k, n, npar)
                if made:
                    v_rest(0, n)
                    v_rest(1, n)
                if ahead:
                    xd_low(i + 2, par)

            xd_low(0, 0)
            x_rest(0)
            for k in range(PAIRS):
                low_parts(k, 0, 0)
            v_rest(0, 0)
            v_rest(1, 0)
            xd_low(1, 1)
            image(0, 0, True, True)
            image(1, 1, True, True)
            with pool.Fori(1, IMAGES // 2 - 1) as it:
                for par in range(2):
                    image(2 * it + par, par, True, True)
            image(IMAGES - 2, 0, True, False)
            image(IMAGES - 1, 1, False, False)


ATTENTION = {"q_w": P, "k_w": P, "v_w": C, "gate_w": EXPERTS, "ident": P, "q_bias": 1, "k_bias": 1,
             "v_bias": C, "gate_bias": EXPERTS, "join": C}
ATTENTION_COLS = sum(ATTENTION.values())


def token_stage(nc, d, out, t_tok, pack, pack_in):
    SLOTS = 8
    DUETS = EXPERTS // 2
    UNITS = EXPERTS * IMAGES
    FIRST = 3
    ROUNDS = FIRST + IMAGES
    FINISH = 4
    PIECE = EXPERTS // 4

    with ExitStack() as ctx:
        def sb(name, shape, dt=F32):
            return ctx.enter_context(nc.sbuf_tensor(name, shape, dt))

        def ps(name):
            return ctx.enter_context(nc.psum_tensor(name, [P, BANK], F32))

        def sem(name):
            return ctx.enter_context(nc.semaphore(name))

        two = range(2)
        at = {n: pack[:, cols] for n, cols in zip(ATTENTION, columns(ATTENTION))}
        ident, q_bias, k_bias = at["ident"], at["q_bias"], at["k_bias"]
        SPLIT = ("q_w", "k_w", "v_w", "gate_w")
        split_cols = sum(ATTENTION[n] for n in SPLIT)
        pack_h = sb("attention_high", [P, split_cols], F32R)
        pack_l = sb("attention_low", [P, split_cols], F32R)
        wh = {n: pack_h[:, cols] for n, cols in zip(SPLIT, columns(ATTENTION))}
        wl = {n: pack_l[:, cols] for n, cols in zip(SPLIT, columns(ATTENTION))}
        minus_half = sb("minus_half2", [P, TPI])
        stats = [sb(f"ln_stats{s}", [P, TPI, 6]) for s in two]
        moments = [sb(f"ln_moments{s}", [P, TPI, 2]) for s in two]
        var_eps = [sb(f"ln_var{s}", [P, TPI]) for s in two]
        rstd = [sb(f"ln_rstd{s}", [P, TPI]) for s in two]
        normed = [sb(f"ln_out{s}", [P, TPI, 2, C]) for s in two]
        xs = [sb(f"xs{s}", [P, PIX], F32R) for s in two]
        q_s = sb("q_s", [P, PIX], F32R)
        k_h = sb("k_h", [P, PIX], F32R)
        k_l = sb("k_l", [P, PIX], F32R)
        v_sb = sb("v_tok", [P, TPI, C])
        top = sb("score_max", [P, TPI])
        ntop = sb("score_nmax", [P, TPI])
        prob = sb("prob", [P, TPI, PIX])
        psum_row = sb("prob_sum", [P, TPI])
        rsum = sb("prob_rsum", [P, TPI])
        prob_t = sb("prob_t", [P, TPI, PIX])
        logit = sb("logit", [P, TPI, EXPERTS])
        ltop = sb("logit_max", [P, TPI])
        nltop = sb("logit_nmax", [P, TPI])
        gexp = sb("gexp", [P, TPI, EXPERTS + 6])
        grest = sb("grest", [P, TPI, EXPERTS + 6])
        top8 = sb("top8", [P, TPI, 8])
        top2 = sb("top2", [P, TPI, 8])
        gsel = sb("gsel", [P, TPI, EXPERTS])
        tsum = sb("tsum", [P, TPI])
        trec = sb("trec", [P, TPI])
        xf = sb("xf", [P, IMAGES * PIX], F32R)
        spaced = sb("spaced", [P, TPI, P])
        dispatch = sb("dispatch", [P, IMAGES * PIX], F32R)
        select_f = sb("select_f", [P, DUETS, P])
        select = sb("select", [P, DUETS, P], F32R)
        w_f = [sb(f"w{k}_f", [P, EXPERTS, HIDDEN]) for k in (1, 2)]
        w_h = [sb(f"w{k}_h", [P, EXPERTS, HIDDEN], F32R) for k in (1, 2)]
        w_l = [sb(f"w{k}_l", [P, EXPERTS, HIDDEN], F32R) for k in (1, 2)]
        w3 = sb("w3", [P, EXPERTS, C])
        gated = [sb(f"gated{b}", [P, PIX]) for b in range(4)]
        hidden = [sb(f"hidden{b}", [P, PIX]) for b in range(4)]
        factor = [sb(f"factor{b}", [P, PIX]) for b in two]
        share = [sb(f"share{b}", [P, PIX]) for b in two]
        total = [sb(f"total{b}", [P, PIX]) for b in two]

        ps_xv = ps("ps_xv")
        ps_x = [ps_xv[:, 0:PIX], None]
        ps_v = ps_xv[:, PIX:PIX + TPI * C].rearrange("p (t c) -> p t c", t=TPI)
        ps_qk = ps_s = ps_p = ps("ps_qk")[:, :].rearrange("p (w x) -> p w x", w=TPI)
        ps_oxg = ps("ps_oxg")
        ps_x[1] = ps_d = ps_oxg[:, 0:PIX]
        ps_o = ps_oxg[:, PIX:PIX + TPI * C].rearrange("p (t c) -> p t c", t=TPI)
        ps_logit = ps_oxg[:, PIX + TPI * C:PIX + TPI * (C + EXPERTS)]
        ps_h1 = [ps(f"ps_h1{b}") for b in two]
        ps_h2 = [ps(f"ps_h2{b}") for b in two]
        ps_yf = ps("ps_yf")
        ps_y, ps_f, ps_z = ps_yf[:, 0:PIX], ps_yf[:, PIX:2 * PIX], ps_yf[:, 0:TPI * C]

        w1_in = sem("w1_in")
        w2_in = sem("w2_in")
        w3_in = sem("w3_in")
        select_in = sem("select_in")
        select_done = sem("select_done")
        cleared = sem("cleared2")
        w_high = sem("w_high")
        w_low = sem("w_low")
        piece_high = sem("piece_high")
        piece_low = sem("piece_low")
        ln_stat = [sem(f"ln_stat{s}") for s in two]
        ln_pow = [sem(f"ln_pow{s}") for s in two]
        ln_done = [sem(f"ln_done{s}") for s in two]
        x_ps = [sem(f"x_ps{s}") for s in two]
        x_high = [sem(f"x_high{s}") for s in two]
        x_low = [sem(f"x_low{s}") for s in two]
        qk_ps = sem("qk_ps")
        v_ps = sem("v_ps2")
        q_high = sem("q_high")
        k_high = sem("k_high")
        q_low = sem("q_low")
        k_low = sem("k_low")
        v_done = sem("v_done2")
        s_ps = sem("s_ps")
        max_step = sem("max_step")
        exp_done = sem("exp_done")
        p_ps = sem("p_ps")
        p_done = sem("p_done")
        rsum_done = sem("rsum_done")
        o_ps = sem("o_ps")
        res_done = sem("res_done")
        xf_done = sem("xf_done")
        g_ps = sem("g_ps")
        g_step = sem("g_step")
        g_exp = sem("g_exp")
        d_step = sem("d_step")
        h1_ps = sem("h1_ps")
        h2_ps = sem("h2_ps")
        silu_done = sem("silu_done")
        hidden_done = sem("hidden_done")
        y_ps = sem("y_ps")
        d_ps = sem("d_ps")
        d_high = sem("d_high")
        d_low = sem("d_low")
        factor_done = sem("factor_done")
        weighed = sem("weighed")
        z_ps = sem("z_ps")
        added = sem("added")
        finished = sem("finished")
        stored = sem("stored")
        TOP_STEPS = 9

        out_view = out.rearrange("n h w c -> (n h w) c").rearrange("(t p) c -> p t c", p=P)

        def duet_at(r, slot):
            p = DUETS * (r - FIRST) + slot
            return p if 0 <= p < DUETS * IMAGES else None

        def adds(p):
            return p - (p + DUETS - 1) // DUETS

        def stages(r):
            return [n if 0 <= n < IMAGES else None for n in (r, r - 1, r - 2, r - 3)]

        def piece_at(r, slot):
            places = [(0, 5), (0, 6), (0, 7), (1, 4), (1, 5), (1, 6), (2, 1), (2, 2)]
            return places.index((r, slot)) if (r, slot) in places else None

        block = ctx.enter_context(nc.Block())

        @block.sync
        def _(sp):
            for w, name, arrived in ((w_f[0], "w1", w1_in), (w_f[1], "w2", w2_in), (w3, "w3", w3_in),
                                     (select_f, "select", select_in)):
                sp.dma_start(w[:, :, :], d[name].rearrange("p (e h) -> p e h", e=w.shape[1])).then_inc(arrived, 16)
            for n in range(0, IMAGES, 2):
                sp.wait_ge(finished, n + 2)
                sp.dma_start(out_view[:, TPI * n:TPI * (n + 2), :],
                             t_tok[:, TPI * n:TPI * (n + 2), :]).then_inc(stored, 16)
            sp.wait_ge(stored, 16 * IMAGES // 2)

        @block.vector
        def _(dve):
            def ln_stats(s, i):
                if s:
                    dve.wait_ge(res_done, TPI * (i + 1))
                for t in range(TPI):
                    dve.bn_stats(stats[s][:, t, :], t_tok[:, TPI * i + t, :]).then_inc(ln_stat[s], 1)

            def ln_moments(s, i):
                dve.wait_ge(ln_stat[s], 5 * i + 2)
                for t in range(TPI):
                    dve.bn_aggr(moments[s][:, t, :], stats[s][:, t, :]).then_inc(ln_stat[s], 1)

            def ln_variance(s, i):
                dve.wait_ge(ln_stat[s], 5 * i + 4)
                dve.tensor_scalar(var_eps[s][:, :], moments[s][:, :, 1], LN_EPS, None, ALU.add)\
                   .then_inc(ln_stat[s], 1)

            def ln_apply(s, i):
                dve.wait_ge(ln_pow[s], i + 1)
                if positive(i):
                    dve.wait_ge(x_ps[s], i)
                for t in range(TPI):
                    op = dve.tensor_scalar(normed[s][:, t, :, :], spread(t_tok[:, TPI * i + t, :], 1, 2),
                                           moments[s][:, t, 0:1], rstd[s][:, t:t + 1],
                                           ALU.subtract, ALU.mult)
                op.then_inc(ln_done[s], 1)

            def x_split(s, i):
                dve.wait_ge(x_high[s], i + 1)
                dve.tensor_tensor(xs[s][64:P, :], ps_x[s][64:P, :], xs[s][64:P, :].bitcast(F32), ALU.subtract)\
                   .then_inc(x_low[s], 1)

            def qkv_low(i):
                dve.wait_ge(k_high, i + 1)
                dve.scalar_tensor_tensor(out=q_s[64:P, :], in0=ps_qk[64:P, 0, :], scalar=q_bias[64:P, :],
                                         in1=q_s[64:P, :].bitcast(F32), op0=ALU.add, op1=ALU.subtract)\
                   .then_inc(q_low, 1)
                dve.scalar_tensor_tensor(out=k_l[:, :], in0=ps_qk[:, 1, :], scalar=k_bias,
                                         in1=k_h[:, :].bitcast(F32), op0=ALU.add, op1=ALU.subtract)\
                   .then_inc(k_low, 1)
                dve.wait_ge(v_ps, i + 1)
                if positive(i):
                    dve.wait_ge(o_ps, i)
                dve.tensor_tensor(v_sb[:, :, :], ps_v, spread(at["v_bias"], 1, TPI), ALU.add).then_inc(v_done, 1)

            def score_max(i):
                dve.wait_ge(s_ps, i + 1)
                if positive(TPI * i):
                    dve.wait_ge(exp_done, TPI * i)
                dve.tensor_reduce(top[:, :], ps_s, AX_X, ALU.max).then_inc(max_step, 1)

            def score_negate(i):
                dve.wait_ge(max_step, 2 * i + 1)
                dve.tensor_scalar(ntop[:, :], top[:, :], -SCALE, None, ALU.mult).then_inc(max_step, 1)

            def invert_sums(i):
                dve.wait_ge(exp_done, TPI * (i + 1))
                dve.reciprocal(rsum[:, :], psum_row[:, :]).then_inc(rsum_done, 1)

            def add_values(i):
                dve.wait_ge(rsum_done, i + 1)
                dve.wait_ge(o_ps, i + 1)
                for t in range(TPI):
                    tok = t_tok[:, TPI * i + t, :]
                    dve.scalar_tensor_tensor(out=tok, in0=ps_o[:, t, :], scalar=rsum[:, t:t + 1], in1=tok,
                                             op0=ALU.mult, op1=ALU.add).then_inc(res_done, 1)

            def gate_logits(i):
                dve.wait_ge(g_ps, i + 1)
                dve.tensor_tensor(logit[:, :, :], ps_logit.rearrange("p (t e) -> p t e", t=TPI),
                                  spread(at["gate_bias"], 1, TPI), ALU.add).then_inc(g_step, 1)

            def gate_max(i):
                dve.wait_ge(g_step, 3 * i + 1)
                dve.tensor_reduce(ltop[:, :], logit[:, :, :], AX_X, ALU.max).then_inc(g_step, 1)

            def gate_negate(i):
                dve.wait_ge(g_step, 3 * i + 2)
                dve.tensor_scalar(nltop[:, :], ltop[:, :], -1.0, None, ALU.mult).then_inc(g_step, 1)

            def top_largest(i):
                dve.wait_ge(g_exp, TPI * (i + 1))
                for t in range(TPI):
                    dve.max(top8[:, t, :], gexp[:, t, 0:EXPERTS]).then_inc(d_step, 1)

            def top_sum(i):
                dve.wait_ge(d_step, TOP_STEPS * i + 2)
                dve.tensor_copy(top2[:, :, 0:2], top8[:, :, 0:2]).then_inc(d_step, 1)
                dve.tensor_tensor(tsum[:, :], top8[:, :, 0], top8[:, :, 1], ALU.add).then_inc(d_step, 1)

            def top_drop(i):
                dve.wait_ge(d_step, TOP_STEPS * i + 4)
                for t in range(TPI):
                    dve.match_replace(grest[:, t, :], top2[:, t, :], gexp[:, t, :], 0.0).then_inc(d_step, 1)
                dve.reciprocal(trec[:, :], tsum[:, :]).then_inc(d_step, 1)

            def top_keep(i):
                dve.wait_ge(d_step, TOP_STEPS * i + 7)
                dve.tensor_tensor(gsel[:, :, :], gexp[:, :, 0:EXPERTS], grest[:, :, 0:EXPERTS], ALU.subtract)\
                   .then_inc(d_step, 1)

            def top_share(i):
                dve.wait_ge(d_step, TOP_STEPS * i + 8)
                if positive(i):
                    dve.wait_ge(d_ps, i)
                rows = spaced[:, :, 0:64].rearrange("p t (a e) -> p t a e", a=2)[:, :, :, 0:EXPERTS]
                dve.tensor_tensor(rows, spread(gsel[:, :, :], 2, 2), spread(spread(trec[:, :], 2, 2), 3, EXPERTS),
                                  ALU.mult).then_inc(d_step, 1)

            def dispatch_low(i):
                dve.wait_ge(d_high, i + 1)
                rows = dispatch[32:32 + EXPERTS, PIX * i:PIX * (i + 1)]
                dve.tensor_tensor(rows, ps_d[32:32 + EXPERTS, :], rows.bitcast(F32), ALU.subtract)\
                   .then_inc(d_low, 1)

            def hide(u):
                dve.wait_ge(silu_done, u + 1)
                dve.wait_ge(h2_ps, u + 1)
                if positive(u // 2 - 1):
                    dve.wait_ge(y_ps, u // 2 - 1)
                dve.tensor_tensor(hidden[u % 4][:, :], ps_h2[u % 2][:, 0:PIX], gated[u % 4][:, :], ALU.mult)\
                   .then_inc(hidden_done, 1)

            def weigh(p):
                n = p // DUETS
                dve.wait_ge(y_ps, p + 1)
                dve.wait_ge(factor_done, p + 1)
                if p % DUETS == 0:
                    if positive(n - 1):
                        dve.wait_ge(z_ps, n - 1)
                    target = total[n % 2]
                else:
                    if positive(adds(p - 1)):
                        dve.wait_ge(added, adds(p - 1))
                    target = share[p % 2]
                dve.tensor_tensor(target[:, :], ps_y, factor[p % 2][:, :], ALU.mult).then_inc(weighed, 1)

            def finish(n):
                dve.wait_ge(z_ps, n + 1)
                tokens = t_tok[:, TPI * n:TPI * (n + 1), :].rearrange("p t c -> p (t c)")
                dve.tensor_tensor(tokens, ps_z, tokens, ALU.add).then_inc(finished, 1)

            for r in range(ROUNDS):
                project, attend, gate, serve = stages(r)
                for slot in range(SLOTS):
                    p = duet_at(r, slot)
                    if (r, slot) == (0, 1):
                        dve.wait_ge(pack_in, 16)
                        dve.wait_ge(w_high, 1)
                        dve.tensor_tensor(pack_l[:, :], pack[:, 0:split_cols], pack_h[:, :].bitcast(F32),
                                          ALU.subtract).then_inc(w_low, 1)
                        dve.wait_ge(cleared, 5)
                    if p is not None and p >= 2:
                        weigh(p - 2)
                    if slot == FINISH and p is not None and p > DUETS:
                        finish(p // DUETS - 1)
                    if slot == 0 and gate is not None:
                        ln_variance(1, gate)
                    if slot == 0 and project is not None:
                        ln_stats(0, project)
                    if slot == 3 and attend is not None:
                        score_negate(attend)
                    if slot == 4 and gate is not None:
                        gate_max(gate)
                    if slot == 5 and gate is not None:
                        top_largest(gate)
                    if slot == 6 and gate is not None:
                        top_keep(gate)
                    if slot == 7 and attend is not None:
                        add_values(attend)
                    if p is not None:
                        hide(2 * p)
                    if slot == 0 and project is not None:
                        ln_moments(0, project)
                    if slot == 2 and project is not None:
                        ln_apply(0, project)
                    if slot == 4 and gate is not None:
                        gate_negate(gate)
                    if slot == 5 and gate is not None:
                        top_sum(gate)
                    if slot == 6 and gate is not None:
                        top_share(gate)
                    if slot == 7 and attend is not None:
                        ln_stats(1, attend)
                    if p is not None:
                        hide(2 * p + 1)
                    if slot == 1 and project is not None:
                        ln_variance(0, project)
                    if slot == 0 and serve is not None:
                        dispatch_low(serve)
                    if slot == 1 and gate is not None:
                        ln_apply(1, gate)
                    if slot == 2 and attend is not None:
                        score_max(attend)
                    if slot == 2 and gate is not None:
                        x_split(1, gate)
                    if slot == 3 and gate is not None:
                        gate_logits(gate)
                    if slot == 5 and project is not None:
                        x_split(0, project)
                    if slot == 5 and gate is not None:
                        top_drop(gate)
                    if slot == 5 and attend is not None:
                        invert_sums(attend)
                    if slot == 7 and attend is not None:
                        ln_moments(1, attend)
                    if slot == 7 and project is not None:
                        qkv_low(project)
            weigh(DUETS * IMAGES - 2)
            weigh(DUETS * IMAGES - 1)
            finish(IMAGES - 1)

        @block.gpsimd
        def _(pool):
            pool.memset(minus_half[:, :], -0.5).then_inc(cleared, 1)
            pool.memset(gexp[:, :, EXPERTS:EXPERTS + 6], -1.0).then_inc(cleared, 1)
            pool.memset(top2[:, :, :], -1.0).then_inc(cleared, 1)
            pool.memset(grest[:, :, :], 0.0).then_inc(cleared, 1)
            pool.memset(spaced[:, :, :], 0.0).then_inc(cleared, 1)
            pool.wait_ge(cleared, 1)

            def power(s, i):
                pool.wait_ge(ln_stat[s], 5 * (i + 1))
                if positive(i):
                    pool.wait_ge(ln_done[s], i)
                pool.tensor_tensor(rstd[s][:, :], var_eps[s][:, :], minus_half[:, :], ALU.pow)\
                    .then_inc(ln_pow[s], 1)

            def keep_x(i):
                pool.wait_ge(x_low[1], i + 1)
                pool.tensor_copy(xf[:, PIX * i:PIX * (i + 1)], xs[1][:, :].bitcast(F32)).then_inc(xf_done, 1)

            def add(p):
                if p % DUETS:
                    sums = total[p // DUETS % 2]
                    pool.wait_ge(weighed, p + 1)
                    if positive(adds(p)):
                        pool.wait_ge(added, adds(p))
                    pool.tensor_tensor(sums[:, :], sums[:, :], share[p % 2][:, :], ALU.add).then_inc(added, 1)

            def low_piece(k):
                w, e = k // 4, PIECE * (k % 4)
                pool.wait_ge(piece_high, k + 1)
                pool.tensor_tensor(w_l[w][:, e:e + PIECE, :], w_f[w][:, e:e + PIECE, :],
                                   w_h[w][:, e:e + PIECE, :].bitcast(F32), ALU.subtract).then_inc(piece_low, 1)

            for r in range(ROUNDS):
                project, attend, gate, serve = stages(r)
                for slot in range(SLOTS):
                    p = duet_at(r, slot)
                    if p is not None and p >= 2:
                        add(p - 2)
                    if slot == 0 and gate is not None:
                        power(1, gate)
                    if slot == 0 and project is not None:
                        power(0, project)
                    if slot == 1 and gate is not None:
                        keep_x(gate)
                    if piece_at(r, slot) is not None:
                        low_piece(piece_at(r, slot))
            add(DUETS * IMAGES - 2)
            add(DUETS * IMAGES - 1)

        @block.scalar
        def _(act):
            act.wait_ge(pack_in, 16)
            act.activation(pack_h[:, :], pack[:, 0:split_cols], ACT.Copy).then_inc(w_high, 1)

            def high(s, i):
                act.wait_ge(x_ps[s], i + 1)
                if s:
                    if positive(i):
                        act.wait_ge(xf_done, i)
                    if positive(i):
                        act.wait_ge(g_ps, i)
                else:
                    if positive(i):
                        act.wait_ge(v_ps, i)
                act.activation(xs[s][:, :], ps_x[s][:, :], ACT.Copy).then_inc(x_high[s], 1)

            def qk_high(i):
                act.wait_ge(qk_ps, i + 1)
                if positive(i):
                    act.wait_ge(s_ps, i)
                act.activation(q_s[:, :], ps_qk[:, 0, :], ACT.Identity, bias=q_bias).then_inc(q_high, 1)
                act.activation(k_h[:, :], ps_qk[:, 1, :], ACT.Identity, bias=k_bias).then_inc(k_high, 1)

            def exps(i):
                act.wait_ge(max_step, 2 * i + 2)
                if positive(i):
                    act.wait_ge(p_ps, i)
                if positive(i):
                    act.wait_ge(rsum_done, i)
                for t in range(TPI):
                    act.activation(prob[:, t, :], ps_s[:, t, :], ACT.Exp, bias=ntop[:, t:t + 1], scale=SCALE,
                                   accum_out=psum_row[:, t:t + 1]).then_inc(exp_done, 1)

            def copy_p(i):
                act.wait_ge(p_ps, i + 1)
                if positive(i):
                    act.wait_ge(o_ps, i)
                act.activation(prob_t[:, :, :], ps_p, ACT.Copy).then_inc(p_done, 1)

            def gate_exp(i):
                act.wait_ge(g_step, 3 * i + 3)
                if positive(TOP_STEPS * i):
                    act.wait_ge(d_step, TOP_STEPS * i)
                for t in range(TPI):
                    act.activation(gexp[:, t, 0:EXPERTS], logit[:, t, :], ACT.Exp, bias=nltop[:, t:t + 1])\
                       .then_inc(g_exp, 1)

            def high_piece(k):
                w, e = k // 4, PIECE * (k % 4)
                act.wait_ge((w1_in, w2_in)[w], 16)
                act.activation(w_h[w][:, e:e + PIECE, :], w_f[w][:, e:e + PIECE, :], ACT.Copy)\
                   .then_inc(piece_high, 1)

            def dispatch_high(i):
                act.wait_ge(d_ps, i + 1)
                act.activation(dispatch[:, PIX * i:PIX * (i + 1)], ps_d, ACT.Copy).then_inc(d_high, 1)

            def copy_factor(p):
                act.wait_ge(y_ps, p + 1)
                if positive(p - 1):
                    act.wait_ge(weighed, p - 1)
                act.activation(factor[p % 2][:, :], ps_f, ACT.Copy).then_inc(factor_done, 1)

            def silu(u):
                act.wait_ge(h1_ps, u + 1)
                if positive(u - 3):
                    act.wait_ge(hidden_done, u - 3)
                act.activation(gated[u % 4][:, :], ps_h1[u % 2][:, 0:PIX], ACT.Silu).then_inc(silu_done, 1)

            for r in range(ROUNDS):
                project, attend, gate, serve = stages(r)
                for slot in range(SLOTS):
                    p = duet_at(r, slot)
                    if p is not None:
                        if p >= 2:
                            copy_factor(p - 2)
                        if p == 0:
                            silu(0)
                        for u in (2 * p + 1, 2 * p + 2):
                            if u < UNITS:
                                silu(u)
                    if slot == 0 and serve is not None:
                        dispatch_high(serve)
                    if slot == 2 and gate is not None:
                        high(1, gate)
                    if slot == 3 and project is not None:
                        high(0, project)
                    if slot == 4 and attend is not None:
                        exps(attend)
                    if slot == 4 and gate is not None:
                        gate_exp(gate)
                    if slot == 5 and attend is not None:
                        copy_p(attend)
                    if slot == 7 and project is not None:
                        qk_high(project)
                    if piece_at(r, slot) is not None:
                        high_piece(piece_at(r, slot))
                    if (r, slot) == (0, 7):
                        act.wait_ge(select_in, 16)
                        act.activation(select[:, :, :], select_f[:, :, :], ACT.Copy).then_inc(select_done, 1)
            copy_factor(DUETS * IMAGES - 2)
            copy_factor(DUETS * IMAGES - 1)

        @block.tensor
        def _(pe):
            pe.wait_ge(pack_in, 16)

            def turn(s, i):
                pe.wait_ge(ln_done[s], i + 1)
                if s:
                    if positive(i):
                        pe.wait_ge(d_low, i)
                if s == 0:
                    if positive(i):
                        pe.wait_ge(v_done, i)
                for t in range(TPI):
                    mm = pe.transpose(ps_x[s][:, t * P:(t + 1) * P],
                                      normed[s][:, t, :, :].rearrange("p a c -> p (a c)"), ident)
                mm.then_inc(x_ps[s], 1)

            def project_qkv(i):
                if i == 0:
                    pe.wait_ge(w_low, 1)
                pe.wait_ge(x_low[0], i + 1)
                if positive(i):
                    pe.wait_ge(q_low, i)
                if positive(i):
                    pe.wait_ge(k_low, i)
                if positive(i):
                    pe.wait_ge(p_done, i)
                for c, n in enumerate(("q_w", "k_w")):
                    for w, first in ((wh[n], True), (wl[n], False)):
                        mm = pe.matmul(ps_qk[:, c, :], w, xs[0][:, :], start=first, stop=not first)
                mm.then_inc(qk_ps, 1)
                for t in range(TPI):
                    for w, first in ((wh["v_w"], True), (wl["v_w"], False)):
                        mm = pe.matmul(ps_v[:, t, :], xs[0][:, t * P:(t + 1) * P], w,
                                       start=first, stop=not first)
                mm.then_inc(v_ps, 1)

            def scores(i):
                pe.wait_ge(q_low, i + 1)
                pe.wait_ge(k_low, i + 1)
                if positive(i):
                    pe.wait_ge(p_done, i)
                for t in range(TPI):
                    for k, first in ((k_h, True), (k_l, False)):
                        mm = pe.matmul(ps_s[:, t, :], q_s[:, t * P:(t + 1) * P], k[:, :],
                                       start=first, stop=not first)
                mm.then_inc(s_ps, 1)

            def turn_p(i):
                pe.wait_ge(exp_done, TPI * (i + 1))
                for t in range(TPI):
                    for k in range(TPI):
                        mm = pe.transpose(ps_p[:, k, t * P:(t + 1) * P], prob[:, t, k * P:(k + 1) * P], ident)
                mm.then_inc(p_ps, 1)

            def values(i):
                pe.wait_ge(p_done, i + 1)
                pe.wait_ge(v_done, i + 1)
                if positive(3 * i - 2):
                    pe.wait_ge(g_step, 3 * i - 2)
                for t in range(TPI):
                    for k in range(TPI):
                        mm = pe.matmul(ps_o[:, t, :], prob_t[:, k, t * P:(t + 1) * P], v_sb[:, k, :],
                                       start=k == 0, stop=k == TPI - 1)
                mm.then_inc(o_ps, 1)

            def gate_product(i):
                pe.wait_ge(x_low[1], i + 1)
                for t in range(TPI):
                    for w, first in ((wh["gate_w"], True), (wl["gate_w"], False)):
                        mm = pe.matmul(ps_logit[:, t * EXPERTS:(t + 1) * EXPERTS],
                                       xs[1][:, t * P:(t + 1) * P], w, start=first, stop=not first)
                mm.then_inc(g_ps, 1)

            def product_1(u):
                n, e = u // EXPERTS, u % EXPERTS
                tokens = xf[:, PIX * n:PIX * (n + 1)]
                if e == 0:
                    pe.wait_ge(xf_done, n + 1)
                if n == 0 and e % PIECE == 0:
                    pe.wait_ge(piece_low, 4 + e // PIECE + 1)
                if positive(u - 1):
                    pe.wait_ge(silu_done, u - 1)
                for w, first in ((w_h[0], True), (w_l[0], False)):
                    mm = pe.matmul(ps_h1[u % 2][:, 0:PIX], w[:, e, :], tokens, start=first, stop=not first)
                mm.then_inc(h1_ps, 1)

            def product_2(u):
                n, e = u // EXPERTS, u % EXPERTS
                tokens = xf[:, PIX * n:PIX * (n + 1)]
                if positive(u - 1):
                    pe.wait_ge(hidden_done, u - 1)
                for w, first in ((w_h[1], True), (w_l[1], False)):
                    mm = pe.matmul(ps_h2[u % 2][:, 0:PIX], w[:, e, :], tokens, start=first, stop=not first)
                mm.then_inc(h2_ps, 1)

            def turn_dispatch(i):
                pe.wait_ge(d_step, TOP_STEPS * (i + 1))
                pe.wait_ge(res_done, TPI * min(i + 2, IMAGES))
                for t in range(TPI):
                    mm = pe.transpose(ps_d[:, t * P:(t + 1) * P], spaced[:, t, :], ident)
                mm.then_inc(d_ps, 1)

            def output(p):
                n = p // DUETS
                if p == 0:
                    pe.wait_ge(w3_in, 16)
                    pe.wait_ge(select_done, 1)
                if p % DUETS == 0:
                    pe.wait_ge(d_low, n + 1)
                if positive(p):
                    pe.wait_ge(weighed, p)
                if positive((p - FINISH + 1) // DUETS):
                    pe.wait_ge(finished, (p - FINISH + 1) // DUETS)
                pe.matmul(ps_f, select[:, p % DUETS, :], dispatch[:, PIX * n:PIX * (n + 1)], start=True, stop=True)
                pe.wait_ge(hidden_done, 2 * (p + 1))
                for k in range(2):
                    u = 2 * p + k
                    mm = pe.matmul(ps_y[64 * k:64 * k + 64, :], w3[:, u % EXPERTS, :], hidden[u % 4][:, :],
                                   start=True, stop=True)
                mm.then_inc(y_ps, 1)

            def turn_sum(n):
                pe.wait_ge(added, adds(DUETS * (n + 1)))
                pe.wait_ge(weighed, min(DUETS * (n + 1) + FINISH - 1, DUETS * IMAGES))
                for t in range(TPI):
                    mm = pe.matmul(ps_z[:, t * C:(t + 1) * C], total[n % 2][:, t * P:(t + 1) * P], at["join"],
                                   start=True, stop=True)
                mm.then_inc(z_ps, 1)

            for r in range(ROUNDS):
                project, attend, gate, serve = stages(r)
                for slot in range(SLOTS):
                    p = duet_at(r, slot)
                    if p is not None:
                        if p == 0:
                            product_1(0)
                        for u in (2 * p, 2 * p + 1):
                            if u + 1 < UNITS:
                                product_1(u + 1)
                            product_2(u)
                    if slot == 0 and serve is not None:
                        turn_dispatch(serve)
                    if slot == 2 and attend is not None:
                        scores(attend)
                    if slot == 2 and gate is not None:
                        turn(1, gate)
                    if slot == 3 and project is not None:
                        turn(0, project)
                    if slot == 3 and gate is not None:
                        gate_product(gate)
                    if slot == 5 and attend is not None:
                        turn_p(attend)
                    if slot == 7 and project is not None:
                        project_qkv(project)
                    if slot == 6 and attend is not None:
                        values(attend)
                    if slot == FINISH and p is not None and p > DUETS:
                        turn_sum(p // DUETS - 1)
                    if p is not None and p:
                        output(p - 1)
            output(DUETS * IMAGES - 1)
            turn_sum(IMAGES - 1)


def shape_arrays(np):
    ident = np.eye(P, dtype=np.float32)
    pair = np.zeros((P, P), np.float32)
    for r in range(P):
        pair[r, r] = pair[r, r ^ 1] = 0.5
    fold = np.zeros((P, QUARTETS, 32), np.float32)
    for q in range(QUARTETS):
        for c in range(GC):
            fold[c::GC, q, GC * q + c] = 1.0
    rep = np.zeros((P, QUART, P), np.float32)
    for j in range(QUART):
        for y in range(16):
            rep[16 * j + y, j, GC * y:GC * y + GC] = rep[64 + 16 * j + y, j, GC * y:GC * y + GC] = 1.0
    rows = (np.arange(P)[:, None] // 16 % DUO == np.arange(DUO)).astype(np.float32)
    grid = np.zeros((P, H, W), np.float32)
    grid[[0, 32, 64, 96]] = 1.0
    grid[97] = np.arange(H)[:, None]
    grid[98] = np.arange(W)[None, :]
    place = np.zeros((3, OFFSETS, GROUPS, 16), np.float32)
    at = np.arange(16)
    for tap in range(TAPS):
        place[0, 2 * tap] = tap % 3 - 1 - at
        place[2, 2 * tap] = 1.0
        place[0, 2 * tap + 1] = tap // 3 - 1 - at
        place[1, 2 * tap + 1] = 1.0
    select = np.zeros((P, EXPERTS // 2, 2, C), np.float32)
    for e in range(EXPERTS):
        select[[e, 32 + e], e // 2, e % 2] = 1.0
    join = np.zeros((P, C), np.float32)
    join[np.arange(P), np.arange(P) % C] = 1.0
    return {"ident": ident, "select": select.reshape(P, -1), "join": join, "pair": pair,
            "fold": fold.reshape(P, -1), "rows": rows, "rep": rep.reshape(P, -1),
            "grid": grid.reshape(P, -1), "place": place.reshape(3, -1)}


def laid_out(inputs, np):
    f = {k: np.asarray(v) for k, v in inputs.items()}
    rows = lambda v: np.ascontiguousarray(np.repeat(v.reshape(1, -1), P, 0))
    mask_bias = np.repeat(f["L0_conv_om_b"].reshape(GROUPS, OMJ)[:, OFFSETS:], 16, 0)
    twice = lambda a: np.ascontiguousarray(np.concatenate([a, a], 0))
    op = f["L0_conv_op_w"].reshape(QUARTETS, QUART, GC, C)
    op_w = np.zeros((QUART, 32, C), op.dtype)
    for q in range(QUARTETS):
        op_w[:, GC * q:GC * q + GC] = op[q]
    om_b = np.zeros((P, GROUPS * OMJ), f["L0_conv_om_b"].dtype)
    om_b[[0, 32, 64]] = f["L0_conv_om_b"]
    four = lambda m: np.ascontiguousarray(np.tile(m, (2, 2)))
    return {
        "q_w": four(f["L1_attn_Wq"].T), "k_w": four(f["L1_attn_Wk"].T), "v_w": twice(f["L1_attn_Wv"].T),
        "q_bias": twice(f["L1_attn_bq"].reshape(C, 1)), "k_bias": twice(f["L1_attn_bk"].reshape(C, 1)),
        "v_bias": rows(f["L1_attn_bv"]), "gate_w": twice(f["L1_ffn_gate_w"]), "gate_bias": rows(f["L1_ffn_gate_b"]),
        "w1": twice(f["L1_ffn_w1"].transpose(1, 0, 2).reshape(C, -1)),
        "w2": twice(f["L1_ffn_w2"].transpose(1, 0, 2).reshape(C, -1)),
        "w3": np.ascontiguousarray(f["L1_ffn_w3"].transpose(1, 0, 2).reshape(HIDDEN, -1)),
        "x": f["x"], "x_turned": twice(f["x"].reshape(-1, C).T),
        "dw": twice(f["L0_conv_dw_w"].reshape(TAPS, C).T), "dw_bias": twice(f["L0_conv_dw_b"].reshape(C, 1)),
        "om_w": twice(f["L0_conv_om_w"]), "om_b": om_b, "mask_bias": mask_bias, "vp_w": twice(f["L0_conv_vp_w"]),
        "vp_bias": rows(f["L0_conv_vp_b"]), "op_w": op_w.reshape(P, C),
    }


def packed(arrays, np):
    packs = {"keep": KEEP, "start": START, "attention": ATTENTION}
    members = {name for pack in packs.values() for name in pack}
    side = {p: np.ascontiguousarray(np.concatenate([arrays[n] for n in pack], 1)) for p, pack in packs.items()}
    return {**{n: a for n, a in arrays.items() if n not in members}, **side}


def program(nc, d, out):
    with ExitStack() as ctx:
        t_tok = ctx.enter_context(nc.sbuf_tensor("t_tok", [P, TT, C], F32))
        pack = ctx.enter_context(nc.sbuf_tensor("attention_pack", [P, ATTENTION_COLS], F32))
        pack_in = ctx.enter_context(nc.semaphore("pack_in"))
        conv_stage(nc, d, t_tok, pack, pack_in)
        token_stage(nc, d, out, t_tok, pack, pack_in)


def kernel(**inputs):
    import numpy as np
    import concourse.bacc as bacc
    from concourse.bass_utils import run_bass_kernel_spmd

    arrays = packed({**laid_out(inputs, np), **shape_arrays(np)}, np)
    nc = bacc.Bacc("TRN2", target_bir_lowering=False, num_devices=1)
    d = {name: nc.dram_tensor(f"in_{name}", a.shape, mybir.dt.from_np(a.dtype), kind="ExternalInput").ap()
         for name, a in arrays.items()}
    out = nc.dram_tensor("out", (IMAGES, H, W, C), F32, kind="ExternalOutput").ap()
    program(nc, d, out)
    result = run_bass_kernel_spmd(nc, [{f"in_{name}": a for name, a in arrays.items()}], core_ids=[0])
    return result.results[0]["out"]
```
